# Optimizing a Trainium2 kernel written in Bass

```python
import numpy as np
import jax
import jax.numpy as jnp

def _softmax(x, axis=-1):
    return jax.nn.softmax(x, axis=axis)

def _gelu(x):
    return jax.nn.gelu(x, approximate=True)

def _silu(x):
    return jax.nn.silu(x)

def _sigmoid(x):
    return jax.nn.sigmoid(x)

def _layernorm(x, axis=-1, eps=1e-05):
    m = jnp.mean(x, axis=axis, keepdims=True)
    v = jnp.var(x, axis=axis, keepdims=True)
    return (x - m) / jnp.sqrt(v + eps)

def _scatter_add(tgt, idx, src, axis=0):
    return tgt.at[idx].add(src)

def _segment_sum(src, seg, n):
    return jax.ops.segment_sum(src, seg, n)
kernel_name = 'mk_gps_d2_gnn_r32_300b6e'

def setup_inputs(seed: int=0):
    np.random.seed(seed)
    _w = jnp.asarray

    def _rec_inputs():
        import jax
        import jax.numpy as jnp
        _gk = jax.random.key(seed)
        x = -0.0002117 + 1 * jax.random.normal(jax.random.fold_in(_gk, 1), (3125, 256), jnp.float32)
        _s = jax.random.randint(jax.random.fold_in(_gk, 2), (25000,), 0, 3125, jnp.int32)
        _d = jax.random.randint(jax.random.fold_in(_gk, 3), (25000,), 0, 3125, jnp.int32)
        _loop = jnp.arange(3125, dtype=jnp.int32)
        src = jnp.concatenate([_s, _d, _loop])
        dst = jnp.concatenate([_d, _s, _loop])
        _o = jnp.argsort(dst, stable=True)
        src = src[_o]
        dst = dst[_o]
        edge_weight = jax.random.uniform(jax.random.fold_in(_gk, 12), (53125,), jnp.float32, 0.0, 1)
        return (x, src, dst, edge_weight)
    x, src, dst, edge_weight = _rec_inputs()

    def _L0_gnn_setup():
        import jax, jax.numpy as jnp
        import numpy as np
        N_NODES = 3125
        K_HOPS = 2
        ALPHA = 0.5

        def _gcn_norm(edge_index, edge_weight, num_nodes):
            loops = jnp.arange(num_nodes, dtype=edge_index.dtype)
            src = jnp.concatenate([edge_index[0], loops])
            dst = jnp.concatenate([edge_index[1], loops])
            w = jnp.concatenate([edge_weight, jnp.ones((num_nodes,), edge_weight.dtype)])
            deg = jax.ops.segment_sum(w, dst, num_segments=num_nodes)
            dinv = jnp.where(deg > 0, jax.lax.rsqrt(jnp.maximum(deg, 1e-12)), 0.0)
            norm = dinv[src] * w * dinv[dst]
            return (src, dst, norm)
        key = jax.random.key(seed)
        k1, k2, k3, k4, k5 = jax.random.split(key, 5)
        N, E, D_IN, D_OUT = (N_NODES, 100000, 256, 256)
        x = jax.random.normal(k1, (N, D_IN), dtype=jnp.float32)
        edge_index = jax.random.randint(k2, (2, E), 0, N, dtype=jnp.int64)
        edge_weight = jax.random.uniform(k3, (E,), dtype=jnp.float32)
        W = jax.random.normal(k4, (D_OUT, D_IN), dtype=jnp.float32) / np.sqrt(D_IN)
        b = jax.random.normal(k5, (D_OUT,), dtype=jnp.float32) * 0.01
        return {'x': x, 'edge_index': edge_index, 'edge_weight': edge_weight, 'W': W, 'b': b}
    _L0_gnn_all = _L0_gnn_setup()
    _L0_gnn_in = {k: v for k, v in _L0_gnn_all.items() if k in ('W', 'b')}
    del _L0_gnn_all

    def _L0_mix_setup():
        import jax, jax.numpy as jnp
        import numpy as np
        HEADS, DIM_HEAD = (8, 64)
        EPS = 1e-05

        def instance_norm(t):
            mu = jnp.mean(t, axis=-1, keepdims=True)
            var = jnp.mean((t - mu) ** 2, axis=-1, keepdims=True)
            return (t - mu) * jax.lax.rsqrt(var + EPS)
        key = jax.random.key(seed)
        k1, k2, k3, k4 = jax.random.split(key, 4)
        B, N, D = (8, 256, 256)
        inner = HEADS * DIM_HEAD
        x = jax.random.normal(k1, (B, N, D), jnp.float32)
        w_qkv = jax.random.normal(k2, (3 * inner, D), jnp.float32) / np.sqrt(D).astype(np.float32)
        w_out = jax.random.normal(k3, (D, inner), jnp.float32) / np.sqrt(inner).astype(np.float32)
        b_out = 0.01 * jax.random.normal(k4, (D,), jnp.float32)
        return {'x': x, 'w_qkv': w_qkv, 'w_out': w_out, 'b_out': b_out}
    _L0_mix_all = _L0_mix_setup()
    _L0_mix_in = {k: v for k, v in _L0_mix_all.items() if k in ('w_qkv', 'w_out', 'b_out')}
    del _L0_mix_all

    def _L0_ffn_setup():
        import math
        import jax, jax.numpy as jnp
        import numpy as np
        CAPACITY_FACTOR = 1.25
        TOP_K = 2
        LN_EPS = 1e-05

        def _layer_norm(x, gamma, beta):
            mu = jnp.mean(x, axis=-1, keepdims=True)
            var = jnp.var(x, axis=-1, keepdims=True)
            return (x - mu) * jax.lax.rsqrt(var + LN_EPS) * gamma + beta
        key = jax.random.key(seed)
        ks = jax.random.split(key, 4)
        B, S, D, F, E = (8, 128, 256, 512, 8)
        x = jax.random.normal(ks[0], (B, S, D), dtype=jnp.float32)
        Wr = jax.random.normal(ks[1], (D, E), dtype=jnp.float32) / np.sqrt(D)
        br = jnp.zeros((E,), jnp.float32)
        W1 = jax.random.normal(ks[2], (E, D, F), dtype=jnp.float32) / np.sqrt(D)
        b1 = jnp.zeros((E, F), jnp.float32)
        W2 = jax.random.normal(ks[3], (E, F, D), dtype=jnp.float32) / np.sqrt(F)
        b2 = jnp.zeros((E, D), jnp.float32)
        gamma = jnp.ones((D,), jnp.float32)
        beta = jnp.zeros((D,), jnp.float32)
        return {'x': x, 'Wr': Wr, 'br': br, 'W1': W1, 'b1': b1, 'W2': W2, 'b2': b2, 'gamma': gamma, 'beta': beta}
    _L0_ffn_all = _L0_ffn_setup()
    _L0_ffn_in = {k: v for k, v in _L0_ffn_all.items() if k in ('Wr', 'br', 'W1', 'b1', 'W2', 'b2', 'gamma', 'beta')}
    del _L0_ffn_all

    def _L1_gnn_setup():
        import jax, jax.numpy as jnp
        import numpy as np
        N_NODES = 3125
        N_EDGES = 50000
        NFEAT, NHID, NCLASS = (256, 512, 256)

        def _init_params(key):
            ks = jax.random.split(key, 8)
            s = 0.02
            p = {'W1a': jax.random.normal(ks[0], (NFEAT, NHID), jnp.float32) * s, 'b1a': jnp.zeros((NHID,), jnp.float32), 'W1b': jax.random.normal(ks[1], (NHID, NHID), jnp.float32) * s, 'b1b': jnp.zeros((NHID,), jnp.float32), 'W2a': jax.random.normal(ks[2], (NHID, NHID), jnp.float32) * s, 'b2a': jnp.zeros((NHID,), jnp.float32), 'W2b': jax.random.normal(ks[3], (NHID, NCLASS), jnp.float32) * s, 'b2b': jnp.zeros((NCLASS,), jnp.float32), 'eps1': jnp.zeros((), jnp.float32), 'eps2': jnp.zeros((), jnp.float32)}
            return p

        def _gin_agg(h, src, dst, eps, n_nodes):
            agg = jax.ops.segment_sum(h[src], dst, num_segments=n_nodes)
            return (1.0 + eps) * h + agg
        key = jax.random.key(seed)
        kx, ke, kp = jax.random.split(key, 3)
        x = jax.random.normal(kx, (N_NODES, NFEAT), jnp.float32)
        edge_index = jax.random.randint(ke, (2, N_EDGES), 0, N_NODES, jnp.int64)
        inp = {'x': x, 'edge_index': edge_index}
        inp.update(_init_params(kp))
        return inp
    _L1_gnn_all = _L1_gnn_setup()
    _L1_gnn_in = {k: v for k, v in _L1_gnn_all.items() if k in ('W1a', 'b1a', 'W1b', 'b1b', 'W2a', 'b2a', 'W2b', 'b2b', 'eps1', 'eps2')}
    del _L1_gnn_all

    def _L1_mix_setup():
        import jax, jax.numpy as jnp
        import numpy as np
        DIM = 256
        HEADS = 4
        DIM_HEAD = 32
        NUM_MEM = 4
        HIDDEN = HEADS * DIM_HEAD
        SCALE = DIM_HEAD ** (-0.5)

        def rmsnorm(x, g):
            n = jnp.linalg.norm(x, axis=-1, keepdims=True)
            return x / jnp.maximum(n, 1e-12) * g * x.shape[-1] ** 0.5
        key = jax.random.key(seed)
        ks = jax.random.split(key, 8)
        B, N = (4, 512)
        return {'x': jax.random.normal(ks[0], (B, N, DIM), jnp.float32), 't': jax.random.normal(ks[1], (B,), jnp.float32), 'w_qkv': jax.random.normal(ks[2], (DIM, 3 * HIDDEN), jnp.float32) * 0.02, 'mem_kv': jax.random.normal(ks[3], (2, HEADS, DIM_HEAD, NUM_MEM), jnp.float32), 'w_out': jax.random.normal(ks[4], (HIDDEN, DIM), jnp.float32) * 0.02, 'b_out': jnp.zeros((DIM,), jnp.float32), 'g_out': jnp.ones((DIM,), jnp.float32), 'g_pre': jnp.ones((DIM,), jnp.float32)}
    _L1_mix_all = _L1_mix_setup()
    _L1_mix_in = {k: v for k, v in _L1_mix_all.items() if k in ('t', 'w_qkv', 'mem_kv', 'w_out', 'b_out', 'g_out', 'g_pre')}
    del _L1_mix_all

    def _L1_ffn_setup():
        import jax, jax.numpy as jnp
        import numpy as np
        E, D, H, TOP_K = (6, 256, 256, 2)
        ROUTER_H = D // 2
        key = jax.random.key(seed)
        ks = jax.random.split(key, 12)
        s = 1.0 / np.sqrt(D)
        sh = 1.0 / np.sqrt(H)
        sr = 1.0 / np.sqrt(ROUTER_H)
        return {'features': jax.random.normal(ks[0], (8, 128, D), dtype=jnp.float32), 'router_w1': jax.random.uniform(ks[1], (D, ROUTER_H), jnp.float32, -s, s), 'router_b1': jnp.zeros((ROUTER_H,), jnp.float32), 'router_w2': jax.random.uniform(ks[2], (ROUTER_H, E), jnp.float32, -sr, sr), 'router_b2': jnp.zeros((E,), jnp.float32), 'expert_w1': jax.random.uniform(ks[3], (E, D, H), jnp.float32, -s, s), 'expert_b1': jnp.zeros((E, H), jnp.float32), 'expert_w2': jax.random.uniform(ks[4], (E, H, H), jnp.float32, -sh, sh), 'expert_b2': jnp.zeros((E, H), jnp.float32), 'expert_w3': jax.random.uniform(ks[5], (E, H, D), jnp.float32, -sh, sh), 'expert_b3': jnp.zeros((E, D), jnp.float32)}
    _L1_ffn_all = _L1_ffn_setup()
    _L1_ffn_in = {k: v for k, v in _L1_ffn_all.items() if k in ('router_w1', 'router_b1', 'router_w2', 'router_b2', 'expert_w1', 'expert_b1', 'expert_w2', 'expert_b2', 'expert_w3', 'expert_b3')}
    del _L1_ffn_all
    return {'x': x, 'src': src, 'dst': dst, 'edge_weight': edge_weight, 'L0_gnn_W': _L0_gnn_in['W'], 'L0_gnn_b': _L0_gnn_in['b'], 'L0_mix_w_qkv': _L0_mix_in['w_qkv'], 'L0_mix_w_out': _L0_mix_in['w_out'], 'L0_mix_b_out': _L0_mix_in['b_out'], 'L0_ffn_Wr': _L0_ffn_in['Wr'], 'L0_ffn_br': _L0_ffn_in['br'], 'L0_ffn_W1': _L0_ffn_in['W1'], 'L0_ffn_b1': _L0_ffn_in['b1'], 'L0_ffn_W2': _L0_ffn_in['W2'], 'L0_ffn_b2': _L0_ffn_in['b2'], 'L0_ffn_gamma': _L0_ffn_in['gamma'], 'L0_ffn_beta': _L0_ffn_in['beta'], 'L1_gnn_W1a': _L1_gnn_in['W1a'], 'L1_gnn_b1a': _L1_gnn_in['b1a'], 'L1_gnn_W1b': _L1_gnn_in['W1b'], 'L1_gnn_b1b': _L1_gnn_in['b1b'], 'L1_gnn_W2a': _L1_gnn_in['W2a'], 'L1_gnn_b2a': _L1_gnn_in['b2a'], 'L1_gnn_W2b': _L1_gnn_in['W2b'], 'L1_gnn_b2b': _L1_gnn_in['b2b'], 'L1_gnn_eps1': _L1_gnn_in['eps1'], 'L1_gnn_eps2': _L1_gnn_in['eps2'], 'L1_mix_t': _L1_mix_in['t'], 'L1_mix_w_qkv': _L1_mix_in['w_qkv'], 'L1_mix_mem_kv': _L1_mix_in['mem_kv'], 'L1_mix_w_out': _L1_mix_in['w_out'], 'L1_mix_b_out': _L1_mix_in['b_out'], 'L1_mix_g_out': _L1_mix_in['g_out'], 'L1_mix_g_pre': _L1_mix_in['g_pre'], 'L1_ffn_router_w1': _L1_ffn_in['router_w1'], 'L1_ffn_router_b1': _L1_ffn_in['router_b1'], 'L1_ffn_router_w2': _L1_ffn_in['router_w2'], 'L1_ffn_router_b2': _L1_ffn_in['router_b2'], 'L1_ffn_expert_w1': _L1_ffn_in['expert_w1'], 'L1_ffn_expert_b1': _L1_ffn_in['expert_b1'], 'L1_ffn_expert_w2': _L1_ffn_in['expert_w2'], 'L1_ffn_expert_b2': _L1_ffn_in['expert_b2'], 'L1_ffn_expert_w3': _L1_ffn_in['expert_w3'], 'L1_ffn_expert_b3': _L1_ffn_in['expert_b3']}

def reference(x, src, dst, edge_weight, L0_gnn_W, L0_gnn_b, L0_mix_w_qkv, L0_mix_w_out, L0_mix_b_out, L0_ffn_Wr, L0_ffn_br, L0_ffn_W1, L0_ffn_b1, L0_ffn_W2, L0_ffn_b2, L0_ffn_gamma, L0_ffn_beta, L1_gnn_W1a, L1_gnn_b1a, L1_gnn_W1b, L1_gnn_b1b, L1_gnn_W2a, L1_gnn_b2a, L1_gnn_W2b, L1_gnn_b2b, L1_gnn_eps1, L1_gnn_eps2, L1_mix_t, L1_mix_w_qkv, L1_mix_mem_kv, L1_mix_w_out, L1_mix_b_out, L1_mix_g_out, L1_mix_g_pre, L1_ffn_router_w1, L1_ffn_router_b1, L1_ffn_router_w2, L1_ffn_router_b2, L1_ffn_expert_w1, L1_ffn_expert_b1, L1_ffn_expert_w2, L1_ffn_expert_b2, L1_ffn_expert_w3, L1_ffn_expert_b3):
    import jax
    import jax.numpy as jnp

    def _L0_gnn_ref(x, edge_index, edge_weight, W, b):
        import jax, jax.numpy as jnp
        import numpy as np
        N_NODES = 3125
        K_HOPS = 2
        ALPHA = 0.5

        def _gcn_norm(edge_index, edge_weight, num_nodes):
            loops = jnp.arange(num_nodes, dtype=edge_index.dtype)
            src = jnp.concatenate([edge_index[0], loops])
            dst = jnp.concatenate([edge_index[1], loops])
            w = jnp.concatenate([edge_weight, jnp.ones((num_nodes,), edge_weight.dtype)])
            deg = jax.ops.segment_sum(w, dst, num_segments=num_nodes)
            dinv = jnp.where(deg > 0, jax.lax.rsqrt(jnp.maximum(deg, 1e-12)), 0.0)
            norm = dinv[src] * w * dinv[dst]
            return (src, dst, norm)
        N = x.shape[0]
        src, dst, norm = _gcn_norm(edge_index, edge_weight, N)
        h = x
        for _ in range(K_HOPS):
            msg = jax.ops.segment_sum(norm[:, None] * h[src], dst, num_segments=N)
            h = (1.0 - ALPHA) * msg + ALPHA * x
        h = jax.nn.relu(h)
        return h @ W.T + b

    def _L0_mix_ref(x, w_qkv, w_out, b_out):
        import jax, jax.numpy as jnp
        import numpy as np
        HEADS, DIM_HEAD = (8, 64)
        EPS = 1e-05

        def instance_norm(t):
            mu = jnp.mean(t, axis=-1, keepdims=True)
            var = jnp.mean((t - mu) ** 2, axis=-1, keepdims=True)
            return (t - mu) * jax.lax.rsqrt(var + EPS)
        B, N, _ = x.shape
        H, Dh = (HEADS, DIM_HEAD)
        qkv = jnp.einsum('bnd,ed->bne', x, w_qkv)
        q, k, v = jnp.split(qkv, 3, axis=-1)

        def to_heads(t):
            return t.reshape(B, N, H, Dh).transpose(0, 2, 1, 3)
        q, k, v = (to_heads(q), to_heads(k), to_heads(v))
        k = instance_norm(k)
        v = instance_norm(v)
        dots = jnp.einsum('bhnd,bhne->bhde', k, v)
        out = jnp.einsum('bhnd,bhde->bhne', q, dots) / N
        out = out.transpose(0, 2, 1, 3).reshape(B, N, H * Dh)
        return jnp.einsum('bne,de->bnd', out, w_out) + b_out

    def _L0_ffn_ref(x, Wr, br, W1, b1, W2, b2, gamma, beta):
        import math
        import jax, jax.numpy as jnp
        import numpy as np
        CAPACITY_FACTOR = 1.25
        TOP_K = 2
        LN_EPS = 1e-05

        def _layer_norm(x, gamma, beta):
            mu = jnp.mean(x, axis=-1, keepdims=True)
            var = jnp.var(x, axis=-1, keepdims=True)
            return (x - mu) * jax.lax.rsqrt(var + LN_EPS) * gamma + beta
        B, S, D = x.shape
        E = Wr.shape[1]
        N = B * S
        K = TOP_K
        logits = jnp.mean(x, axis=1) @ Wr + br
        routing_weights = jax.nn.softmax(logits, axis=-1)
        capacity = float(math.ceil(N * CAPACITY_FACTOR / E))
        expected_loads = routing_weights.sum(axis=0) * (N / B)
        scale = jnp.where(expected_loads > capacity, capacity / expected_loads, 1.0)
        routing_weights = jax.nn.softmax(routing_weights * scale, axis=-1)
        rw_tok = jnp.broadcast_to(routing_weights[:, None, :], (B, S, E)).reshape(N, E)
        top_w, top_i = jax.lax.top_k(rw_tok, K)
        top_w = jax.nn.softmax(top_w, axis=-1)
        xf = x.reshape(N, D)
        h = jax.nn.gelu(jnp.einsum('nd,edf->enf', xf, W1) + b1[:, None, :], approximate=False)
        y = jnp.einsum('enf,efd->end', h, W2) + b2[:, None, :]
        w_dense = jnp.zeros((N, E), x.dtype).at[jnp.arange(N)[:, None], top_i].add(top_w)
        out = jnp.einsum('ne,end->nd', w_dense, y).reshape(B, S, D)
        out = _layer_norm(out + x, gamma, beta)
        return out

    def _L1_gnn_ref(x, edge_index, W1a, b1a, W1b, b1b, W2a, b2a, W2b, b2b, eps1, eps2):
        import jax, jax.numpy as jnp
        import numpy as np
        N_NODES = 3125
        N_EDGES = 50000
        NFEAT, NHID, NCLASS = (256, 512, 256)

        def _init_params(key):
            ks = jax.random.split(key, 8)
            s = 0.02
            p = {'W1a': jax.random.normal(ks[0], (NFEAT, NHID), jnp.float32) * s, 'b1a': jnp.zeros((NHID,), jnp.float32), 'W1b': jax.random.normal(ks[1], (NHID, NHID), jnp.float32) * s, 'b1b': jnp.zeros((NHID,), jnp.float32), 'W2a': jax.random.normal(ks[2], (NHID, NHID), jnp.float32) * s, 'b2a': jnp.zeros((NHID,), jnp.float32), 'W2b': jax.random.normal(ks[3], (NHID, NCLASS), jnp.float32) * s, 'b2b': jnp.zeros((NCLASS,), jnp.float32), 'eps1': jnp.zeros((), jnp.float32), 'eps2': jnp.zeros((), jnp.float32)}
            return p

        def _gin_agg(h, src, dst, eps, n_nodes):
            agg = jax.ops.segment_sum(h[src], dst, num_segments=n_nodes)
            return (1.0 + eps) * h + agg
        src, dst = (edge_index[0], edge_index[1])
        n = x.shape[0]
        h = _gin_agg(x, src, dst, eps1, n)
        h = jax.nn.relu(h @ W1a + b1a)
        h = jax.nn.relu(h @ W1b + b1b)
        h = _gin_agg(h, src, dst, eps2, n)
        h = jax.nn.relu(h @ W2a + b2a)
        out = h @ W2b + b2b
        return out

    def _L1_mix_ref(x, t, w_qkv, mem_kv, w_out, b_out, g_out, g_pre):
        import jax, jax.numpy as jnp
        import numpy as np
        DIM = 256
        HEADS = 4
        DIM_HEAD = 32
        NUM_MEM = 4
        HIDDEN = HEADS * DIM_HEAD
        SCALE = DIM_HEAD ** (-0.5)

        def rmsnorm(x, g):
            n = jnp.linalg.norm(x, axis=-1, keepdims=True)
            return x / jnp.maximum(n, 1e-12) * g * x.shape[-1] ** 0.5
        b, n, c = x.shape
        xn = rmsnorm(x, g_pre)
        qkv = xn @ w_qkv
        q, k, v = jnp.split(qkv, 3, axis=-1)

        def to_heads(z):
            return z.reshape(b, n, HEADS, DIM_HEAD).transpose(0, 2, 3, 1)
        q, k, v = map(to_heads, (q, k, v))
        mk = jnp.broadcast_to(mem_kv[0], (b, HEADS, DIM_HEAD, NUM_MEM))
        mv = jnp.broadcast_to(mem_kv[1], (b, HEADS, DIM_HEAD, NUM_MEM))
        k = jnp.concatenate([mk, k], axis=-1)
        v = jnp.concatenate([mv, v], axis=-1)
        q = jax.nn.softmax(q, axis=-2) * SCALE
        k = jax.nn.softmax(k, axis=-1)
        context = jnp.einsum('bhdn,bhen->bhde', k, v)
        out = jnp.einsum('bhde,bhdn->bhen', context, q)
        out = out.transpose(0, 3, 1, 2).reshape(b, n, HIDDEN)
        out = rmsnorm(out @ w_out + b_out, g_out)
        return out + x

    def _L1_ffn_ref(features, router_w1, router_b1, router_w2, router_b2, expert_w1, expert_b1, expert_w2, expert_b2, expert_w3, expert_b3):
        import jax, jax.numpy as jnp
        import numpy as np
        E, D, H, TOP_K = (6, 256, 256, 2)
        ROUTER_H = D // 2
        rh = jax.nn.relu(features @ router_w1 + router_b1)
        expert_logits = jax.nn.softmax(rh @ router_w2 + router_b2, axis=-1)
        top_w, top_i = jax.lax.top_k(expert_logits, TOP_K)
        routing_weights = jax.nn.softmax(top_w, axis=-1)
        h1 = jax.nn.relu(jnp.einsum('bsd,edh->bseh', features, expert_w1) + expert_b1)
        h2 = jax.nn.relu(jnp.einsum('bseh,ehf->bsef', h1, expert_w2) + expert_b2)
        expert_out = jnp.einsum('bsef,efo->bseo', h2, expert_w3) + expert_b3
        sel = jnp.take_along_axis(expert_out, top_i[:, :, :, None], axis=2)
        combined = jnp.sum(sel * routing_weights[..., None], axis=2)
        return combined
    edge_index = jnp.stack([src, dst])
    xn = _layernorm(x, axis=-1)
    x = x + _L0_gnn_ref(xn, edge_index, edge_weight, L0_gnn_W, L0_gnn_b) + _L0_mix_ref(xn[None], L0_mix_w_qkv, L0_mix_w_out, L0_mix_b_out)[0]
    x = x + _L0_ffn_ref(_layernorm(x, axis=-1)[None], L0_ffn_Wr, L0_ffn_br, L0_ffn_W1, L0_ffn_b1, L0_ffn_W2, L0_ffn_b2, L0_ffn_gamma, L0_ffn_beta)[0]
    xn = _layernorm(x, axis=-1)
    x = x + _L1_gnn_ref(xn, edge_index, L1_gnn_W1a, L1_gnn_b1a, L1_gnn_W1b, L1_gnn_b1b, L1_gnn_W2a, L1_gnn_b2a, L1_gnn_W2b, L1_gnn_b2b, L1_gnn_eps1, L1_gnn_eps2) + _L1_mix_ref(xn[None], L1_mix_t, L1_mix_w_qkv, L1_mix_mem_kv, L1_mix_w_out, L1_mix_b_out, L1_mix_g_out, L1_mix_g_pre)[0]
    x = x + _L1_ffn_ref(_layernorm(x, axis=-1)[None], L1_ffn_router_w1, L1_ffn_router_b1, L1_ffn_router_w2, L1_ffn_router_b2, L1_ffn_expert_w1, L1_ffn_expert_b1, L1_ffn_expert_w2, L1_ffn_expert_b2, L1_ffn_expert_w3, L1_ffn_expert_b3)[0]
    return x

_drawn_inputs = setup_inputs


def setup_inputs(seed=0):
    import zlib

    import numpy as np

    out = dict(_drawn_inputs(seed))
    spreads = {'L0_ffn_br': (0.0, 0.8),
     'L0_ffn_b1': (0.0, 0.371),
     'L0_ffn_b2': (0.0, 0.1),
     'L0_ffn_gamma': (1.0, 0.2),
     'L0_ffn_beta': (0.0, 0.1),
     'L1_gnn_b1a': (0.0, 0.682),
     'L1_gnn_b1b': (0.0, 0.1),
     'L1_gnn_b2a': (0.0, 0.8),
     'L1_gnn_b2b': (0.0, 0.279),
     'L1_mix_b_out': (0.0, 0.1),
     'L1_mix_g_out': (1.0, 0.2),
     'L1_mix_g_pre': (1.0, 0.6),
     'L1_ffn_router_b1': (0.0, 0.589),
     'L1_ffn_router_b2': (0.0, 0.701),
     'L1_ffn_expert_b1': (0.0, 0.8),
     'L1_ffn_expert_b2': (0.0, 0.8),
     'L1_ffn_expert_b3': (0.0, 0.414)}
    factors = {'L0_gnn_b': 6.038,
     'L0_mix_b_out': 6.388,
     'L1_mix_w_qkv': 6.646,
     'L1_mix_mem_kv': 8.0,
     'L1_mix_w_out': 6.005,
     'L1_ffn_expert_w1': 3.916,
     'L1_ffn_expert_w2': 3.318}
    for name, (base, spread) in spreads.items():
        noise = np.random.default_rng([zlib.crc32(name.encode()), seed]).standard_normal(out[name].shape)
        drawn = base * np.exp(spread * noise) if base else spread * noise
        out[name] = jnp.asarray(drawn.astype(out[name].dtype))
    for name, factor in factors.items():
        out[name] = (out[name] * factor).astype(out[name].dtype)
    return out
```

```python
from contextlib import ExitStack

import concourse.bass as bass
from concourse import mybir

F32 = mybir.dt.float32
I32 = mybir.dt.int32
U32 = mybir.dt.uint32
ALU = mybir.AluOpType
ACT = mybir.ActivationFunctionType
AX = mybir.AxisListType.X

P = 128
NODES, D = 3125, 256
EDGES = 53125
T = -(-NODES // P)
LAST = NODES - (T - 1) * P
NP = T * P
WIDE = NP + P
U = 8
C = -(-EDGES // (P * U)) * U
ROUNDS = C // U
KC = D // P
HID = 512
HC = HID // P
SL = 400
SLICES = NP // SL
LN_EPS = 1e-5
H0, DH0 = 8, 64
E0, CAP_FACTOR = 8, 1.25
CAPACITY = float(-int(-(NODES * CAP_FACTOR) // E0))
GROUP = 5
HALF = GROUP * P // 2
H1, DH1, MEM = 4, 32, 4
HD1 = H1 * DH1
E1 = 6


class Bank:

    def __init__(self, eng, banks, wait_on, writer):
        self.eng, self.banks, self.wait_on, self.writer, self.n = eng, banks, wait_on, writer, 0

    def next(self):
        need = self.n + 1 - (len(self.banks) if self.writer else 0)
        if need > 0:
            self.eng.wait_ge(self.wait_on, need)
        bank = self.banks[self.n % len(self.banks)]
        self.n += 1
        return bank


class Steps:

    def __init__(self, eng, sem):
        self.eng, self.sem, self.n = eng, sem, 0

    def add(self, ins):
        ins.then_inc(self.sem, 1)
        self.n += 1

    def settle(self):
        self.eng.wait_ge(self.sem, self.n)

    def do(self, ins):
        self.add(ins)
        self.settle()


def build(nc, a, out, stop=None):
    with ExitStack() as ctx:
        def sb(name, shape, dt=F32):
            return ctx.enter_context(nc.sbuf_tensor(name, shape, dt))

        def sem(name):
            return ctx.enter_context(nc.semaphore(name))

        X = sb("X", [P, T, D])
        NN = sb("NN", [P, 2 * T * D])
        N = NN[:, 0:T * D].rearrange("p (t d) -> p t d", d=D)
        NT = NN[:, T * D:2 * T * D].rearrange("p (c n) -> p c n", n=NP)
        HT = NN[:, :].rearrange("p (c n) -> p c n", n=NP)
        HN = NN[:, :].rearrange("p (t d) -> p t d", d=HID)
        AS = sb("AS", [P, HC * WIDE])
        AT = AS[:, :].rearrange("p (c n) -> p c n", n=WIDE)
        rows = sb("rows", [P, U, HID])
        VB = sb("VB", [P, WIDE])
        WA = sb("WA", [P, 5120])
        WB = sb("WB", [P, 3072])
        onehot = sb("onehot", [P, U, P])
        src_i = sb("src_i", [P, C], I32)
        cur = sb("cur", [P, U], I32)
        rel = sb("rel", [P, C])
        wgt = sb("wgt", [P, C])
        base_i = sb("base_i", [1, ROUNDS], I32)
        first_base = sb("first_base", [1, ROUNDS], mybir.dt.uint16)
        passes_i = sb("passes_i", [1, 1], I32)
        ident = sb("ident", [P, P])
        ones = sb("ones", [P, P])
        iota_w = sb("iota_w", [P, P])
        small = sb("small", [P, 1024])
        bias_b = sb("bias_b", [P, D])

        ps = [ctx.enter_context(nc.psum_tensor(f"ps{i}", [P, 512], F32)) for i in range(8)]
        TA, TV, PACC = ps[0:4], ps[4:7], ps[7]

        stats = small[:, 0:150].rearrange("p (t s) -> p t s", s=6)
        mv = small[:, 150:200].rearrange("p (t s) -> p t s", s=2)
        rstd = small[:, 200:225]
        valid = small[:, 225:250]
        iota_p = small[:, 250:251]
        sc = small[:, 256:640]
        eps_c = small[:, 251:253]
        cols = small[:, 640:1024]

        table = [nc.dram_tensor(f"table{i}", (NP, HID if i == 3 else D), F32, kind="Internal").ap()
                 for i in range(4)]

        pa_full, pa_free = sem("pa_full"), sem("pa_free")
        pv_full, pv_free = sem("pv_full"), sem("pv_free")
        dve_step, act_step, pool_step = sem("dve_step"), sem("act_step"), sem("pool_step")
        x_zeroed, x_loaded = sem("x_zeroed"), sem("x_loaded")
        edges_loaded, dst_loaded = sem("edges_loaded"), sem("dst_loaded")
        consts_ready = sem("consts_ready")
        wa_loaded = [sem("wa0_loaded"), sem("wa1_loaded")]
        wb_loaded = sem("wb_loaded")
        ranges_ready, range_mm, diag_ready = sem("ranges_ready"), sem("range_mm"), sem("diag_ready")
        xn_ready, nt_ready = sem("xn_ready"), sem("nt_ready")
        edge_wait = sem("edge_wait")
        idx_ready = [sem(f"idx_ready{h}") for h in range(4)]
        gathered = [[sem(f"gathered{h}_{k}") for k in range(U)] for h in range(4)]
        onehot_ready = [sem(f"onehot_ready{h}") for h in range(5)]
        product_done = [sem(f"product_done{h}") for h in range(5)]
        added = [sem(f"added{h}") for h in range(5)]
        pass_ready = [sem(f"pass_ready{h}") for h in range(5)]
        table_sbuf = [sem(f"table_sbuf{h}") for h in range(4)]
        table_written = [sem(f"table_written{h}") for h in range(4)]
        at_ready = sem("at_ready")
        out_stored = sem("out_stored")
        stored_ready = sem("stored_ready")
        kv_ready, kv_normed, kv_used = sem("kv_ready"), sem("kv_normed"), sem("kv_used")
        wkv_centred = sem("wkv_centred")
        mix_mm, mix_sb = sem("mix_mm"), sem("mix_sb")
        layer_mm = sem("layer_mm")
        bias_loaded = sem("bias_loaded")
        route_mm, route_sb = sem("route_mm"), sem("route_sb")
        expert_loaded = sem("expert_loaded")
        w2_scaled, w2b_loaded = sem("w2_scaled"), sem("w2b_loaded")
        rn_ready, norm_asked = sem("rn_ready"), sem("norm_asked")
        experts_loaded = [sem("experts0_loaded"), sem("experts1_loaded")]
        experts_gathered, idx0_ready = sem("experts_gathered"), sem("idx0_ready")
        cols_loaded, b2_loaded = sem("cols_loaded"), sem("b2_loaded")
        w1_loaded, w1_used = sem("w1_loaded"), sem("w1_used")
        qk_ready = sem("qk_ready")
        asked, answered = sem("asked"), sem("answered")

        def load(eng, dst, src, s):
            eng.dma_start(dst, src).then_inc(s, 16)

        block = ctx.enter_context(nc.Block())
        DUMP = {"ln": 0, "deg": 0, "mix": 1, "gnn0": 2, "ffn0": 3, "mix1": 4, "gnn1": 5}
        level = DUMP.get(stop, 99)

        wkvT = WA[:, 0:2048].rearrange("p (c n) -> p c n", n=1024)
        wq = WA[:, 2048:3072].rearrange("p (j f) -> p j f", f=D)
        woT = WA[:, 3072:4096].rearrange("p (j f) -> p j f", f=D)
        wgT = WA[:, 4096:4608].rearrange("p (c f) -> p c f", f=D)
        mixM = WA[:, 4608:5120].rearrange("p (c f) -> p c f", f=D)
        bdT = AS[:, 5120:5632].rearrange("p (j d) -> p j d", d=P)
        w1g = WA[:, 0:2048].rearrange("p (e c f) -> p e c f", c=KC, f=HID)
        w2g = WA[:, 2048:4096].rearrange("p (e c f) -> p e c f", c=HC, f=D)
        hG = AS[:, 0:2 * 8 * GROUP * P].rearrange("p (b c n) -> p b c n", c=8, n=GROUP * P)
        rflat = rows[:, :, :].rearrange("p u d -> p (u d)")
        b2g = rflat[:, 0:512].rearrange("p (e f) -> p e f", f=D)
        gamma_b, beta_b, b2c = rflat[:, 512:768], rflat[:, 768:1024], rflat[:, 1024:1280]
        ybar = rflat[:, 1280:1536].rearrange("p (c m) -> p c m", m=P)
        w1a = WA[:, 0:1024].rearrange("p (c f) -> p c f", f=HID)
        w1b = WA[:, 1024:3072].rearrange("p (c f) -> p c f", f=HID)
        w2a = WA[:, 3072:5120].rearrange("p (c f) -> p c f", f=HID)
        w2b = WA[:, 0:1024].rearrange("p (c f) -> p c f", f=D)
        wqkv = WB[:, 0:768].rearrange("p (c f) -> p c f", f=3 * HD1)
        wout1 = WB[:, 768:1024]
        memk, memv = WB[0:MEM, 1024:1152], WB[0:MEM, 1152:1280]
        gout_b, bout_b, b2b_b = WB[:, 1280:1536], WB[:, 1536:1792], WB[:, 1792:2048]
        rw1 = WB[:, 2048:2304].rearrange("p (c f) -> p c f", f=P)
        rw2 = WB[:, 2304:2304 + E1]
        b3 = WB[0:E1, 2560:2816]
        mixb_b = WB[:, 2816:3072]
        qkv = AS[:, 0:3 * NP].rearrange("p (s t c) -> p s t c", s=3, c=HD1)
        Y = AS[:, 0:T * D].rearrange("p (t d) -> p t d", d=D)
        qT = VB[:, 0:NP]
        junk = rflat[:, 0:256]
        kmax, diag1, ctx_bd = rflat[:, 256:384], rflat[:, 384:512], rflat[:, 512:640]
        m2 = rflat[:, 640:896]
        rn = rflat[:, 896:896 + T]
        qstat = rflat[:, 1024:1024 + T * H1]
        we = WA[:, 0:3072].rearrange("p (b l c f) -> p b l c f", b=2, l=3, f=D)
        h1 = AS[:, 0:KC * NP].rearrange("p (c n) -> p c n", n=NP)
        h2 = AS[:, KC * NP:2 * KC * NP].rearrange("p (c n) -> p c n", n=NP)
        wT = rflat[0:E1, 0:NP]
        route = [WA[:, 3072 + 150 * i:3222 + 150 * i].rearrange("p (t e) -> p t e", e=E1) for i in range(6)]
        rcol = [WA[:, 4000 + 32 * i:4000 + 32 * i + T] for i in range(8)]
        memkT, gpre = cols[:, 0:4], cols[:, 4:6]
        b1a, b1b, b2a = cols[:, 6:10], cols[:, 10:14], cols[:, 14:18]
        eb1, eb2 = cols[:, 18:30], cols[:, 30:42]
        rb1, rb2 = cols[:, 42:43], cols[:, 43:49]
        wr = cols[:, 49:65].rearrange("p (c e) -> p c e", e=E0)
        br = cols[:, 65:73]
        eps_in = cols[:, 73:75]
        b1g = cols[:, 80:88]
        gidx = cols[:, 96:112].bitcast(I32)
        iota4, iota6 = cols[:, 112:116], cols[:, 116:122]
        V_GNN0, V_FFN0 = 1 + T, 1 + 2 * T
        A_QKV = T + 2 * T + 4 + KC + 2 * T + T + GROUP * 16 + T + T
        V_MIX1 = V_FFN0 + 3 + T
        V_GNN1 = V_MIX1 + T
        V_B3 = V_GNN1 + T
        kv = AS[:, 0:2048].rearrange("p (b n) -> p b n", n=1024)
        kvsq = AS[:, 2048:4096].rearrange("p (b n) -> p b n", n=1024)
        pj = AS[:, 4096:5120].rearrange("p (j f) -> p j f", f=D)

        def hop_width(h):
            return {0: 1, 1: 2, 2: 2, 3: 2, 4: 4}[h]

        @block.sync
        def _(sp):
            load(sp, src_i[:, :], a["src_pc"], edges_loaded)
            load(sp, wgt[:, :], a["wgt_pc"], edges_loaded)
            load(sp, rel[:, :].bitcast(I32), a["dst_pc"], edges_loaded)
            load(sp, AS[0:ROUNDS, 0:U * P].bitcast(I32), a["dst_rounds"], dst_loaded)
            sp.wait_ge(x_zeroed, 1)
            load(sp, X[:, 0:T - 1, :], a["x"][0:(T - 1) * P, :].rearrange("(t p) d -> p t d", p=P), x_loaded)
            load(sp, X[0:LAST, T - 1, :], a["x"][(T - 1) * P:NODES, :], x_loaded)
            load(sp, WA[:, 0:2048], a["wkvT"], wa_loaded[0])
            load(sp, WA[:, 2048:3072], a["wq"], wa_loaded[0])
            load(sp, WA[:, 3072:4096], a["woT"], wa_loaded[0])
            load(sp, WA[:, 4096:4608], a["wgT"], wa_loaded[0])
            load(sp, bias_b[:, :], a["L0_gnn_b"].partition_broadcast(P), bias_loaded)
            load(sp, mixb_b, a["L0_mix_b_out"].partition_broadcast(P), bias_loaded)
            load(sp, cols[:, 0:75], a["cols"], cols_loaded)
            for dst, src in ((WB[:, 0:768], "wqkv1"), (wout1, "L1_mix_w_out"), (memk, "memk"), (memv, "memv"),
                             (WB[:, 2048:2304], "rw1"), (rw2, "L1_ffn_router_w2"), (b3, "L1_ffn_expert_b3")):
                load(sp, dst, a[src], wb_loaded)
            for dst, src in ((gout_b, "L1_mix_g_out"), (bout_b, "L1_mix_b_out"), (b2b_b, "L1_gnn_b2b")):
                load(sp, dst, a[src].partition_broadcast(P), wb_loaded)
            if level >= 2:
                for h in range(2):
                    sp.wait_ge(table_sbuf[h], T)
                    load(sp, table[h].rearrange("(t p) d -> p t d", p=P), N, table_written[h])
            if level >= 3:
                sp.wait_ge(pv_full, V_GNN0)
                load(sp, gamma_b, a["L0_ffn_gamma"].partition_broadcast(P), b2_loaded)
                load(sp, beta_b, a["L0_ffn_beta"].partition_broadcast(P), b2_loaded)
            if level >= 4:
                sp.wait_ge(pv_full, V_FFN0)
                load(sp, WA[:, 0:1024], a["w1a"], w1_loaded)
                load(sp, WA[:, 1024:3072], a["w1b"], w1_loaded)
                load(sp, WA[:, 3072:5120], a["w2a"], w1_loaded)
                sp.wait_ge(xn_ready, 3 * T)
                load(sp, table[2].rearrange("(t p) d -> p t d", p=P), N, table_written[2])
            if level >= 5:
                sp.wait_ge(w1_used, 1)
                load(sp, WA[:, 0:1024], a["w2b"], w2b_loaded)
                sp.wait_ge(table_sbuf[3], T)
                load(sp, table[3].rearrange("(t p) d -> p t d", p=P), HN, table_written[3])
            if level >= 6:
                for e in range(E1):
                    sp.wait_ge(pv_full, V_GNN1 if e < 2 else V_B3 + T * (e - 1))
                    load(sp, WA[:, (e % 2) * 1536:(e % 2) * 1536 + 1536], a["experts1"][e], experts_loaded[e % 2])
            sp.wait_ge(stored_ready, 1)
            load(sp, out[0:(T - 1) * P, :].rearrange("(t p) d -> p t d", p=P), X[:, 0:T - 1, :], out_stored)
            load(sp, out[(T - 1) * P:NODES, :], X[0:LAST, T - 1, :], out_stored)
            sp.wait_ge(out_stored, 32)

        def gather_pass(pool, st, h):
            sems = gathered[h - 1]
            pool.wait_ge(table_written[h - 1], 16)
            pool.wait_ge(ranges_ready, 2)
            windows = pool.value_load(passes_i[0:1, 0:1], min_val=1, max_val=T)
            with pool.Fori(0, windows) as w:
                with pool.Fori(0, ROUNDS) as i:
                    r = pool.snap(w * ROUNDS + i)
                    for half in range(2):
                        pool.wait_ge(product_done[h], r * U + half * 4 + 4)
                        pool.sem_inc(edge_wait, 1)
                        nc.gpsimd.tensor_copy(cur[:, half * 4:half * 4 + 4],
                                              src_i[:, bass.ds(i * U + half * 4, 4)]).then_inc(idx_ready[h - 1], 1)
                        pool.wait_ge(idx_ready[h - 1], r * 2 + half + 1)
                        pool.sem_inc(edge_wait, 1)
                        for k in range(half * 4, half * 4 + 4):
                            nc.gpsimd.indirect_dma_start(
                                rows[:, k, 0:hop_width(h) * P], None, table[h - 1][:, :],
                                bass.IndirectOffsetOnAxis(cur[:, k:k + 1], 0)).then_inc(sems[k], 16)

        def product_pass(pe, h):
            pe.sem_inc(product_done[h], U)
            pe.wait_ge(ranges_ready, 2)
            windows = pe.value_load(passes_i[0:1, 0:1], min_val=1, max_val=T)
            with pe.Fori(0, windows) as w:
                with pe.Fori(0, ROUNDS // 2) as i:
                    for j in range(2):
                        r = pe.snap(w * ROUNDS + i * 2 + j)
                        pe.wait_ge(added[h], r + 1)
                        for k in range(U):
                            pe.wait_ge(onehot_ready[h], r * U + k + 1)
                            if h:
                                pe.wait_ge(gathered[h - 1][k], r * 16 + 16)
                            for c in range(hop_width(h)):
                                lhs = rows[:, k, c * P:(c + 1) * P] if h else ones[:, :]
                                mm = nc.tensor.matmul(ps[4 + j][:, c * P:(c + 1) * P], lhs, onehot[:, k, :],
                                                      start=(k == 0 and c == 0), stop=(k == U - 1), skip_group_check=True)
                            mm.then_inc(product_done[h], 1)

        def add_pass(dve, st, h):
            if h:
                st.add(nc.vector.tensor_copy(base_i[:, :], first_base[:, :]))
                st.do(nc.vector.tensor_copy(sc[:, 26:27], iota_w[:, 0:1]))
                st.do(nc.vector.tensor_scalar(iota_w[:, :], iota_w[:, :], sc[:, 26:27], None, ALU.subtract))
            dve.sem_inc(added[h], 2)
            target = AT if h else VB[:, :].rearrange("p (c n) -> p c n", c=1)
            nch = hop_width(h)
            windows = dve.value_load(passes_i[0:1, 0:1], min_val=1, max_val=T)
            with dve.Fori(0, windows) as w:
                with dve.Fori(0, ROUNDS // 2) as i:
                    for j in range(2):
                        r = dve.snap(w * ROUNDS + i * 2 + j)
                        for k in range(U):
                            c = i * 2 * U + j * U + k
                            dve.wait_ge(product_done[h], r * U + k + 1)
                            nc.vector.tensor_scalar(onehot[:, k, :], iota_w[:, :], rel[:, bass.ds(c, 1)], wgt[:, bass.ds(c, 1)],
                                                    ALU.is_equal, ALU.mult).then_inc(onehot_ready[h], 1)
                        b = dve.value_load(base_i[0:1, bass.ds(i * 2 + j, 1)], min_val=0, max_val=NP)
                        dve.wait_ge(added[h], r + 2)
                        dve.wait_ge(product_done[h], r * U + 2 * U)
                        win = target[:, 0:nch, bass.ds(b, P)]
                        nc.vector.tensor_tensor(win, win, ps[4 + j][:, 0:nch * P].rearrange(
                            "p (c n) -> p c n", n=P), ALU.add).then_inc(added[h], 1)
                dve.wait_ge(onehot_ready[h], w * C + C)
                dve.sem_inc(edge_wait, 1)
                nc.vector.tensor_scalar(iota_w[:, :], iota_w[:, :], float(P), None, ALU.add).then_inc(pass_ready[h], 1)
                dve.wait_ge(pass_ready[h], w * 2 + 1)
                nc.vector.tensor_scalar(base_i[:, :], base_i[:, :], P, NP, ALU.add, ALU.min).then_inc(pass_ready[h], 1)
                dve.wait_ge(pass_ready[h], w * 2 + 2)
            dve.wait_ge(added[h], 2 + ROUNDS)

        @block.gpsimd
        def _(pool):
            st = Steps(pool, pool_step)
            nc.gpsimd.memset(X[:, T - 1, :], 0.0).then_inc(x_zeroed, 1)
            st.add(nc.gpsimd.memset(ident[:, :], 1.0))
            st.add(nc.gpsimd.memset(ones[:, :], 1.0))
            st.do(nc.gpsimd.memset(valid, 1.0))
            st.add(nc.gpsimd.affine_select(out=ident[:, :], in_=ident[:, :], compare_op=ALU.is_equal, fill=0.0,
                                           base=0, pattern=[[-1, P]], channel_multiplier=1))
            st.add(nc.gpsimd.affine_select(out=valid, in_=valid, compare_op=ALU.is_ge, fill=0.0,
                                           base=NODES - 1, pattern=[[-P, T]], channel_multiplier=-1))
            st.add(nc.gpsimd.iota(iota_w[:, :], pattern=[[1, P]], base=0, channel_multiplier=0,
                                  allow_small_or_imprecise_dtypes=True))
            st.add(nc.gpsimd.iota(iota_p, pattern=[[0, 1]], base=0, channel_multiplier=1,
                                  allow_small_or_imprecise_dtypes=True))
            pool.wait_ge(cols_loaded, 16)
            st.add(nc.gpsimd.iota(iota4, pattern=[[P, 4]], base=0, channel_multiplier=1,
                                  allow_small_or_imprecise_dtypes=True))
            st.add(nc.gpsimd.iota(iota6, pattern=[[1, E1]], base=0, channel_multiplier=0,
                                  allow_small_or_imprecise_dtypes=True))
            st.settle()
            if level >= 2:
                gather_pass(pool, st, 1)
                gather_pass(pool, st, 2)
            if level >= 3:
                pool.wait_ge(idx0_ready, 1)
                pool.wait_ge(pv_full, V_GNN0)
                pool.sem_inc(edge_wait, 1)
                for e in range(2):
                    for c in range(KC):
                        nc.gpsimd.indirect_dma_start(w1g[:, e, c, :], None, a["w1_rows"][:, :], bass.IndirectOffsetOnAxis(
                            gidx[:, 8 * e + c:8 * e + c + 1], 0)).then_inc(experts_gathered, 16)
                    for c in range(HC):
                        nc.gpsimd.indirect_dma_start(w2g[:, e, c, :], None, a["w2_rows"][:, :], bass.IndirectOffsetOnAxis(
                            gidx[:, 8 * e + 2 + c:8 * e + 3 + c], 0)).then_inc(experts_gathered, 16)
                    nc.gpsimd.indirect_dma_start(b1g[:, 4 * e:4 * e + 4], None, a["b1_rows"][:, :], bass.IndirectOffsetOnAxis(
                        gidx[:, 8 * e + 6:8 * e + 7], 0)).then_inc(experts_gathered, 16)
                    nc.gpsimd.indirect_dma_start(b2g[:, e, :], None, a["b2_rows"][:, :], bass.IndirectOffsetOnAxis(
                        gidx[:, 8 * e + 7:8 * e + 8], 0)).then_inc(experts_gathered, 16)
            if level >= 5:
                gather_pass(pool, st, 3)
                gather_pass(pool, st, 4)

        def transposes(pe, bank, src, k):
            for t in range(T):
                o = bank.next()
                for c in range(k):
                    mm = nc.tensor.transpose(o[:, c * P:(c + 1) * P], src(t, c), ident[:, :])
                mm.then_inc(pa_full, 1)

        @block.tensor
        def _(pe):
            A = Bank(pe, TA, pa_free, True)
            V = Bank(pe, TV, pv_free, True)
            pe.wait_ge(pool_step, 7)
            pe.wait_ge(diag_ready, 1)
            nc.tensor.matmul(PACC[:, 0:ROUNDS], ones[0:ROUNDS, :], sc[0:ROUNDS, 0:ROUNDS],
                             start=True, stop=True).then_inc(range_mm, 1)
            pe.wait_ge(diag_ready, 2)
            nc.tensor.transpose(V.next()[0:1, 0:ROUNDS], sc[0:ROUNDS, 82:83], ident[0:ROUNDS, 0:ROUNDS]).then_inc(pv_full, 1)

            def normalised_transposed(first):
                for t in range(T):
                    pe.wait_ge(xn_ready, first * T + t + 1)
                    o = A.next()
                    for c in range(KC):
                        mm = nc.tensor.transpose(o[:, c * P:(c + 1) * P], N[:, t, c * P:(c + 1) * P], ident[:, :])
                    mm.then_inc(pa_full, 1)

            normalised_transposed(0)
            if level < 1:
                product_pass(pe, 0)
                return
            pe.wait_ge(wkv_centred, 1)
            for t in range(T + 1):
                if t < T:
                    pe.wait_ge(nt_ready, t + 1)
                    for half in range(2):
                        o = A.next()
                        for c in range(KC):
                            mm = nc.tensor.matmul(o[:, :], NT[:, c, t * P:(t + 1) * P], wkvT[:, c, half * 512:(half + 1) * 512],
                                                  start=(c == 0), stop=(c == KC - 1))
                        mm.then_inc(pa_full, 1)
                if t >= 1:
                    pe.wait_ge(kv_normed, t)
                    b = (t - 1) % 2
                    for j in range(4):
                        mm = nc.tensor.matmul(PACC[:, j * P:(j + 1) * P], kv[:, b, 512 + j * P:512 + (j + 1) * P],
                                              kv[:, b, j * P:(j + 1) * P], start=(t == 1 and j == 0),
                                              stop=(t == T), skip_group_check=True)
                    mm.then_inc(kv_used, 1)
            pe.wait_ge(mix_sb, 1)
            for j in range(4):
                o = A.next()
                nc.tensor.matmul(o[:, 0:D], bdT[:, j, :], woT[:, j, :], start=True, stop=True).then_inc(pa_full, 1)
            pe.wait_ge(mix_sb, 5)
            for c in range(KC):
                o = A.next()
                for j in range(4):
                    mm = nc.tensor.matmul(o[:, 0:D], wq[:, j, c * P:(c + 1) * P], pj[:, j, :], start=(j == 0), stop=(j == 3))
                mm.then_inc(pa_full, 1)
            product_pass(pe, 0)
            if level < 2:
                return
            for h in (1, 2):
                pe.wait_ge(at_ready, h)
                transposes(pe, A, lambda t, c: AT[:, c, t * P:(t + 1) * P], KC)
                product_pass(pe, h)
            pe.wait_ge(at_ready, 3)
            for t in range(T):
                o = V.next()
                for n, (lhs, rhs) in enumerate([(AT[:, c, t * P:(t + 1) * P], wgT[:, c, :]) for c in range(KC)]
                                               + [(NT[:, c, t * P:(t + 1) * P], mixM[:, c, :]) for c in range(KC)]):
                    mm = nc.tensor.matmul(o[:, 0:D], lhs, rhs, start=(n == 0), stop=(n == 3))
                mm.then_inc(pv_full, 1)
            if level < 3:
                return

            normalised_transposed(1)
            for c in range(KC):
                for t in range(T):
                    mm = nc.tensor.matmul(PACC[:, c:c + 1], N[:, t, c * P:(c + 1) * P], valid[:, t:t + 1],
                                          start=(t == 0), stop=(t == T - 1))
            mm.then_inc(route_mm, 1)
            pe.wait_ge(route_sb, 1)
            pe.wait_ge(cols_loaded, 16)
            for c in range(KC):
                mm = nc.tensor.matmul(PACC[:, 8:8 + E0], ybar[:, c, :], wr[:, c, :], start=(c == 0), stop=(c == KC - 1))
            mm.then_inc(route_mm, 1)
            pe.wait_ge(experts_gathered, 256)
            pe.wait_ge(nt_ready, 2 * T)
            first_done = [0] * GROUP
            for g in range(GROUP + 1):
                if g < GROUP:
                    for c in range(8):
                        for half in range(2):
                            o = A.next()
                            n0 = g * GROUP * P + half * HALF
                            for k in range(KC):
                                mm = nc.tensor.matmul(o[:, 0:HALF], w1g[:, c // 4, k, (c % 4) * P:(c % 4 + 1) * P],
                                                      NT[:, k, n0:n0 + HALF], start=(k == 0), stop=(k == KC - 1))
                            mm.then_inc(pa_full, 1)
                    first_done[g] = A.n
                if g >= 1:
                    pe.wait_ge(pa_free, first_done[g - 1])
                    if g == 1:
                        pe.wait_ge(w2_scaled, 1)
                    for t in range(GROUP):
                        o = V.next()
                        for c in range(8):
                            mm = nc.tensor.matmul(o[:, 0:D], hG[:, (g - 1) % 2, c, t * P:(t + 1) * P], w2g[:, c // 4, c % 4, :],
                                                  start=(c == 0), stop=(c == 7))
                        mm.then_inc(pv_full, 1)
            assert V.n == V_FFN0
            if level < 4:
                return

            normalised_transposed(2)
            pe.wait_ge(mix_sb, 7)
            for t in range(T):
                pe.wait_ge(nt_ready, 2 * T + t + 1)
                o = A.next()
                for c in range(KC):
                    mm = nc.tensor.matmul(o[:, 0:3 * HD1], NT[:, c, t * P:(t + 1) * P], wqkv[:, c, :],
                                          start=(c == 0), stop=(c == KC - 1))
                mm.then_inc(pa_full, 1)
            pe.wait_ge(qk_ready, 1)
            nc.tensor.transpose(V.next()[:, 0:P], kmax, ident[:, :]).then_inc(pv_full, 1)
            pe.wait_ge(qk_ready, 2)
            nc.tensor.matmul(V.next()[:, 0:P], ones[:, :], diag1, start=True, stop=True).then_inc(pv_full, 1)
            pe.wait_ge(qk_ready, 3)
            for t in range(T):
                nc.tensor.transpose(A.next()[:, 0:P], qkv[:, 0, t, :], ident[:, :]).then_inc(pa_full, 1)
            queries_turned = A.n
            pe.wait_ge(qk_ready, 4)
            for t in range(T):
                m = P if t < T - 1 else LAST
                nc.tensor.matmul(PACC[:, 0:P], qkv[0:m, 2, t, :], qkv[0:m, 1, t, :], start=(t == 0), stop=False)
            mm = nc.tensor.matmul(PACC[:, 0:P], memv, memk, start=False, stop=True)
            for t in range(T):
                m = P if t < T - 1 else LAST
                nc.tensor.matmul(PACC[:, P:P + 1], qkv[0:m, 1, t, :], ones[0:m, 0:1], start=(t == 0), stop=False)
            nc.tensor.matmul(PACC[:, P:P + 1], memk, ones[0:MEM, 0:1], start=False, stop=True).then_inc(mix_mm, 1)
            pe.wait_ge(qk_ready, 5)
            nc.tensor.matmul(V.next()[:, 0:D], ctx_bd, wout1, start=True, stop=True).then_inc(pv_full, 1)
            pe.wait_ge(qk_ready, 6)
            pe.wait_ge(pa_free, queries_turned)
            for t in range(T):
                nc.tensor.matmul(V.next()[:, 0:D], qT[:, t * P:(t + 1) * P], m2, start=True, stop=True).then_inc(pv_full, 1)
            assert V.n == V_MIX1
            if level < 5:
                return

            def wide(weights, src, chunks, ready):
                ends = []
                for s in range(SLICES):
                    if ready:
                        pe.wait_ge(pa_free, ready[s])
                    for c in range(weights.shape[2] // P):
                        o = A.next()
                        for k in range(chunks):
                            mm = nc.tensor.matmul(o[:, 0:SL], weights[:, k, c * P:(c + 1) * P], src[:, k, s * SL:(s + 1) * SL],
                                                  start=(k == 0), stop=(k == chunks - 1))
                        mm.then_inc(pa_full, 1)
                    ends.append(A.n)
                return ends

            pe.wait_ge(at_ready, 4)
            product_pass(pe, 3)
            pe.wait_ge(w1_loaded, 48)
            pe.wait_ge(added[3], 2 + ROUNDS)
            pe.wait_ge(at_ready, 5)
            ends = wide(w1a, AT, KC, None)
            ends = wide(w1b, HT, HC, ends)
            pe.wait_ge(pa_free, A.n)
            pe.sem_inc(w1_used, 1)
            transposes(pe, A, lambda t, c: AT[:, c, t * P:(t + 1) * P], HC)
            pe.wait_ge(at_ready, 6)
            product_pass(pe, 4)
            pe.wait_ge(at_ready, 7)
            wide(w2a, AT, HC, None)
            pe.wait_ge(pa_free, A.n)
            pe.wait_ge(w2b_loaded, 16)
            for t in range(T):
                o = V.next()
                for c in range(HC):
                    mm = nc.tensor.matmul(o[:, 0:D], HT[:, c, t * P:(t + 1) * P], w2b[:, c, :], start=(c == 0), stop=(c == HC - 1))
                mm.then_inc(pv_full, 1)
            assert V.n == V_GNN1
            if level < 6:
                return

            normalised_transposed(3)
            pe.wait_ge(nt_ready, 4 * T)
            ends = wide(rw1, NT, KC, None)
            for t in range(T):
                pe.wait_ge(pa_free, ends[((t + 1) * P - 1) // SL])
                mm = nc.tensor.matmul(PACC[:, t * E1:(t + 1) * E1], VB[:, t * P:(t + 1) * P], rw2, start=True, stop=True)
            mm.then_inc(route_mm, 1)
            pe.wait_ge(route_sb, 2)
            for q in range(0, T, 4):
                o = A.next()
                for t in range(q, min(q + 4, T)):
                    mm = nc.tensor.transpose(o[0:E1, (t - q) * P:(t - q + 1) * P], route[5][:, t, :], ident[:, :])
                mm.then_inc(pa_full, 1)
            pe.wait_ge(pa_free, A.n)
            for t in range(T):
                nc.tensor.matmul(V.next()[:, 0:D], wT[:, t * P:(t + 1) * P], b3, start=True, stop=True).then_inc(pv_full, 1)
            assert V.n == V_B3
            for e in range(E1):
                w = we[:, e % 2]
                pe.wait_ge(experts_loaded[e % 2], 16 * (e // 2 + 1))
                ends = wide(w[:, 0], NT, KC, None)
                ends = wide(w[:, 1], h1, KC, ends)
                for t in range(T):
                    pe.wait_ge(pa_free, ends[((t + 1) * P - 1) // SL])
                    o = V.next()
                    for k in range(KC):
                        mm = nc.tensor.matmul(o[:, 0:D], h2[:, k, t * P:(t + 1) * P], w[:, 2, k, :], start=(k == 0), stop=(k == KC - 1))
                    mm.then_inc(pv_full, 1)

        @block.scalar
        def _(act):
            A = Bank(act, TA, pa_full, False)
            st = Steps(act, act_step)
            roots = [0]

            def root(v):
                roots[0] += 1
                act.wait_ge(asked, roots[0])
                nc.scalar.activation(v, v, ACT.Sqrt).then_inc(answered, 1)

            def exp(v):
                roots[0] += 1
                act.wait_ge(asked, roots[0])
                nc.scalar.activation(v, v, ACT.Exp).then_inc(answered, 1)

            def transposed_copies():
                for t in range(T):
                    o = A.next()
                    nc.scalar.copy(NT[:, :, t * P:(t + 1) * P], o[:, 0:D].rearrange("p (c n) -> p c n", n=P)).then_inc(pa_free, 1)
                    act.wait_ge(pa_free, A.n)
                    act.sem_inc(nt_ready, 1)

            root(rstd)
            transposed_copies()
            if level < 1:
                root(VB[:, :])
                return
            for t in range(T + 1):
                b = t % 2
                if t == T:
                    root(sc[:, 256 + 32 * (1 - b):256 + 32 * (1 - b) + 16])
                    break
                if t >= 2:
                    act.wait_ge(kv_used, t - 1)
                for half in range(2):
                    o = A.next()
                    cut = slice(half * 512, (half + 1) * 512)
                    nc.scalar.copy(kv[:, b, cut], o[:, :]).then_inc(kv_ready, 1)
                    nc.scalar.activation(kvsq[:, b, cut], o[:, :], ACT.Square).then_inc(pa_free, 1)
                if t >= 1:
                    root(sc[:, 256 + 32 * (1 - b):256 + 32 * (1 - b) + 16])
            for j in range(4):
                o = A.next()
                nc.scalar.mul(pj[:, j, :], o[:, 0:D], 1.0 / NODES).then_inc(pa_free, 1)
            act.wait_ge(pa_free, A.n)
            act.sem_inc(mix_sb, 4)
            for c in range(KC):
                o = A.next()
                nc.scalar.copy(mixM[:, c, :], o[:, 0:D]).then_inc(pa_free, 1)
            act.wait_ge(pa_free, A.n)
            act.sem_inc(mix_sb, 1)
            root(VB[:, :])
            if level < 2:
                return
            for h in (1, 2):
                if h == 2:
                    act.wait_ge(table_written[0], 16)
                for t in range(T):
                    o = A.next()
                    nc.scalar.copy(N[:, t, :], o[:, 0:D]).then_inc(pa_free, 1)
                    act.wait_ge(pa_free, A.n)
                    act.sem_inc(table_sbuf[h - 1], 1)
            if level < 3:
                return

            root(rstd)
            transposed_copies()
            exp(sc[:, 0:8])
            exp(sc[:, 0:8])
            exp(sc[:, 40:41])
            act.wait_ge(experts_gathered, 256)
            for g in range(GROUP):
                for c in range(8):
                    for half in range(2):
                        o = A.next()
                        nc.scalar.activation(hG[:, g % 2, c, half * HALF:(half + 1) * HALF], o[:, 0:HALF], ACT.Gelu,
                                             bias=b1g[:, c:c + 1]).then_inc(pa_free, 1)
            root(rstd)
            if level < 4:
                return

            def norms(src, n):
                for t in range(T):
                    if t:
                        st.settle()
                    st.add(nc.scalar.activation(junk, src[:, t, :], ACT.Square, accum_out=rn[:, t:t + 1]))
                st.settle()
                nc.scalar.activation(rn, rn, ACT.Sqrt).then_inc(norm_asked, 1)

            root(rstd)
            transposed_copies()
            act.wait_ge(xn_ready, 3 * T)
            norms(N, 1)
            act.wait_ge(rn_ready, 1)
            for t in range(T):
                o = A.next()
                nc.scalar.activation(qkv[:, :, t, :], o[:, 0:3 * HD1].rearrange("p (s c) -> p s c", c=HD1), ACT.Identity,
                                     scale=rn[:, t:t + 1]).then_inc(pa_free, 1)
            exp(qkv[:, 1, :, :].rearrange("p t c -> p (t c)"))
            exp(memk)
            exp(qkv[:, 0, :, :].rearrange("p t c -> p (t c)"))
            for t in range(T):
                o = A.next()
                nc.scalar.copy(qT[:, t * P:(t + 1) * P], o[:, 0:P]).then_inc(pa_free, 1)
            act.wait_ge(pv_free, V_MIX1)
            norms(Y, 2)
            if level < 5:
                return

            def wide(dst, bias, chunks):
                for s in range(SLICES):
                    for c in range(chunks):
                        o = A.next()
                        nc.scalar.activation(dst[:, c, s * SL:(s + 1) * SL], o[:, 0:SL], ACT.Relu,
                                             bias=bias[:, c:c + 1]).then_inc(pa_free, 1)

            act.wait_ge(table_written[2], 16)
            act.wait_ge(at_ready, 5)
            wide(HT, b1a, HC)
            wide(AT, b1b, HC)
            for t in range(T):
                o = A.next()
                nc.scalar.copy(HN[:, t, :], o[:, :]).then_inc(pa_free, 1)
                act.wait_ge(pa_free, A.n)
                act.sem_inc(table_sbuf[3], 1)
            act.wait_ge(table_written[3], 16)
            wide(HT, b2a, HC)
            if level < 6:
                return

            root(rstd)
            transposed_copies()
            wide(VB[:, :].rearrange("p (c n) -> p c n", c=1), rb1, 1)
            exp(route[0].rearrange("p t e -> p (t e)"))
            exp(rcol[0])
            for q in range(0, T, 4):
                n = (min(q + 4, T) - q) * P
                o = A.next()
                nc.scalar.copy(wT[:, q * P:q * P + n], o[0:E1, 0:n]).then_inc(pa_free, 1)
            for e in range(E1):
                wide(h1, eb1[:, 2 * e:2 * e + 2], KC)
                wide(h2, eb2[:, 2 * e:2 * e + 2], KC)

        @block.vector
        def _(dve):
            st = Steps(dve, dve_step)
            V = Bank(dve, TV, pv_full, False)

            dve.wait_ge(edges_loaded, 48)
            dve.wait_ge(dst_loaded, 16)
            dve.wait_ge(pool_step, 7)
            low, high = sc[0:ROUNDS, 80:81], sc[0:ROUNDS, 81:82]
            dstf = AS[0:ROUNDS, U * P:2 * U * P]
            st.add(nc.vector.tensor_copy(rel[:, :], rel[:, :].bitcast(I32)))
            st.do(nc.vector.tensor_copy(dstf, AS[0:ROUNDS, 0:U * P].bitcast(I32)))
            st.add(nc.vector.tensor_reduce(low, dstf, AX, ALU.min))
            st.do(nc.vector.tensor_reduce(high, dstf, AX, ALU.max))
            nc.vector.tensor_scalar(sc[0:ROUNDS, 0:ROUNDS], ident[0:ROUNDS, 0:ROUNDS], low, None, ALU.mult).then_inc(diag_ready, 1)
            nc.vector.tensor_tensor(sc[0:ROUNDS, 82:83], high, low, ALU.subtract).then_inc(diag_ready, 1)
            dve.wait_ge(range_mm, 1)
            rel_r = rel[:, :].rearrange("p (r k) -> p r k", k=U)
            st.add(nc.vector.tensor_tensor(rel_r, rel_r, PACC[:, 0:ROUNDS].unsqueeze(2).to_broadcast([P, ROUNDS, U]), ALU.subtract))
            st.do(nc.vector.tensor_copy(first_base[:, :], PACC[0:1, 0:ROUNDS]))
            nc.vector.tensor_copy(base_i[:, :], first_base[:, :]).then_inc(ranges_ready, 1)
            o = V.next()
            nc.vector.tensor_reduce(sc[0:1, 83:84], o[0:1, 0:ROUNDS], AX, ALU.max).then_inc(pv_free, 1)
            st.add(nc.vector.tensor_scalar(sc[0:1, 96:96 + T - 1], iota_w[0:1, 1:T], float(P), None, ALU.mult))
            dve.wait_ge(pv_free, V.n)
            st.settle()
            st.do(nc.vector.tensor_scalar(sc[0:1, 128:128 + T - 1], sc[0:1, 96:96 + T - 1], sc[0:1, 83:84], None, ALU.is_le))
            st.do(nc.vector.tensor_reduce(sc[0:1, 84:85], sc[0:1, 128:128 + T - 1], AX, ALU.add))
            nc.vector.tensor_scalar(passes_i[:, :], sc[0:1, 84:85], 1.0, None, ALU.add).then_inc(ranges_ready, 1)
            dve.wait_ge(ranges_ready, 2)

            roots = [0]

            def one_over_root(v):
                roots[0] += 1
                dve.wait_ge(answered, roots[0])
                st.do(nc.vector.reciprocal(v, v))

            def statistics(src):
                for t in range(T):
                    st.add(nc.vector.bn_stats(stats[:, t, :], src[:, t, :]))
                st.settle()
                for t in range(T):
                    st.add(nc.vector.bn_aggr(mv[:, t, :], stats[:, t, :]))
                st.settle()
                nc.vector.tensor_scalar(rstd, mv[:, :, 1], LN_EPS, None, ALU.add).then_inc(asked, 1)
                one_over_root(rstd)

            def normalise():
                statistics(X)
                for t in range(T):
                    nc.vector.tensor_scalar(N[:, t, :], X[:, t, :], mv[:, t, 0:1], rstd[:, t:t + 1],
                                            ALU.subtract, ALU.mult).then_inc(xn_ready, 1)

            dve.wait_ge(wa_loaded[0], 64)
            heads = WA[:, 0:2048].rearrange("p (g d) -> p g d", d=DH0)
            st.do(nc.vector.tensor_reduce(sc[:, 256:256 + 32], heads, AX, ALU.add))
            st.do(nc.vector.tensor_scalar(sc[:, 256:256 + 32], sc[:, 256:256 + 32], 1.0 / DH0, None, ALU.mult))
            nc.vector.tensor_tensor(heads, heads, sc[:, 256:256 + 32].unsqueeze(2).to_broadcast([P, 32, DH0]),
                                    ALU.subtract).then_inc(wkv_centred, 1)
            dve.wait_ge(x_loaded, 32)
            normalise()

            def degrees():
                st.do(nc.vector.memset(VB[:, :], 1.0))
                add_pass(dve, st, 0)
                deg = AS[:, 0:WIDE]
                st.do(nc.vector.tensor_scalar(deg, VB[:, :], 0.0, None, ALU.is_gt))
                nc.vector.tensor_scalar(VB[:, :], VB[:, :], 1e-12, None, ALU.max).then_inc(asked, 1)
                one_over_root(VB[:, :])
                st.do(nc.vector.tensor_tensor(VB[:, :], VB[:, :], deg, ALU.mult))

            if level < 1:
                degrees()
                if stop == "deg":
                    for t in range(T):
                        st.add(nc.vector.tensor_copy(X[:, t, :], AS[:, 0:256] if 0 else VB[:, t * P:t * P + 1].to_broadcast([P, 256])))
                else:
                    dve.wait_ge(xn_ready, T)
                    st.add(nc.vector.tensor_copy(X[:, :, :], N[:, :, :]))
                st.settle()
                dve.sem_inc(stored_ready, 1)
                return
            bdz = bdT
            for t in range(T):
                b = t % 2
                dve.wait_ge(kv_ready, 2 * t + 2)
                dve.wait_ge(pa_free, T + 2 * t + 2)
                ss = sc[:, 256 + 32 * b:256 + 32 * b + 16]
                st.do(nc.vector.tensor_reduce(ss, kvsq[:, b, :].rearrange("p (g d) -> p g d", d=DH0), AX, ALU.add))
                nc.vector.tensor_scalar(ss, ss, 1.0 / DH0, LN_EPS, ALU.mult, ALU.add).then_inc(asked, 1)
                one_over_root(ss)
                r = sc[:, 320 + 8 * b:328 + 8 * b]
                st.do(nc.vector.tensor_tensor(r, ss[:, 0:8], ss[:, 8:16], ALU.mult))
                vh = kv[:, b, 512:1024].rearrange("p (g d) -> p g d", d=DH0)
                nc.vector.tensor_tensor(vh, vh, r.unsqueeze(2).to_broadcast([P, H0, DH0]), ALU.mult).then_inc(kv_normed, 1)
            st.do(nc.vector.memset(bdT, 0.0))
            dve.wait_ge(kv_used, T)
            for half in range(2):
                s = slice(half * DH0, (half + 1) * DH0)
                st.add(nc.vector.tensor_copy(bdT[s, :, s], PACC[s, :].rearrange("p (j d) -> p j d", d=P)[:, :, s]))
            st.settle()
            dve.sem_inc(mix_sb, 1)
            dve.wait_ge(mix_sb, 6)
            degrees()
            dve.wait_ge(bias_loaded, 32)
            st.do(nc.vector.tensor_tensor(bias_b[:, :], bias_b[:, :], mixb_b, ALU.add))
            if level < 2:
                for c in range(2):
                    st.add(nc.vector.tensor_copy(X[:, c, :], mixM[:, c, :]))
                st.settle()
                dve.sem_inc(stored_ready, 1)
                return

            st.do(nc.vector.memset(AS[:, :], 0.0))
            dve.wait_ge(nt_ready, T)
            dinv = VB[:, 0:NP]
            for c in range(KC):
                st.add(nc.vector.tensor_tensor(AT[:, c, 0:NP], NT[:, c, :], dinv, ALU.mult))
            st.settle()
            dve.sem_inc(at_ready, 1)
            for h in (1, 2):
                dve.wait_ge(table_sbuf[h - 1], T)
                add_pass(dve, st, h)
                for c in range(KC):
                    st.add(nc.vector.scalar_tensor_tensor(out=AT[:, c, 0:NP], in0=AT[:, c, 0:NP], scalar=0.5, in1=dinv,
                                                          op0=ALU.mult, op1=ALU.mult))
                st.settle()
                for c in range(KC):
                    st.add(nc.vector.scalar_tensor_tensor(out=AT[:, c, 0:NP], in0=NT[:, c, :], scalar=0.5, in1=AT[:, c, 0:NP],
                                                          op0=ALU.mult, op1=ALU.add))
                st.settle()
                for c in range(KC):
                    if h == 1:
                        st.add(nc.vector.tensor_tensor(AT[:, c, 0:NP], AT[:, c, 0:NP], dinv, ALU.mult))
                    else:
                        st.add(nc.vector.tensor_scalar(AT[:, c, 0:NP], AT[:, c, 0:NP], 0.0, None, ALU.max))
                st.settle()
                dve.sem_inc(at_ready, 1)
            for t in range(T):
                st.add(nc.vector.tensor_tensor(X[:, t, :], X[:, t, :], bias_b[:, :], ALU.add))
            st.settle()
            def accumulate(dst):
                for t in range(T):
                    o = V.next()
                    nc.vector.tensor_tensor(dst[:, t, :], dst[:, t, :], o[:, 0:D], ALU.add).then_inc(pv_free, 1)
                dve.wait_ge(pv_free, V.n)

            def softmax(v, part, stat):
                wide_stat = stat.unsqueeze(2).to_broadcast(list(part.shape))
                st.do(nc.vector.tensor_reduce(stat, part, AX, ALU.max))
                nc.vector.tensor_tensor(part, part, wide_stat, ALU.subtract).then_inc(asked, 1)
                answer()
                st.do(nc.vector.tensor_reduce(stat, part, AX, ALU.add))
                st.do(nc.vector.reciprocal(stat, stat))
                st.do(nc.vector.tensor_tensor(part, part, wide_stat, ALU.mult))

            def answer():
                roots[0] += 1
                dve.wait_ge(answered, roots[0])

            accumulate(X)
            if level < 3:
                dve.sem_inc(stored_ready, 1)
                return

            normalise()
            dve.wait_ge(route_mm, 1)
            for c in range(KC):
                st.add(nc.vector.tensor_scalar(ybar[:, c, :], PACC[:, c:c + 1].to_broadcast([P, P]), 1.0 / NODES, None, ALU.mult))
            st.settle()
            dve.sem_inc(route_sb, 1)
            dve.wait_ge(route_mm, 2)
            dve.wait_ge(cols_loaded, 16)
            rw = sc[:, 0:8]
            rw3, stat = rw.unsqueeze(1), sc[:, 8:9]
            st.do(nc.vector.tensor_tensor(rw, PACC[:, 8:16], br, ALU.add))
            softmax(rw, rw3, stat)
            st.do(nc.vector.tensor_scalar(sc[:, 16:24], rw, float(NODES), None, ALU.mult))
            st.do(nc.vector.reciprocal(sc[:, 16:24], sc[:, 16:24]))
            st.do(nc.vector.tensor_scalar(sc[:, 16:24], sc[:, 16:24], CAPACITY, 1.0, ALU.mult, ALU.min))
            st.do(nc.vector.tensor_tensor(rw, rw, sc[:, 16:24], ALU.mult))
            softmax(rw, rw3, stat)
            st.do(nc.vector.max(sc[:, 24:32], rw))
            st.do(nc.vector.max_index(sc[:, 32:40].bitcast(U32), sc[:, 24:32], rw))
            nc.vector.tensor_tensor(sc[:, 40:41], sc[:, 25:26], sc[:, 24:25], ALU.subtract).then_inc(asked, 1)
            st.do(nc.vector.tensor_copy(sc[:, 48:50], sc[:, 32:34].bitcast(U32)))
            for e in range(2):
                chosen = sc[:, 48 + e:49 + e]
                for i, (first, n, rows_each) in enumerate(((0, KC, D), (2, HC, HID), (6, 1, P))):
                    k = sc[:, 56 + 4 * e + i:57 + 4 * e + i]
                    st.do(nc.vector.tensor_scalar(k, chosen, float(rows_each), None, ALU.mult))
                    st.add(nc.vector.tensor_scalar(gidx[:, 8 * e + first:8 * e + first + n], iota4[:, 0:n], k, None, ALU.add))
                st.add(nc.vector.tensor_copy(gidx[:, 8 * e + 7:8 * e + 8], chosen))
            st.settle()
            dve.sem_inc(idx0_ready, 1)
            answer()
            st.do(nc.vector.tensor_scalar(sc[:, 41:42], sc[:, 40:41], 1.0, None, ALU.add))
            st.do(nc.vector.reciprocal(sc[:, 41:42], sc[:, 41:42]))
            st.do(nc.vector.tensor_tensor(sc[:, 42:43], sc[:, 40:41], sc[:, 41:42], ALU.mult))
            dve.wait_ge(experts_gathered, 256)
            for e in range(2):
                st.add(nc.vector.tensor_scalar(WA[:, 2048 + 1024 * e:3072 + 1024 * e], WA[:, 2048 + 1024 * e:3072 + 1024 * e],
                                               sc[:, 41 + e:42 + e], None, ALU.mult))
                st.add(nc.vector.tensor_scalar(b2g[:, e, :], b2g[:, e, :], sc[:, 41 + e:42 + e], None, ALU.mult))
            st.settle()
            dve.sem_inc(w2_scaled, 1)
            st.do(nc.vector.tensor_tensor(b2c, b2g[:, 0, :], b2g[:, 1, :], ALU.add))
            nodes_wide = [P, T, D]
            dve.wait_ge(nt_ready, 2 * T)
            st.do(nc.vector.tensor_tensor(N, N, b2c.unsqueeze(1).to_broadcast(nodes_wide), ALU.add))
            accumulate(N)
            statistics(N)
            for t in range(T):
                st.add(nc.vector.tensor_scalar(N[:, t, :], N[:, t, :], mv[:, t, 0:1], rstd[:, t:t + 1], ALU.subtract, ALU.mult))
            st.settle()
            dve.wait_ge(b2_loaded, 32)
            st.do(nc.vector.tensor_tensor(N, N, gamma_b.unsqueeze(1).to_broadcast(nodes_wide), ALU.mult))
            st.do(nc.vector.tensor_tensor(N, N, beta_b.unsqueeze(1).to_broadcast(nodes_wide), ALU.add))
            st.do(nc.vector.tensor_tensor(X[:, :, :], X[:, :, :], N, ALU.add))
            if level < 4:
                dve.sem_inc(stored_ready, 1)
                return

            normalise()
            dve.wait_ge(wb_loaded, 160)
            st.add(nc.vector.tensor_scalar(gpre, gpre, float(D) ** 0.5, None, ALU.mult))
            st.do(nc.vector.tensor_scalar(gout_b, gout_b, float(D) ** 0.5, None, ALU.mult))
            for c in range(KC):
                st.add(nc.vector.tensor_scalar(wqkv[:, c, :], wqkv[:, c, :], gpre[:, c:c + 1], None, ALU.mult))
            st.settle()
            dve.sem_inc(mix_sb, 1)

            def over_norm(n):
                dve.wait_ge(norm_asked, n)
                st.do(nc.vector.tensor_scalar(rn, rn, 1e-12, None, ALU.max))
                nc.vector.reciprocal(rn, rn).then_inc(rn_ready, 1)
                dve.wait_ge(rn_ready, n)

            over_norm(1)
            dve.wait_ge(pa_free, A_QKV)
            st.do(nc.vector.tensor_reduce(kmax, qkv[:, 1, 0:T - 1, :].rearrange("p t c -> p c t"), AX, ALU.max))
            nc.vector.tensor_tensor(kmax[0:LAST, :], kmax[0:LAST, :], qkv[0:LAST, 1, T - 1, :], ALU.max).then_inc(qk_ready, 1)
            o = V.next()
            st.add(nc.vector.tensor_reduce(sc[:, 1:2], memkT, AX, ALU.max))
            nc.vector.tensor_reduce(sc[:, 0:1], o[:, 0:P], AX, ALU.max).then_inc(pv_free, 1)
            dve.wait_ge(pv_free, V.n)
            st.settle()
            st.do(nc.vector.tensor_tensor(sc[:, 0:1], sc[:, 0:1], sc[:, 1:2], ALU.max))
            nc.vector.tensor_scalar(diag1, ident[:, :], sc[:, 0:1], None, ALU.mult).then_inc(qk_ready, 1)
            o = V.next()
            k3 = qkv[:, 1, :, :]
            nc.vector.tensor_tensor(k3, k3, o[:, 0:P].unsqueeze(1).to_broadcast([P, T, P]), ALU.subtract).then_inc(asked, 1)
            dve.wait_ge(asked, roots[0] + 1)
            nc.vector.tensor_tensor(memk, memk, o[0:MEM, 0:P], ALU.subtract).then_inc(asked, 1)
            dve.wait_ge(asked, roots[0] + 2)
            dve.sem_inc(pv_free, 1)
            q3 = qkv[:, 0, :, :].rearrange("p t (h d) -> p (t h) d", d=DH1)
            qs = qstat.unsqueeze(2).to_broadcast([P, T * H1, DH1])
            st.do(nc.vector.tensor_reduce(qstat, q3, AX, ALU.max))
            nc.vector.tensor_tensor(q3, q3, qs, ALU.subtract).then_inc(asked, 1)
            answer()
            answer()
            answer()
            st.do(nc.vector.tensor_reduce(qstat, q3, AX, ALU.add))
            st.do(nc.vector.reciprocal(qstat, qstat))
            nc.vector.tensor_tensor(q3, q3, qs, ALU.mult).then_inc(qk_ready, 1)
            dve.wait_ge(qk_ready, 3)
            dve.sem_inc(qk_ready, 1)
            st.do(nc.vector.memset(ctx_bd, 0.0))
            dve.wait_ge(mix_mm, 1)
            for h in range(H1):
                s = slice(h * DH1, (h + 1) * DH1)
                st.add(nc.vector.tensor_copy(ctx_bd[s, s], PACC[s, s]))
            st.do(nc.vector.reciprocal(sc[:, 2:3], PACC[:, P:P + 1]))
            st.do(nc.vector.tensor_scalar(sc[:, 2:3], sc[:, 2:3], float(DH1) ** -0.5, None, ALU.mult))
            dve.sem_inc(qk_ready, 1)
            o = V.next()
            nc.vector.tensor_scalar(m2, o[:, 0:D], sc[:, 2:3], None, ALU.mult).then_inc(pv_free, 1)
            dve.wait_ge(pv_free, V.n)
            dve.sem_inc(qk_ready, 1)
            for t in range(T):
                o = V.next()
                nc.vector.tensor_tensor(Y[:, t, :], o[:, 0:D], bout_b, ALU.add).then_inc(pv_free, 1)
            over_norm(2)
            for t in range(T):
                st.add(nc.vector.tensor_scalar(Y[:, t, :], Y[:, t, :], rn[:, t:t + 1], None, ALU.mult))
            st.settle()
            st.do(nc.vector.tensor_tensor(Y, Y, gout_b.unsqueeze(1).to_broadcast(nodes_wide), ALU.mult))
            st.do(nc.vector.tensor_tensor(X[:, :, :], X[:, :, :], N, ALU.add))
            st.do(nc.vector.tensor_tensor(X[:, :, :], X[:, :, :], Y, ALU.add))
            if level < 5:
                dve.sem_inc(stored_ready, 1)
                return

            st.add(nc.vector.memset(wgt[:, 0:C - 1], 1.0))
            st.add(nc.vector.tensor_scalar(wgt[:, C - 1:C], iota_p, float(EDGES - (C - 1) * P), None, ALU.is_lt))
            st.add(nc.vector.memset(AS[:, :], 0.0))
            st.do(nc.vector.tensor_scalar(eps_c, eps_in, 1.0, None, ALU.add))
            for c in range(KC):
                st.add(nc.vector.tensor_scalar(AT[:, c, 0:NP], NT[:, c, :], eps_c[:, 0:1], None, ALU.mult))
            st.settle()
            dve.sem_inc(at_ready, 1)
            add_pass(dve, st, 3)
            dve.sem_inc(at_ready, 1)
            dve.wait_ge(table_sbuf[3], T)
            for c in range(HC):
                st.add(nc.vector.tensor_scalar(AT[:, c, 0:NP], AT[:, c, 0:NP], eps_c[:, 1:2], None, ALU.mult))
            st.settle()
            dve.sem_inc(at_ready, 1)
            add_pass(dve, st, 4)
            dve.sem_inc(at_ready, 1)
            st.do(nc.vector.tensor_tensor(X[:, :, :], X[:, :, :], b2b_b.unsqueeze(1).to_broadcast(nodes_wide), ALU.add))
            accumulate(X)
            if level < 6:
                dve.sem_inc(stored_ready, 1)
                return

            normalise()
            dve.wait_ge(route_mm, 3)
            p, hit, rest, one, two, dense = route
            groups = [P, T, E1]
            c0, c1, c2, c3, c4 = rcol[0:5]

            def each(col):
                return col.unsqueeze(2).to_broadcast(groups)

            st.do(nc.vector.tensor_tensor(p, PACC[:, 0:T * E1].rearrange("p (t e) -> p t e", e=E1),
                                          rb2.unsqueeze(1).to_broadcast(groups), ALU.add))
            softmax(p, p, c0)
            index = iota6.unsqueeze(1).to_broadcast(groups)

            def first_hit(prob, best, mask):
                st.do(nc.vector.tensor_reduce(best, prob, AX, ALU.max))
                st.do(nc.vector.tensor_tensor(hit, prob, each(best), ALU.is_lt))
                st.do(nc.vector.tensor_scalar(hit, hit, 99.0, None, ALU.mult))
                st.do(nc.vector.tensor_tensor(hit, hit, index, ALU.add))
                st.do(nc.vector.tensor_reduce(c4, hit, AX, ALU.min))
                st.do(nc.vector.tensor_tensor(mask, hit, each(c4), ALU.is_equal))

            first_hit(p, c1, one)
            st.do(nc.vector.tensor_scalar(rest, one, -2.0, None, ALU.mult))
            st.do(nc.vector.tensor_tensor(rest, rest, p, ALU.add))
            first_hit(rest, c2, two)
            nc.vector.tensor_tensor(c0, c2, c1, ALU.subtract).then_inc(asked, 1)
            answer()
            st.do(nc.vector.tensor_scalar(c1, c0, 1.0, None, ALU.add))
            st.do(nc.vector.reciprocal(c1, c1))
            st.do(nc.vector.tensor_tensor(c2, c0, c1, ALU.mult))
            st.do(nc.vector.tensor_tensor(one, one, each(c1), ALU.mult))
            st.do(nc.vector.tensor_tensor(two, two, each(c2), ALU.mult))
            st.do(nc.vector.tensor_tensor(dense, one, two, ALU.add))
            dve.sem_inc(route_sb, 1)
            accumulate(X)
            for e in range(E1):
                for t in range(T):
                    o = V.next()
                    nc.vector.scalar_tensor_tensor(out=X[:, t, :], in0=o[:, 0:D], scalar=dense[:, t, e:e + 1], in1=X[:, t, :],
                                                   op0=ALU.mult, op1=ALU.add).then_inc(pv_free, 1)
            dve.wait_ge(pv_free, V.n)
            dve.sem_inc(stored_ready, 1)


STOP = None


def kernel(**inputs):
    import numpy as np
    import concourse.bacc as bacc
    from concourse.bass_utils import run_bass_kernel_spmd

    def by_partition(m):
        m = np.asarray(m)
        return np.ascontiguousarray(m.reshape(-1, P, m.shape[1]).transpose(1, 0, 2).reshape(P, -1))

    def columns(v):
        return np.asarray(v).reshape(-1, P).T

    def rows_of(v):
        return np.broadcast_to(np.asarray(v).reshape(1, -1), (P, np.asarray(v).size))

    g = {k: np.asarray(v) for k, v in inputs.items()}
    mem = g["L1_mix_mem_kv"]
    pad = C * P - EDGES
    src = np.pad(g["src"], (0, pad)).astype(np.int32)
    dst = np.pad(g["dst"], (0, pad), mode="edge").astype(np.int32)
    ew = np.pad(g["edge_weight"], (0, pad))
    arrays = {
        "x": g["x"],
        "src_pc": src.reshape(C, P).T, "dst_pc": dst.reshape(C, P).T, "wgt_pc": ew.reshape(C, P).T,
        "dst_rounds": dst.reshape(ROUNDS, U * P),
        "wkvT": by_partition(g["L0_mix_w_qkv"][512:].T), "wq": by_partition(g["L0_mix_w_qkv"][:512]),
        "woT": by_partition(g["L0_mix_w_out"].T), "wgT": by_partition(g["L0_gnn_W"].T),
        "L0_gnn_b": g["L0_gnn_b"], "L0_mix_b_out": g["L0_mix_b_out"],
        "L0_ffn_gamma": g["L0_ffn_gamma"], "L0_ffn_beta": g["L0_ffn_beta"],
        "w1_rows": g["L0_ffn_W1"].reshape(E0 * D, HID), "w2_rows": g["L0_ffn_W2"].reshape(E0 * HID, D),
        "b1_rows": g["L0_ffn_b1"].reshape(E0, HC, P).transpose(0, 2, 1).reshape(E0 * P, HC), "b2_rows": g["L0_ffn_b2"],
        "cols": np.concatenate([
            mem[0].reshape(HD1, MEM), columns(g["L1_mix_g_pre"]), columns(g["L1_gnn_b1a"]), columns(g["L1_gnn_b1b"]),
            columns(g["L1_gnn_b2a"]), columns(g["L1_ffn_expert_b1"]), columns(g["L1_ffn_expert_b2"]),
            columns(g["L1_ffn_router_b1"]), rows_of(g["L1_ffn_router_b2"]), by_partition(g["L0_ffn_Wr"]),
            rows_of(g["L0_ffn_br"]), rows_of(g["L1_gnn_eps1"]), rows_of(g["L1_gnn_eps2"])], axis=1),
        "wqkv1": by_partition(g["L1_mix_w_qkv"]), "L1_mix_w_out": g["L1_mix_w_out"],
        "memk": mem[0].reshape(HD1, MEM).T, "memv": mem[1].reshape(HD1, MEM).T,
        "rw1": by_partition(g["L1_ffn_router_w1"]), "L1_ffn_router_w2": g["L1_ffn_router_w2"],
        "L1_ffn_expert_b3": g["L1_ffn_expert_b3"], "L1_mix_g_out": g["L1_mix_g_out"], "L1_mix_b_out": g["L1_mix_b_out"],
        "L1_gnn_b2b": g["L1_gnn_b2b"],
        "w1a": by_partition(g["L1_gnn_W1a"]), "w1b": by_partition(g["L1_gnn_W1b"]),
        "w2a": by_partition(g["L1_gnn_W2a"]), "w2b": by_partition(g["L1_gnn_W2b"]),
        "experts1": np.stack([np.concatenate([by_partition(g[f"L1_ffn_expert_w{i}"][e]) for i in (1, 2, 3)], axis=1)
                              for e in range(E1)]),
    }
    nc = bacc.Bacc("TRN2", target_bir_lowering=False, num_devices=1)
    arrays = {"in_" + k: np.ascontiguousarray(v) for k, v in arrays.items()}
    args = {k[3:]: nc.dram_tensor(k, v.shape, mybir.dt.from_np(v.dtype), kind="ExternalInput").ap()
            for k, v in arrays.items()}
    out = nc.dram_tensor("out_0", (NODES, D), F32, kind="ExternalOutput").ap()
    build(nc, args, out, STOP)
    r = run_bass_kernel_spmd(nc, [arrays], core_ids=[0])
    return r.results[0]["out_0"]
```

```python
from contextlib import ExitStack

import concourse.bass as bass
from concourse import mybir

F32 = mybir.dt.float32
F16 = mybir.dt.float16
BF16 = mybir.dt.bfloat16
I32 = mybir.dt.int32
U32 = mybir.dt.uint32
ALU = mybir.AluOpType
ACT = mybir.ActivationFunctionType
AX = mybir.AxisListType.X

P = 128
NODES, D = 3125, 256
EDGES = 53125
T = -(-NODES // P)
LAST = NODES - (T - 1) * P
NP = T * P
WIDE = NP + P
U = 8
C = -(-EDGES // (P * U)) * U
ROUNDS = C // U
KC = D // P
HID = 512
HC = HID // P
SL = 400
SLICES = NP // SL
PARTS = 4
LN_EPS = 1e-5
H0, DH0 = 8, 64
E0, CAP_FACTOR = 8, 1.25
CAPACITY = float(-int(-(NODES * CAP_FACTOR) // E0))
GROUP = 5
HALF = GROUP * P // 2
H1, DH1, MEM = 4, 32, 4
HD1 = H1 * DH1
E1 = 6


class Bank:

    def __init__(self, eng, banks, wait_on, writer):
        self.eng, self.banks, self.wait_on, self.writer, self.n = eng, banks, wait_on, writer, 0

    def next(self):
        need = self.n + 1 - (len(self.banks) if self.writer else 0)
        if need > 0:
            self.eng.wait_ge(self.wait_on, need)
        bank = self.banks[self.n % len(self.banks)]
        self.n += 1
        return bank


class Steps:

    def __init__(self, eng, sem):
        self.eng, self.sem, self.n = eng, sem, 0

    def add(self, ins):
        ins.then_inc(self.sem, 1)
        self.n += 1

    def settle(self):
        self.eng.wait_ge(self.sem, self.n)

    def do(self, ins):
        self.add(ins)
        self.settle()


def build(nc, a, out, stop=None):
    with ExitStack() as ctx:
        def sb(name, shape, dt=F32):
            return ctx.enter_context(nc.sbuf_tensor(name, shape, dt))

        def sem(name):
            return ctx.enter_context(nc.semaphore(name))

        X = sb("X", [P, T, D])
        NN = sb("NN", [P, 2 * T * D])
        N = NN[:, 0:T * D].rearrange("p (t d) -> p t d", d=D)
        NT = NN[:, T * D:2 * T * D].rearrange("p (c n) -> p c n", n=NP)
        HT = NN[:, :].rearrange("p (c n) -> p c n", n=NP)
        HN = NN[:, :].rearrange("p (t d) -> p t d", d=HID)
        AS = sb("AS", [P, HC * WIDE])
        AT = AS[:, :].rearrange("p (c n) -> p c n", n=WIDE)
        rows = sb("rows", [P, U, HID])
        VB = sb("VB", [P, WIDE])
        WA = sb("WA", [P, 5120])
        WB = sb("WB", [P, 3072])
        onehot = sb("onehot", [P, U, P])
        src_i = sb("src_i", [P, C + U], I32)
        cur = sb("cur", [P, 2 * U], I32)
        rel = sb("rel", [P, C])
        wgt = sb("wgt", [P, C])
        base_i = sb("base_i", [1, ROUNDS], I32)
        first_base = sb("first_base", [1, ROUNDS], mybir.dt.uint16)
        passes_i = sb("passes_i", [1, 1], I32)
        ident = sb("ident", [P, P])
        ones = sb("ones", [P, P])
        iota_w = sb("iota_w", [P, P])
        small = sb("small", [P, 1024])
        bias_b = sb("bias_b", [P, D])

        ps = [ctx.enter_context(nc.psum_tensor(f"ps{i}", [P, 512], F32)) for i in range(8)]
        TA, EDGE, TV, PACC = ps[0:3], ps[3:5], ps[5:7], ps[7]

        stats = small[:, 0:150].rearrange("p (t s) -> p t s", s=6)
        mv = small[:, 150:200].rearrange("p (t s) -> p t s", s=2)
        rstd = small[:, 200:225]
        valid = small[:, 225:250]
        iota_p = small[:, 250:251]
        sc = small[:, 256:640]
        eps_c = small[:, 251:253]
        cols = small[:, 640:1024]

        table = [nc.dram_tensor(f"table{i}", (NP, HID if i == 3 else D), F32, kind="Internal").ap()
                 for i in range(4)]

        degree_row = [nc.dram_tensor(f"degree_row{i}", (3, NP), F32, kind="Internal").ap() for i in range(2)]

        pa_full, pa_free = sem("pa_full"), sem("pa_free")
        pv_full, pv_free = sem("pv_full"), sem("pv_free")
        dve_step, act_step, pool_step = sem("dve_step"), sem("act_step"), sem("pool_step")
        x_zeroed, x_loaded = sem("x_zeroed"), sem("x_loaded")
        edges_loaded, dst_loaded = sem("edges_loaded"), sem("dst_loaded")
        consts_ready = sem("consts_ready")
        wa_loaded = [sem("wa0_loaded"), sem("wa1_loaded")]
        wb_loaded = sem("wb_loaded")
        ranges_ready, range_mm, diag_ready = sem("ranges_ready"), sem("range_mm"), sem("diag_ready")
        xn_ready, nt_ready = sem("xn_ready"), sem("nt_ready")
        edge_wait = sem("edge_wait")
        idx_ready = [sem(f"idx_ready{h}") for h in range(4)]
        gathered = [[sem(f"gathered{h}_{k}") for k in range(U)] for h in range(4)]
        onehot_ready = [sem(f"onehot_ready{h}") for h in range(5)]
        product_done = [sem(f"product_done{h}") for h in range(5)]
        added = [sem(f"added{h}") for h in range(5)]
        pass_ready = [sem(f"pass_ready{h}") for h in range(5)]
        table_sbuf = [sem(f"table_sbuf{h}") for h in range(4)]
        table_written = [sem(f"table_written{h}") for h in range(4)]
        at_ready = sem("at_ready")
        out_stored = sem("out_stored")
        stored_ready = sem("stored_ready")
        kv_ready, kv_normed, kv_used = sem("kv_ready"), sem("kv_normed"), sem("kv_used")
        wkv_centred = sem("wkv_centred")
        mix_mm, mix_sb = sem("mix_mm"), sem("mix_sb")
        layer_mm = sem("layer_mm")
        bias_loaded = sem("bias_loaded")
        route_mm, route_sb = sem("route_mm"), sem("route_sb")
        expert_loaded = sem("expert_loaded")
        w2_scaled, w2b_loaded = sem("w2_scaled"), sem("w2b_loaded")
        w2a_loaded, q_normed, q_in = sem("w2a_loaded"), sem("q_normed"), sem("q_in")
        rn_ready, norm_asked = sem("rn_ready"), sem("norm_asked")
        experts_loaded = [sem("experts0_loaded"), sem("experts1_loaded")]
        experts_gathered, idx0_ready = sem("experts_gathered"), sem("idx0_ready")
        cols_loaded, b2_loaded = sem("cols_loaded"), sem("b2_loaded")
        w1_loaded, w1_used = sem("w1_loaded"), sem("w1_used")
        qk_ready = sem("qk_ready")
        degree_ready, degree_moved = sem("degree_ready"), sem("degree_moved")
        asked, answered = sem("asked"), sem("answered")

        def load(eng, dst, src, s):
            eng.dma_start(dst, src).then_inc(s, 16)

        block = ctx.enter_context(nc.Block())
        DUMP = {"ln": 0, "deg": 0, "mix": 1, "gnn0": 2, "ffn0": 3, "mix1": 4, "gnn1": 5}
        level = DUMP.get(stop, 99)

        wkvT = WA[:, 0:2048].rearrange("p (c n) -> p c n", n=1024)
        wq = WA[:, 2048:3072].rearrange("p (j f) -> p j f", f=D)
        woT = WA[:, 3072:4096].rearrange("p (j f) -> p j f", f=D)
        wgT = WA[:, 4096:4608].rearrange("p (c f) -> p c f", f=D)
        mixM = WA[:, 4608:5120].rearrange("p (c f) -> p c f", f=D)
        w1g = WA[:, 0:2048].rearrange("p (e c f) -> p e c f", c=KC, f=HID)
        w2g = WA[:, 2048:4096].rearrange("p (e c f) -> p e c f", c=HC, f=D)
        hG = AS[:, 0:2 * 8 * GROUP * P].rearrange("p (b c n) -> p b c n", c=8, n=GROUP * P)
        rflat = rows[:, :, :].rearrange("p u d -> p (u d)")
        b2g = rflat[:, 0:512].rearrange("p (e f) -> p e f", f=D)
        gamma_b, beta_b, b2c = rflat[:, 512:768], rflat[:, 768:1024], rflat[:, 1024:1280]
        ybar = rflat[:, 1280:1536].rearrange("p (c m) -> p c m", m=P)
        w1a = WA[:, 0:1024].rearrange("p (c f) -> p c f", f=HID)
        w1b = WA[:, 1024:3072].rearrange("p (c f) -> p c f", f=HID)
        w2a = WA[:, 3072:5120].rearrange("p (c f) -> p c f", f=HID)
        w2b = WA[:, 0:1024].rearrange("p (c f) -> p c f", f=D)
        wqkv = WB[:, 0:768].rearrange("p (c f) -> p c f", f=3 * HD1)
        wout1 = WB[:, 768:1024]
        memk, memv = WB[0:MEM, 1024:1152], WB[0:MEM, 1152:1280]
        gout_b, bout_b, b2b_b = WB[:, 1280:1536], WB[:, 1536:1792], WB[:, 1792:2048]
        rw1 = WB[:, 2048:2304].rearrange("p (c f) -> p c f", f=P)
        rw2 = WB[:, 2304:2304 + E1]
        b3 = WB[0:E1, 2560:2816]
        mixb_b = WB[:, 2816:3072]
        kv1 = AS[:, 2 * WIDE:2 * WIDE + 2 * NP].rearrange("p (s t c) -> p s t c", s=2, c=HD1)
        Y = AS[:, 2 * WIDE:2 * WIDE + T * D].rearrange("p (t d) -> p t d", d=D)
        qT = VB[:, 0:NP]
        W3 = WA[:, 3072:5120]
        junk = W3[:, 0:256]
        kmax, diag1, ctx_bd = W3[:, 256:384], W3[:, 384:512], W3[:, 512:640]
        m2 = W3[:, 640:896]
        rn = W3[:, 896:896 + T]
        q1 = W3[:, 1024:1280].rearrange("p (b c) -> p b c", b=2)
        we = WA[:, 0:3072].rearrange("p (b l c f) -> p b l c f", b=2, l=3, f=D)
        h1 = AS[:, 0:KC * NP].rearrange("p (c n) -> p c n", n=NP)
        h2 = AS[:, KC * NP:2 * KC * NP].rearrange("p (c n) -> p c n", n=NP)
        wT = rflat[0:E1, 0:NP]
        route = [WA[:, 3072 + 150 * i:3222 + 150 * i].rearrange("p (t e) -> p t e", e=E1) for i in range(6)]
        rcol = [WA[:, 4000 + 32 * i:4000 + 32 * i + T] for i in range(8)]
        memkT, gpre = cols[:, 0:4], cols[:, 4:6]
        b1a, b1b, b2a = cols[:, 6:10], cols[:, 10:14], cols[:, 14:18]
        eb1, eb2 = cols[:, 18:30], cols[:, 30:42]
        rb1, rb2 = cols[:, 42:43], cols[:, 43:49]
        wr = cols[:, 49:65].rearrange("p (c e) -> p c e", e=E0)
        br = cols[:, 65:73]
        eps_in = cols[:, 73:75]
        b1g = cols[:, 80:88]
        gidx = cols[:, 96:112].bitcast(I32)
        iota4, iota6 = cols[:, 112:116], cols[:, 116:122]
        V_GNN0, V_FFN0 = 1 + T, 1 + 2 * T
        ROUND_OUT = T + 10
        assert ROUND_OUT + T // 2 + 3 < ROUNDS
        A_MIX1 = T + 2 * T + 4 + KC + 2 * T + T + GROUP * 16 + T

        def out_of_ring(t):
            return A_MIX1 + max(1, 2 * t)
        V_MIX1 = V_FFN0 + 3 + T
        V_GNN1 = V_MIX1 + T
        V_B3 = V_GNN1 + T
        A2 = AS[:, 2 * WIDE:4 * WIDE]
        onehot16 = onehot[:, :, :].rearrange("p u n -> p (u n)").bitcast(BF16).rearrange("p (b u n) -> p b u n", b=2, n=P)
        rel16, iota16 = A2[:, 0:C // 2].bitcast(F16), A2[:, 512:512 + P // 2].bitcast(F16)
        wflat = A2[:, 640:640 + (PARTS * C + P) // 2].bitcast(BF16)
        wparts = wflat[:, 0:PARTS * C].rearrange("p (c s) -> p c s", s=PARTS)
        wrest = A2[:, 2048:2048 + C]
        dnode = A2[:, 2560:2560 + 3 * T]
        kv = A2[:, 0:2048].rearrange("p (b n) -> p b n", n=1024)
        kvsq = A2[:, 2048:4096].rearrange("p (b n) -> p b n", n=1024)
        pj = A2[:, 4096:5120].rearrange("p (j f) -> p j f", f=D)
        bdT = A2[:, 5120:5632].rearrange("p (j d) -> p j d", d=P)

        TABLE_DMAS = [1, 1, 1, 1]

        def hop_width(h):
            return HC if h == 4 else KC

        @block.sync
        def _(sp):
            load(sp, src_i[:, :], a["src_pc"], edges_loaded)
            load(sp, wgt[:, :], a["wgt_pc"], edges_loaded)
            load(sp, rel[:, :].bitcast(I32), a["dst_pc"], edges_loaded)
            load(sp, AS[0:ROUNDS, 0:U * P].bitcast(I32), a["dst_rounds"], dst_loaded)
            sp.wait_ge(x_zeroed, 1)
            load(sp, X[:, 0:T - 1, :], a["x"][0:(T - 1) * P, :].rearrange("(t p) d -> p t d", p=P), x_loaded)
            load(sp, X[0:LAST, T - 1, :], a["x"][(T - 1) * P:NODES, :], x_loaded)
            load(sp, WA[:, 0:2048], a["wkvT"], wa_loaded[0])
            load(sp, WA[:, 2048:3072], a["wq"], wa_loaded[0])
            load(sp, WA[:, 3072:4096], a["woT"], wa_loaded[0])
            load(sp, WA[:, 4096:4608], a["wgT"], wa_loaded[0])
            load(sp, bias_b[:, :], a["L0_gnn_b"].partition_broadcast(P), bias_loaded)
            load(sp, mixb_b, a["L0_mix_b_out"].partition_broadcast(P), bias_loaded)
            load(sp, cols[:, 0:75], a["cols"], cols_loaded)
            for dst, src in ((WB[:, 0:768], "wqkv1"), (wout1, "L1_mix_w_out"), (memk, "memk"), (memv, "memv"),
                             (WB[:, 2048:2304], "rw1"), (rw2, "L1_ffn_router_w2"), (b3, "L1_ffn_expert_b3")):
                load(sp, dst, a[src], wb_loaded)
            for dst, src in ((gout_b, "L1_mix_g_out"), (bout_b, "L1_mix_b_out"), (b2b_b, "L1_gnn_b2b")):
                load(sp, dst, a[src].partition_broadcast(P), wb_loaded)
            sp.wait_ge(degree_ready, 1)
            load(sp, degree_row[0], VB[0:3, 0:NP], degree_moved)
            sp.wait_ge(degree_moved, 16)
            for part in range(3):
                load(sp, dnode[:, part * T:(part + 1) * T], degree_row[0][part, :].rearrange("(p t) -> p t", t=T), degree_moved)
            sp.wait_ge(degree_ready, 2)
            load(sp, degree_row[1][0, :].rearrange("(p t) -> p t", t=T), dnode[:, 0:T], degree_moved)
            sp.wait_ge(degree_moved, 80)
            load(sp, VB[:, 0:NP], degree_row[1][0, :].partition_broadcast(P), degree_moved)
            if level >= 2:
                for h in range(2):
                    sp.wait_ge(table_sbuf[h], T)
                    load(sp, table[h].rearrange("(t p) d -> p t d", p=P), N, table_written[h])
            if level >= 3:
                sp.wait_ge(pv_full, V_GNN0)
                load(sp, gamma_b, a["L0_ffn_gamma"].partition_broadcast(P), b2_loaded)
                load(sp, beta_b, a["L0_ffn_beta"].partition_broadcast(P), b2_loaded)
            if level >= 4:
                sp.wait_ge(pv_full, V_FFN0)
                load(sp, WA[:, 0:1024], a["w1a"], w1_loaded)
                load(sp, WA[:, 1024:3072], a["w1b"], w1_loaded)
                sp.wait_ge(xn_ready, 3 * T)
                load(sp, table[2].rearrange("(t p) d -> p t d", p=P), N, table_written[2])
            if level >= 5:
                sp.wait_ge(at_ready, 5)
                load(sp, WA[:, 3072:5120], a["w2a"], w2a_loaded)
                sp.wait_ge(w1_used, 1)
                load(sp, WA[:, 0:1024], a["w2b"], w2b_loaded)
                sp.wait_ge(table_sbuf[3], T)
                load(sp, table[3].rearrange("(t p) d -> p t d", p=P), HN, table_written[3])
            if level >= 6:
                for e in range(E1):
                    sp.wait_ge(pv_full, V_GNN1 if e < 2 else V_B3 + T * (e - 1))
                    load(sp, WA[:, (e % 2) * 1536:(e % 2) * 1536 + 1536], a["experts1"][e], experts_loaded[e % 2])
            sp.wait_ge(stored_ready, 1)
            load(sp, out[0:(T - 1) * P, :].rearrange("(t p) d -> p t d", p=P), X[:, 0:T - 1, :], out_stored)
            load(sp, out[(T - 1) * P:NODES, :], X[0:LAST, T - 1, :], out_stored)
            sp.wait_ge(out_stored, 32)

        def gather_pass(pool, h):
            pool.wait_ge(table_written[h - 1], 16 * TABLE_DMAS[h - 1])
            pool.wait_ge(ranges_ready, 2)
            windows = pool.value_load(passes_i[0:1, 0:1], min_val=1, max_val=T)
            with pool.Fori(0, windows) as w:
                with pool.Fori(0, ROUNDS // 2) as i:
                    for j in range(2):
                        r = pool.snap(w * ROUNDS + i * 2 + j)
                        for half in range(2):
                            if half == 0:
                                pool.wait_ge(idx_ready[h - 1], r + 1)
                            pool.wait_ge(product_done[h], r * U + half * 4 + 4)
                            pool.sem_inc(edge_wait, 1)
                            for k in range(half * 4, half * 4 + 4):
                                nc.gpsimd.indirect_dma_start(
                                    rows[:, k, 0:hop_width(h) * P], None, table[h - 1][:, :],
                                    bass.IndirectOffsetOnAxis(cur[:, j * U + k:j * U + k + 1], 0)).then_inc(gathered[h - 1][k], 16)

        def product_pass(pe, h, side=None):
            def one_round(r, j):
                pe.wait_ge(added[h], r + 1)
                for k in range(U):
                    pe.wait_ge(onehot_ready[h], r * U + k + 1)
                    pe.wait_ge(gathered[h - 1][k], r * 16 + 16)
                    for c in range(hop_width(h)):
                        mm = nc.tensor.matmul(EDGE[j][:, c * P:(c + 1) * P], rows[:, k, c * P:(c + 1) * P], onehot[:, k, :],
                                              start=(k == 0 and c == 0), stop=(k == U - 1), skip_group_check=True)
                    mm.then_inc(product_done[h], 1)
                    if side and k % 4 == 3:
                        side.get((r, k // 4), lambda: None)()

            def window(w):
                with pe.Fori(0, ROUNDS // 2) as i:
                    for j in range(2):
                        one_round(pe.snap(w * ROUNDS + i * 2 + j), j)

            pe.sem_inc(product_done[h], U)
            pe.wait_ge(ranges_ready, 2)
            windows = pe.value_load(passes_i[0:1, 0:1], min_val=1, max_val=T)
            if side:
                for r in range(ROUNDS):
                    one_round(r, r % 2)
                side = None
                with pe.If(windows > 1):
                    with pe.Fori(1, windows) as w:
                        window(w)
            else:
                with pe.Fori(0, windows) as w:
                    window(w)

        def degree_products(pe):
            pe.sem_inc(product_done[0], 2)
            pe.wait_ge(ranges_ready, 2)
            windows = pe.value_load(passes_i[0:1, 0:1], min_val=1, max_val=T)
            with pe.Fori(0, windows) as w:
                with pe.Fori(0, ROUNDS // 2) as i:
                    for j in range(2):
                        r = pe.snap(w * ROUNDS + i * 2 + j)
                        pe.wait_ge(added[0], r + 1)
                        pe.wait_ge(onehot_ready[0], r + 1)
                        for k in range(U):
                            mm = nc.tensor.matmul(EDGE[j][:, 0:P], wflat[:, bass.ds((i * 2 * U + j * U + k) * PARTS, P)],
                                                  onehot16[:, j, k, :], start=(k == 0), stop=(k == U - 1))
                        mm.then_inc(product_done[0], 1)

        def degree_sums(dve, st):
            dve.sem_inc(added[0], 2)
            windows = dve.value_load(passes_i[0:1, 0:1], min_val=1, max_val=T)
            with dve.Fori(0, windows) as w:
                nc.vector.tensor_scalar(rel16, rel[:, :], iota_w[:, 0:1], None, ALU.subtract).then_inc(pass_ready[0], 1)
                dve.wait_ge(pass_ready[0], w * 3 + 1)
                dve.sem_inc(edge_wait, 1)
                with dve.Fori(0, ROUNDS // 2) as i:
                    for j in range(2):
                        r = dve.snap(w * ROUNDS + i * 2 + j)
                        dve.wait_ge(product_done[0], r + 1)
                        nc.vector.tensor_tensor(
                            onehot16[:, j, :, :], iota16.unsqueeze(1).to_broadcast([P, U, P]),
                            rel16[:, bass.ds(i * 2 * U + j * U, U)].unsqueeze(2).to_broadcast([P, U, P]),
                            ALU.is_equal).then_inc(onehot_ready[0], 1)
                        b = dve.value_load(base_i[0:1, bass.ds(i * 2 + j, 1)], min_val=0, max_val=NP)
                        dve.wait_ge(added[0], r + 2)
                        dve.wait_ge(product_done[0], r + 3)
                        win = VB[0:PARTS, bass.ds(b, P)]
                        nc.vector.tensor_tensor(win, win, EDGE[j][0:PARTS, 0:P], ALU.add).then_inc(added[0], 1)
                nc.vector.tensor_scalar(iota_w[:, :], iota_w[:, :], float(P), None, ALU.add).then_inc(pass_ready[0], 1)
                dve.wait_ge(pass_ready[0], w * 3 + 2)
                nc.vector.tensor_scalar(base_i[:, :], base_i[:, :], P, NP, ALU.add, ALU.min).then_inc(pass_ready[0], 1)
                dve.wait_ge(pass_ready[0], w * 3 + 3)
            dve.wait_ge(added[0], 2 + ROUNDS)

        def add_pass(dve, st, h, side=None):
            nch = hop_width(h)

            def one_round(r, row, j):
                for k in range(U):
                    c = row * U + k
                    dve.wait_ge(product_done[h], r * U + k + 1)
                    nc.vector.tensor_scalar(onehot[:, k, :], iota_w[:, :], rel[:, bass.ds(c, 1)], wgt[:, bass.ds(c, 1)],
                                            ALU.is_equal, ALU.mult).then_inc(onehot_ready[h], 1)
                nc.vector.tensor_copy(cur[:, (1 - j) * U:(2 - j) * U], src_i[:, bass.ds((row + 1) * U, U)]).then_inc(idx_ready[h - 1], 1)
                b = dve.value_load(base_i[0:1, bass.ds(row, 1)], min_val=0, max_val=NP)
                dve.wait_ge(added[h], r + 2)
                dve.wait_ge(product_done[h], r * U + 2 * U)
                win = AT[:, 0:nch, bass.ds(b, P)]
                nc.vector.tensor_tensor(win, win, EDGE[j][:, 0:nch * P].rearrange("p (c n) -> p c n", n=P),
                                        ALU.add).then_inc(added[h], 1)

            def window(w):
                with dve.Fori(0, ROUNDS // 2) as i:
                    for j in range(2):
                        one_round(dve.snap(w * ROUNDS + i * 2 + j), i * 2 + j, j)

            def next_window(w):
                dve.wait_ge(onehot_ready[h], w * C + C)
                dve.sem_inc(edge_wait, 1)
                nc.vector.tensor_scalar(iota_w[:, :], iota_w[:, :], float(P), None, ALU.add).then_inc(pass_ready[h], 1)
                dve.wait_ge(pass_ready[h], w * 2 + 1)
                nc.vector.tensor_scalar(base_i[:, :], base_i[:, :], P, NP, ALU.add, ALU.min).then_inc(pass_ready[h], 1)
                dve.wait_ge(pass_ready[h], w * 2 + 2)

            nc.vector.tensor_copy(cur[:, 0:U], src_i[:, 0:U]).then_inc(idx_ready[h - 1], 1)
            st.add(nc.vector.tensor_copy(base_i[:, :], first_base[:, :]))
            st.do(nc.vector.tensor_copy(sc[:, 26:27], iota_w[:, 0:1]))
            st.do(nc.vector.tensor_scalar(iota_w[:, :], iota_w[:, :], sc[:, 26:27], None, ALU.subtract))
            dve.sem_inc(added[h], 2)
            windows = dve.value_load(passes_i[0:1, 0:1], min_val=1, max_val=T)
            if side:
                for r in range(ROUNDS):
                    one_round(r, r, r % 2)
                    side.get(r, lambda: None)()
                next_window(0)
                with dve.If(windows > 1):
                    with dve.Fori(1, windows) as w:
                        window(w)
                        next_window(w)
            else:
                with dve.Fori(0, windows) as w:
                    window(w)
                    next_window(w)
            dve.wait_ge(added[h], 2 + ROUNDS)

        @block.gpsimd
        def _(pool):
            st = Steps(pool, pool_step)
            nc.gpsimd.memset(X[:, T - 1, :], 0.0).then_inc(x_zeroed, 1)
            st.add(nc.gpsimd.memset(ident[:, :], 1.0))
            st.add(nc.gpsimd.memset(ones[:, :], 1.0))
            st.do(nc.gpsimd.memset(valid, 1.0))
            st.add(nc.gpsimd.affine_select(out=ident[:, :], in_=ident[:, :], compare_op=ALU.is_equal, fill=0.0,
                                           base=0, pattern=[[-1, P]], channel_multiplier=1))
            st.add(nc.gpsimd.affine_select(out=valid, in_=valid, compare_op=ALU.is_ge, fill=0.0,
                                           base=NODES - 1, pattern=[[-P, T]], channel_multiplier=-1))
            st.add(nc.gpsimd.iota(iota_w[:, :], pattern=[[1, P]], base=0, channel_multiplier=0,
                                  allow_small_or_imprecise_dtypes=True))
            st.add(nc.gpsimd.iota(iota_p, pattern=[[0, 1]], base=0, channel_multiplier=1,
                                  allow_small_or_imprecise_dtypes=True))
            pool.wait_ge(cols_loaded, 16)
            st.add(nc.gpsimd.iota(iota4, pattern=[[P, 4]], base=0, channel_multiplier=1,
                                  allow_small_or_imprecise_dtypes=True))
            st.add(nc.gpsimd.iota(iota6, pattern=[[1, E1]], base=0, channel_multiplier=0,
                                  allow_small_or_imprecise_dtypes=True))
            st.settle()
            if level >= 2:
                gather_pass(pool, 1)
                gather_pass(pool, 2)
            if level >= 3:
                pool.wait_ge(idx0_ready, 1)
                pool.wait_ge(pv_full, V_GNN0)
                pool.sem_inc(edge_wait, 1)
                for e in range(2):
                    for c in range(KC):
                        nc.gpsimd.indirect_dma_start(w1g[:, e, c, :], None, a["w1_rows"][:, :], bass.IndirectOffsetOnAxis(
                            gidx[:, 8 * e + c:8 * e + c + 1], 0)).then_inc(experts_gathered, 16)
                    for c in range(HC):
                        nc.gpsimd.indirect_dma_start(w2g[:, e, c, :], None, a["w2_rows"][:, :], bass.IndirectOffsetOnAxis(
                            gidx[:, 8 * e + 2 + c:8 * e + 3 + c], 0)).then_inc(experts_gathered, 16)
                    nc.gpsimd.indirect_dma_start(b1g[:, 4 * e:4 * e + 4], None, a["b1_rows"][:, :], bass.IndirectOffsetOnAxis(
                        gidx[:, 8 * e + 6:8 * e + 7], 0)).then_inc(experts_gathered, 16)
                    nc.gpsimd.indirect_dma_start(b2g[:, e, :], None, a["b2_rows"][:, :], bass.IndirectOffsetOnAxis(
                        gidx[:, 8 * e + 7:8 * e + 8], 0)).then_inc(experts_gathered, 16)
            if level >= 5:
                gather_pass(pool, 3)
                gather_pass(pool, 4)

        def transposes(pe, bank, src, k):
            for t in range(T):
                o = bank.next()
                for c in range(k):
                    mm = nc.tensor.transpose(o[:, c * P:(c + 1) * P], src(t, c), ident[:, :])
                mm.then_inc(pa_full, 1)

        @block.tensor
        def _(pe):
            A = Bank(pe, TA, pa_free, True)
            V = Bank(pe, TV, pv_free, True)
            pe.wait_ge(pool_step, 7)
            pe.wait_ge(diag_ready, 1)
            nc.tensor.matmul(PACC[:, 0:ROUNDS], ones[0:ROUNDS, :], sc[0:ROUNDS, 0:ROUNDS],
                             start=True, stop=True).then_inc(range_mm, 1)
            pe.wait_ge(diag_ready, 2)
            nc.tensor.transpose(V.next()[0:1, 0:ROUNDS], sc[0:ROUNDS, 82:83], ident[0:ROUNDS, 0:ROUNDS]).then_inc(pv_full, 1)

            def normalised_transposed(first):
                for t in range(T):
                    pe.wait_ge(xn_ready, first * T + t + 1)
                    o = A.next()
                    for c in range(KC):
                        mm = nc.tensor.transpose(o[:, c * P:(c + 1) * P], N[:, t, c * P:(c + 1) * P], ident[:, :])
                    mm.then_inc(pa_full, 1)

            normalised_transposed(0)
            if level < 1:
                degree_products(pe)
                return
            degree_products(pe)

            def keys_and_values(t, half):
                o = A.next()
                for c in range(KC):
                    mm = nc.tensor.matmul(o[:, :], NT[:, c, t * P:(t + 1) * P], wkvT[:, c, half * 512:(half + 1) * 512],
                                          start=(c == 0), stop=(c == KC - 1))
                mm.then_inc(pa_full, 1)

            def head_products(t):
                pe.wait_ge(kv_normed, t + 1)
                for j in range(4):
                    mm = nc.tensor.matmul(PACC[:, j * P:(j + 1) * P], kv[:, t % 2, 512 + j * P:512 + (j + 1) * P],
                                          kv[:, t % 2, j * P:(j + 1) * P], start=(t == 0 and j == 0),
                                          stop=(t == T - 1), skip_group_check=True)
                mm.then_inc(kv_used, 1)

            beside_hop1 = {}
            for t in range(T):
                beside_hop1[2 * t, 0] = lambda t=t: keys_and_values(t, 0)
                beside_hop1[2 * t, 1] = lambda t=t: keys_and_values(t, 1)
                beside_hop1[2 * t + 3 if t < T - 1 else 2 * t + 2, 0 if t < T - 1 else 1] = lambda t=t: head_products(t)
            assert max(beside_hop1)[0] < ROUNDS

            def attention_matrix():
                pe.wait_ge(mix_sb, 1)
                for j in range(4):
                    o = A.next()
                    nc.tensor.matmul(o[:, 0:D], bdT[:, j, :], woT[:, j, :], start=True, stop=True).then_inc(pa_full, 1)
                pe.wait_ge(mix_sb, 5)
                for c in range(KC):
                    o = A.next()
                    for j in range(4):
                        mm = nc.tensor.matmul(o[:, 0:D], wq[:, j, c * P:(c + 1) * P], pj[:, j, :], start=(j == 0), stop=(j == 3))
                    mm.then_inc(pa_full, 1)

            if level < 2:
                return
            for h in (1, 2):
                pe.wait_ge(at_ready, h)
                transposes(pe, A, lambda t, c: AT[:, c, t * P:(t + 1) * P], KC)
                if h == 1:
                    pe.wait_ge(wkv_centred, 1)
                    product_pass(pe, h, beside_hop1)
                    attention_matrix()
                else:
                    product_pass(pe, h)
            pe.wait_ge(at_ready, 3)
            for t in range(T):
                o = V.next()
                for n, (lhs, rhs) in enumerate([(AT[:, c, t * P:(t + 1) * P], wgT[:, c, :]) for c in range(KC)]
                                               + [(NT[:, c, t * P:(t + 1) * P], mixM[:, c, :]) for c in range(KC)]):
                    mm = nc.tensor.matmul(o[:, 0:D], lhs, rhs, start=(n == 0), stop=(n == 3))
                mm.then_inc(pv_full, 1)
            if level < 3:
                return

            normalised_transposed(1)
            for c in range(KC):
                for t in range(T):
                    mm = nc.tensor.matmul(PACC[:, c:c + 1], N[:, t, c * P:(c + 1) * P], valid[:, t:t + 1],
                                          start=(t == 0), stop=(t == T - 1))
            mm.then_inc(route_mm, 1)
            pe.wait_ge(route_sb, 1)
            pe.wait_ge(cols_loaded, 16)
            for c in range(KC):
                mm = nc.tensor.matmul(PACC[:, 8:8 + E0], ybar[:, c, :], wr[:, c, :], start=(c == 0), stop=(c == KC - 1))
            mm.then_inc(route_mm, 1)
            pe.wait_ge(experts_gathered, 256)
            pe.wait_ge(nt_ready, 2 * T)
            first_done = [0] * GROUP
            for g in range(GROUP + 1):
                if g < GROUP:
                    for c in range(8):
                        for half in range(2):
                            o = A.next()
                            n0 = g * GROUP * P + half * HALF
                            for k in range(KC):
                                mm = nc.tensor.matmul(o[:, 0:HALF], w1g[:, c // 4, k, (c % 4) * P:(c % 4 + 1) * P],
                                                      NT[:, k, n0:n0 + HALF], start=(k == 0), stop=(k == KC - 1))
                            mm.then_inc(pa_full, 1)
                    first_done[g] = A.n
                if g >= 1:
                    pe.wait_ge(pa_free, first_done[g - 1])
                    if g == 1:
                        pe.wait_ge(w2_scaled, 1)
                    for t in range(GROUP):
                        o = V.next()
                        for c in range(8):
                            mm = nc.tensor.matmul(o[:, 0:D], hG[:, (g - 1) % 2, c, t * P:(t + 1) * P], w2g[:, c // 4, c % 4, :],
                                                  start=(c == 0), stop=(c == 7))
                        mm.then_inc(pv_full, 1)
            assert V.n == V_FFN0
            if level < 4:
                return

            normalised_transposed(2)
            pe.wait_ge(mix_sb, 7)
            pe.wait_ge(nt_ready, 3 * T)

            def queries_keys_values(t):
                o = A.next()
                for c in range(KC):
                    mm = nc.tensor.matmul(o[:, 0:3 * HD1], NT[:, c, t * P:(t + 1) * P], wqkv[:, c, :],
                                          start=(c == 0), stop=(c == KC - 1))
                mm.then_inc(pa_full, 1)

            def turn_queries(t):
                pe.wait_ge(q_normed, t + 1)
                nc.tensor.transpose(A.next()[:, 0:P], q1[:, t % 2, :], ident[:, :]).then_inc(pa_full, 1)

            def turn_maxima():
                pe.wait_ge(qk_ready, 1)
                nc.tensor.transpose(V.next()[:, 0:P], kmax, ident[:, :]).then_inc(pv_full, 1)

            def spread_maxima():
                pe.wait_ge(qk_ready, 2)
                nc.tensor.matmul(V.next()[:, 0:P], ones[:, :], diag1, start=True, stop=True).then_inc(pv_full, 1)

            def context(first, last):
                pe.wait_ge(qk_ready, 3)
                for t in range(first, last):
                    m = P if t < T - 1 else LAST
                    nc.tensor.matmul(PACC[:, 0:P], kv1[0:m, 1, t, :], kv1[0:m, 0, t, :], start=(t == 0), stop=False)
                if last == T:
                    nc.tensor.matmul(PACC[:, 0:P], memv, memk, start=False, stop=True)

            def key_sums():
                for t in range(T):
                    m = P if t < T - 1 else LAST
                    nc.tensor.matmul(PACC[:, P:P + 1], kv1[0:m, 0, t, :], ones[0:m, 0:1], start=(t == 0), stop=False)
                nc.tensor.matmul(PACC[:, P:P + 1], memk, ones[0:MEM, 0:1], start=False, stop=True).then_inc(mix_mm, 1)

            def context_out():
                pe.wait_ge(qk_ready, 4)
                nc.tensor.matmul(V.next()[:, 0:D], ctx_bd, wout1, start=True, stop=True).then_inc(pv_full, 1)

            def attention_out(t):
                if t == 0:
                    pe.wait_ge(qk_ready, 5)
                    pe.wait_ge(pa_free, A_MIX1 + 2 * T)
                nc.tensor.matmul(V.next()[:, 0:D], qT[:, t * P:(t + 1) * P], m2, start=True, stop=True).then_inc(pv_full, 1)

            beside_hop3 = {}
            for t in range(T):
                beside_hop3[t, 0] = lambda t=t: queries_keys_values(t)
                beside_hop3[t + 1, 1] = lambda t=t: turn_queries(t)
                beside_hop3[ROUND_OUT + t // 2, t % 2] = lambda t=t: attention_out(t)
            beside_hop3[T + 1, 0] = turn_maxima
            beside_hop3[T + 2, 0] = spread_maxima
            for n in range(5):
                beside_hop3[T + 4 + n // 2, n % 2] = lambda n=n: context(5 * n, 5 * n + 5)
            beside_hop3[T + 6, 1] = key_sums
            beside_hop3[T + 8, 0] = context_out
            if level < 5:
                return

            def wide(weights, src, chunks, ready):
                ends = []
                for s in range(SLICES):
                    if ready:
                        pe.wait_ge(pa_free, ready[s])
                    for c in range(weights.shape[2] // P):
                        o = A.next()
                        for k in range(chunks):
                            mm = nc.tensor.matmul(o[:, 0:SL], weights[:, k, c * P:(c + 1) * P], src[:, k, s * SL:(s + 1) * SL],
                                                  start=(k == 0), stop=(k == chunks - 1))
                        mm.then_inc(pa_full, 1)
                    ends.append(A.n)
                return ends

            pe.wait_ge(at_ready, 4)
            product_pass(pe, 3, beside_hop3)
            assert V.n == V_MIX1 and A.n == A_MIX1 + 2 * T
            pe.wait_ge(w1_loaded, 32)
            pe.wait_ge(added[3], 2 + ROUNDS)
            pe.wait_ge(at_ready, 5)
            ends = wide(w1a, AT, KC, None)
            ends = wide(w1b, HT, HC, ends)
            pe.wait_ge(pa_free, A.n)
            pe.sem_inc(w1_used, 1)
            transposes(pe, A, lambda t, c: AT[:, c, t * P:(t + 1) * P], HC)
            pe.wait_ge(at_ready, 6)
            product_pass(pe, 4)
            pe.wait_ge(at_ready, 7)
            pe.wait_ge(w2a_loaded, 16)
            wide(w2a, AT, HC, None)
            pe.wait_ge(pa_free, A.n)
            pe.wait_ge(w2b_loaded, 16)
            for t in range(T):
                o = V.next()
                for c in range(HC):
                    mm = nc.tensor.matmul(o[:, 0:D], HT[:, c, t * P:(t + 1) * P], w2b[:, c, :], start=(c == 0), stop=(c == HC - 1))
                mm.then_inc(pv_full, 1)
            assert V.n == V_GNN1
            if level < 6:
                return

            normalised_transposed(3)
            pe.wait_ge(nt_ready, 4 * T)
            ends = wide(rw1, NT, KC, None)
            for t in range(T):
                pe.wait_ge(pa_free, ends[((t + 1) * P - 1) // SL])
                mm = nc.tensor.matmul(PACC[:, t * E1:(t + 1) * E1], VB[:, t * P:(t + 1) * P], rw2, start=True, stop=True)
            mm.then_inc(route_mm, 1)
            pe.wait_ge(route_sb, 2)
            for q in range(0, T, 4):
                o = A.next()
                for t in range(q, min(q + 4, T)):
                    mm = nc.tensor.transpose(o[0:E1, (t - q) * P:(t - q + 1) * P], route[5][:, t, :], ident[:, :])
                mm.then_inc(pa_full, 1)
            pe.wait_ge(pa_free, A.n)
            for t in range(T):
                nc.tensor.matmul(V.next()[:, 0:D], wT[:, t * P:(t + 1) * P], b3, start=True, stop=True).then_inc(pv_full, 1)
            assert V.n == V_B3
            for e in range(E1):
                w = we[:, e % 2]
                pe.wait_ge(experts_loaded[e % 2], 16 * (e // 2 + 1))
                ends = wide(w[:, 0], NT, KC, None)
                ends = wide(w[:, 1], h1, KC, ends)
                for t in range(T):
                    pe.wait_ge(pa_free, ends[((t + 1) * P - 1) // SL])
                    o = V.next()
                    for k in range(KC):
                        mm = nc.tensor.matmul(o[:, 0:D], h2[:, k, t * P:(t + 1) * P], w[:, 2, k, :], start=(k == 0), stop=(k == KC - 1))
                    mm.then_inc(pv_full, 1)

        @block.scalar
        def _(act):
            A = Bank(act, TA, pa_full, False)
            st = Steps(act, act_step)
            roots = [0]

            def root(v):
                roots[0] += 1
                act.wait_ge(asked, roots[0])
                nc.scalar.activation(v, v, ACT.Sqrt).then_inc(answered, 1)

            def exp(v):
                roots[0] += 1
                act.wait_ge(asked, roots[0])
                nc.scalar.activation(v, v, ACT.Exp).then_inc(answered, 1)

            def transposed_copies():
                for t in range(T):
                    o = A.next()
                    nc.scalar.copy(NT[:, :, t * P:(t + 1) * P], o[:, 0:D].rearrange("p (c n) -> p c n", n=P)).then_inc(pa_free, 1)
                    act.wait_ge(pa_free, A.n)
                    act.sem_inc(nt_ready, 1)

            root(rstd)
            transposed_copies()
            root(dnode[:, 0:T])

            def table_rows(h):
                for t in range(T):
                    o = A.next()
                    nc.scalar.copy(N[:, t, :], o[:, 0:D]).then_inc(pa_free, 1)
                    act.wait_ge(pa_free, A.n)
                    act.sem_inc(table_sbuf[h - 1], 1)

            table_rows(1)
            for t in range(T):
                b = t % 2
                if t >= 2:
                    act.wait_ge(kv_used, t - 1)
                for half in range(2):
                    o = A.next()
                    part = slice(half * 512, (half + 1) * 512)
                    nc.scalar.copy(kv[:, b, part], o[:, :]).then_inc(kv_ready, 1)
                    nc.scalar.activation(kvsq[:, b, part], o[:, :], ACT.Square).then_inc(pa_free, 1)
                root(sc[:, 256 + 32 * b:256 + 32 * b + 16])
            for j in range(4):
                o = A.next()
                nc.scalar.mul(pj[:, j, :], o[:, 0:D], 1.0 / NODES).then_inc(pa_free, 1)
            act.wait_ge(pa_free, A.n)
            act.sem_inc(mix_sb, 4)
            for c in range(KC):
                o = A.next()
                nc.scalar.copy(mixM[:, c, :], o[:, 0:D]).then_inc(pa_free, 1)
            act.wait_ge(pa_free, A.n)
            act.sem_inc(mix_sb, 1)
            act.wait_ge(table_written[0], 16)
            table_rows(2)

            root(rstd)
            transposed_copies()
            exp(sc[:, 0:8])
            exp(sc[:, 0:8])
            exp(sc[:, 40:41])
            act.wait_ge(experts_gathered, 256)
            for g in range(GROUP):
                for c in range(8):
                    for half in range(2):
                        o = A.next()
                        nc.scalar.activation(hG[:, g % 2, c, half * HALF:(half + 1) * HALF], o[:, 0:HALF], ACT.Gelu,
                                             bias=b1g[:, c:c + 1]).then_inc(pa_free, 1)
            root(rstd)
            if level < 4:
                return

            def norms(src, n):
                for t in range(T):
                    if t:
                        st.settle()
                    st.add(nc.scalar.activation(junk, src[:, t, :], ACT.Square, accum_out=rn[:, t:t + 1]))
                st.settle()
                nc.scalar.activation(rn, rn, ACT.Sqrt).then_inc(norm_asked, 1)

            root(rstd)
            transposed_copies()
            act.wait_ge(xn_ready, 3 * T)
            norms(N, 1)
            act.wait_ge(rn_ready, 1)
            for t in range(T + 1):
                if t < T:
                    o = A.next()
                    nc.scalar.activation(q1[:, t % 2, :], o[:, 0:HD1], ACT.Identity, scale=rn[:, t:t + 1]).then_inc(q_in, 1)
                    nc.scalar.activation(kv1[:, :, t, :], o[:, HD1:3 * HD1].rearrange("p (s c) -> p s c", c=HD1), ACT.Identity,
                                         scale=rn[:, t:t + 1]).then_inc(pa_free, 1)
                if t >= 1:
                    o = A.next()
                    nc.scalar.copy(qT[:, (t - 1) * P:t * P], o[:, 0:P]).then_inc(pa_free, 1)
                if t < T:
                    exp(q1[:, t % 2, :])
            exp(kv1[:, 0, :, :].rearrange("p t c -> p (t c)"))
            exp(memk)
            act.wait_ge(pv_free, V_MIX1)
            norms(Y, 2)
            if level < 5:
                return

            def wide(dst, bias, chunks):
                for s in range(SLICES):
                    for c in range(chunks):
                        o = A.next()
                        nc.scalar.activation(dst[:, c, s * SL:(s + 1) * SL], o[:, 0:SL], ACT.Relu,
                                             bias=bias[:, c:c + 1]).then_inc(pa_free, 1)

            act.wait_ge(table_written[2], 16)
            act.wait_ge(at_ready, 5)
            wide(HT, b1a, HC)
            wide(AT, b1b, HC)
            for t in range(T):
                o = A.next()
                nc.scalar.copy(HN[:, t, :], o[:, :]).then_inc(pa_free, 1)
                act.wait_ge(pa_free, A.n)
                act.sem_inc(table_sbuf[3], 1)
            act.wait_ge(table_written[3], 16)
            wide(HT, b2a, HC)
            if level < 6:
                return

            root(rstd)
            transposed_copies()
            wide(VB[:, :].rearrange("p (c n) -> p c n", c=1), rb1, 1)
            exp(route[0].rearrange("p t e -> p (t e)"))
            exp(rcol[0])
            for q in range(0, T, 4):
                n = (min(q + 4, T) - q) * P
                o = A.next()
                nc.scalar.copy(wT[:, q * P:q * P + n], o[0:E1, 0:n]).then_inc(pa_free, 1)
            for e in range(E1):
                wide(h1, eb1[:, 2 * e:2 * e + 2], KC)
                wide(h2, eb2[:, 2 * e:2 * e + 2], KC)

        @block.vector
        def _(dve):
            st = Steps(dve, dve_step)
            V = Bank(dve, TV, pv_full, False)

            dve.wait_ge(edges_loaded, 48)
            dve.wait_ge(dst_loaded, 16)
            dve.wait_ge(pool_step, 7)
            low, high = sc[0:ROUNDS, 80:81], sc[0:ROUNDS, 81:82]
            dstf = AS[0:ROUNDS, U * P:2 * U * P]
            st.add(nc.vector.tensor_copy(rel[:, :], rel[:, :].bitcast(I32)))
            st.do(nc.vector.tensor_copy(dstf, AS[0:ROUNDS, 0:U * P].bitcast(I32)))
            st.add(nc.vector.tensor_reduce(low, dstf, AX, ALU.min))
            st.do(nc.vector.tensor_reduce(high, dstf, AX, ALU.max))
            nc.vector.tensor_scalar(sc[0:ROUNDS, 0:ROUNDS], ident[0:ROUNDS, 0:ROUNDS], low, None, ALU.mult).then_inc(diag_ready, 1)
            nc.vector.tensor_tensor(sc[0:ROUNDS, 82:83], high, low, ALU.subtract).then_inc(diag_ready, 1)
            dve.wait_ge(range_mm, 1)
            rel_r = rel[:, :].rearrange("p (r k) -> p r k", k=U)
            st.add(nc.vector.tensor_tensor(rel_r, rel_r, PACC[:, 0:ROUNDS].unsqueeze(2).to_broadcast([P, ROUNDS, U]), ALU.subtract))
            st.do(nc.vector.tensor_copy(first_base[:, :], PACC[0:1, 0:ROUNDS]))
            nc.vector.tensor_copy(base_i[:, :], first_base[:, :]).then_inc(ranges_ready, 1)
            o = V.next()
            nc.vector.tensor_reduce(sc[0:1, 83:84], o[0:1, 0:ROUNDS], AX, ALU.max).then_inc(pv_free, 1)
            st.add(nc.vector.tensor_scalar(sc[0:1, 96:96 + T - 1], iota_w[0:1, 1:T], float(P), None, ALU.mult))
            dve.wait_ge(pv_free, V.n)
            st.settle()
            st.do(nc.vector.tensor_scalar(sc[0:1, 128:128 + T - 1], sc[0:1, 96:96 + T - 1], sc[0:1, 83:84], None, ALU.is_le))
            st.do(nc.vector.tensor_reduce(sc[0:1, 84:85], sc[0:1, 128:128 + T - 1], AX, ALU.add))
            nc.vector.tensor_scalar(passes_i[:, :], sc[0:1, 84:85], 1.0, None, ALU.add).then_inc(ranges_ready, 1)
            dve.wait_ge(ranges_ready, 2)

            roots = [0]

            def one_over_root(v):
                roots[0] += 1
                dve.wait_ge(answered, roots[0])
                st.do(nc.vector.reciprocal(v, v))

            def statistics(src):
                for t in range(T):
                    st.add(nc.vector.bn_stats(stats[:, t, :], src[:, t, :]))
                st.settle()
                for t in range(T):
                    st.add(nc.vector.bn_aggr(mv[:, t, :], stats[:, t, :]))
                st.settle()
                nc.vector.tensor_scalar(rstd, mv[:, :, 1], LN_EPS, None, ALU.add).then_inc(asked, 1)
                one_over_root(rstd)

            def normalise():
                statistics(X)
                for t in range(T):
                    nc.vector.tensor_scalar(N[:, t, :], X[:, t, :], mv[:, t, 0:1], rstd[:, t:t + 1],
                                            ALU.subtract, ALU.mult).then_inc(xn_ready, 1)

            dve.wait_ge(wa_loaded[0], 64)
            heads = WA[:, 0:2048].rearrange("p (g d) -> p g d", d=DH0)
            st.do(nc.vector.tensor_reduce(sc[:, 256:256 + 32], heads, AX, ALU.add))
            st.do(nc.vector.tensor_scalar(sc[:, 256:256 + 32], sc[:, 256:256 + 32], 1.0 / DH0, None, ALU.mult))
            nc.vector.tensor_tensor(heads, heads, sc[:, 256:256 + 32].unsqueeze(2).to_broadcast([P, 32, DH0]),
                                    ALU.subtract).then_inc(wkv_centred, 1)
            dve.wait_ge(x_loaded, 32)
            normalise()

            def degrees():
                st.add(nc.vector.memset(wflat, 0.0))
                st.add(nc.vector.memset(VB[0:PARTS, :], 0.0))
                st.add(nc.vector.tensor_copy(iota16, iota_w[:, :]))
                st.settle()
                st.add(nc.vector.memset(VB[0:1, :], 1.0))
                for part in range(3):
                    st.do(nc.vector.tensor_copy(wparts[:, :, part], wgt[:, :] if part == 0 else wrest))
                    if part < 2:
                        st.do(nc.vector.tensor_tensor(wrest, wgt[:, :] if part == 0 else wrest, wparts[:, :, part], ALU.subtract))
                degree_sums(dve, st)
                dve.sem_inc(degree_ready, 1)
                dve.wait_ge(degree_moved, 64)
                for part in (2, 0):
                    st.do(nc.vector.tensor_tensor(dnode[:, T:2 * T], dnode[:, T:2 * T], dnode[:, part * T:(part + 1) * T], ALU.add))
                st.do(nc.vector.tensor_copy(dnode[:, 0:T], dnode[:, T:2 * T]))
                st.do(nc.vector.tensor_scalar(dnode[:, T:2 * T], dnode[:, 0:T], 0.0, None, ALU.is_gt))
                nc.vector.tensor_scalar(dnode[:, 0:T], dnode[:, 0:T], 1e-12, None, ALU.max).then_inc(asked, 1)
                one_over_root(dnode[:, 0:T])
                nc.vector.tensor_tensor(dnode[:, 0:T], dnode[:, 0:T], dnode[:, T:2 * T], ALU.mult).then_inc(degree_ready, 1)
                dve.wait_ge(degree_moved, 96)

            def normalise_kv(t):
                b = t % 2
                dve.wait_ge(kv_ready, 2 * t + 2)
                dve.wait_ge(pa_free, 2 * T + 2 * t + 2)
                ss = sc[:, 256 + 32 * b:256 + 32 * b + 16]
                st.do(nc.vector.tensor_reduce(ss, kvsq[:, b, :].rearrange("p (g d) -> p g d", d=DH0), AX, ALU.add))
                nc.vector.tensor_scalar(ss, ss, 1.0 / DH0, LN_EPS, ALU.mult, ALU.add).then_inc(asked, 1)
                one_over_root(ss)
                r = sc[:, 320 + 8 * b:328 + 8 * b]
                st.do(nc.vector.tensor_tensor(r, ss[:, 0:8], ss[:, 8:16], ALU.mult))
                vh = kv[:, b, 512:1024].rearrange("p (g d) -> p g d", d=DH0)
                nc.vector.tensor_tensor(vh, vh, r.unsqueeze(2).to_broadcast([P, H0, DH0]), ALU.mult).then_inc(kv_normed, 1)

            def head_products_out():
                st.do(nc.vector.memset(bdT, 0.0))
                dve.wait_ge(kv_used, T)
                for half in range(2):
                    s = slice(half * DH0, (half + 1) * DH0)
                    st.add(nc.vector.tensor_copy(bdT[s, :, s], PACC[s, :].rearrange("p (j d) -> p j d", d=P)[:, :, s]))
                st.settle()
                dve.sem_inc(mix_sb, 1)

            degrees()
            dve.wait_ge(bias_loaded, 32)
            st.do(nc.vector.tensor_tensor(bias_b[:, :], bias_b[:, :], mixb_b, ALU.add))
            st.do(nc.vector.memset(AT[:, 0:KC, NP:WIDE], 0.0))
            dve.wait_ge(nt_ready, T)
            dinv = VB[:, 0:NP]
            for c in range(KC):
                st.add(nc.vector.tensor_tensor(AT[:, c, 0:NP], NT[:, c, :], dinv, ALU.mult))
            st.settle()
            dve.sem_inc(at_ready, 1)
            for h in (1, 2):
                dve.wait_ge(table_sbuf[h - 1], T)
                add_pass(dve, st, h, {2 * t + 1: lambda t=t: normalise_kv(t) for t in range(T)} if h == 1 else None)
                if h == 1:
                    head_products_out()
                for c in range(KC):
                    st.add(nc.vector.scalar_tensor_tensor(out=AT[:, c, 0:NP], in0=AT[:, c, 0:NP], scalar=0.5, in1=dinv,
                                                          op0=ALU.mult, op1=ALU.mult))
                st.settle()
                for c in range(KC):
                    st.add(nc.vector.scalar_tensor_tensor(out=AT[:, c, 0:NP], in0=NT[:, c, :], scalar=0.5, in1=AT[:, c, 0:NP],
                                                          op0=ALU.mult, op1=ALU.add))
                st.settle()
                for c in range(KC):
                    if h == 1:
                        st.add(nc.vector.tensor_tensor(AT[:, c, 0:NP], AT[:, c, 0:NP], dinv, ALU.mult))
                    else:
                        st.add(nc.vector.tensor_scalar(AT[:, c, 0:NP], AT[:, c, 0:NP], 0.0, None, ALU.max))
                st.settle()
                dve.sem_inc(at_ready, 1)
            for t in range(T):
                st.add(nc.vector.tensor_tensor(X[:, t, :], X[:, t, :], bias_b[:, :], ALU.add))
            st.settle()
            def accumulate(dst):
                for t in range(T):
                    o = V.next()
                    nc.vector.tensor_tensor(dst[:, t, :], dst[:, t, :], o[:, 0:D], ALU.add).then_inc(pv_free, 1)
                dve.wait_ge(pv_free, V.n)

            def softmax(v, part, stat):
                wide_stat = stat.unsqueeze(2).to_broadcast(list(part.shape))
                st.do(nc.vector.tensor_reduce(stat, part, AX, ALU.max))
                nc.vector.tensor_tensor(part, part, wide_stat, ALU.subtract).then_inc(asked, 1)
                answer()
                st.do(nc.vector.tensor_reduce(stat, part, AX, ALU.add))
                st.do(nc.vector.reciprocal(stat, stat))
                st.do(nc.vector.tensor_tensor(part, part, wide_stat, ALU.mult))

            def answer():
                roots[0] += 1
                dve.wait_ge(answered, roots[0])

            accumulate(X)
            if level < 3:
                dve.sem_inc(stored_ready, 1)
                return

            normalise()
            dve.wait_ge(route_mm, 1)
            for c in range(KC):
                st.add(nc.vector.tensor_scalar(ybar[:, c, :], PACC[:, c:c + 1].to_broadcast([P, P]), 1.0 / NODES, None, ALU.mult))
            st.settle()
            dve.sem_inc(route_sb, 1)
            dve.wait_ge(route_mm, 2)
            dve.wait_ge(cols_loaded, 16)
            rw = sc[:, 0:8]
            rw3, stat = rw.unsqueeze(1), sc[:, 8:9]
            st.do(nc.vector.tensor_tensor(rw, PACC[:, 8:16], br, ALU.add))
            softmax(rw, rw3, stat)
            st.do(nc.vector.tensor_scalar(sc[:, 16:24], rw, float(NODES), None, ALU.mult))
            st.do(nc.vector.reciprocal(sc[:, 16:24], sc[:, 16:24]))
            st.do(nc.vector.tensor_scalar(sc[:, 16:24], sc[:, 16:24], CAPACITY, 1.0, ALU.mult, ALU.min))
            st.do(nc.vector.tensor_tensor(rw, rw, sc[:, 16:24], ALU.mult))
            softmax(rw, rw3, stat)
            st.do(nc.vector.max(sc[:, 24:32], rw))
            st.do(nc.vector.max_index(sc[:, 32:40].bitcast(U32), sc[:, 24:32], rw))
            nc.vector.tensor_tensor(sc[:, 40:41], sc[:, 25:26], sc[:, 24:25], ALU.subtract).then_inc(asked, 1)
            st.do(nc.vector.tensor_copy(sc[:, 48:50], sc[:, 32:34].bitcast(U32)))
            for e in range(2):
                chosen = sc[:, 48 + e:49 + e]
                for i, (first, n, rows_each) in enumerate(((0, KC, D), (2, HC, HID), (6, 1, P))):
                    k = sc[:, 56 + 4 * e + i:57 + 4 * e + i]
                    st.do(nc.vector.tensor_scalar(k, chosen, float(rows_each), None, ALU.mult))
                    st.add(nc.vector.tensor_scalar(gidx[:, 8 * e + first:8 * e + first + n], iota4[:, 0:n], k, None, ALU.add))
                st.add(nc.vector.tensor_copy(gidx[:, 8 * e + 7:8 * e + 8], chosen))
            st.settle()
            dve.sem_inc(idx0_ready, 1)
            answer()
            st.do(nc.vector.tensor_scalar(sc[:, 41:42], sc[:, 40:41], 1.0, None, ALU.add))
            st.do(nc.vector.reciprocal(sc[:, 41:42], sc[:, 41:42]))
            st.do(nc.vector.tensor_tensor(sc[:, 42:43], sc[:, 40:41], sc[:, 41:42], ALU.mult))
            dve.wait_ge(experts_gathered, 256)
            for e in range(2):
                st.add(nc.vector.tensor_scalar(WA[:, 2048 + 1024 * e:3072 + 1024 * e], WA[:, 2048 + 1024 * e:3072 + 1024 * e],
                                               sc[:, 41 + e:42 + e], None, ALU.mult))
                st.add(nc.vector.tensor_scalar(b2g[:, e, :], b2g[:, e, :], sc[:, 41 + e:42 + e], None, ALU.mult))
            st.settle()
            dve.sem_inc(w2_scaled, 1)
            st.do(nc.vector.tensor_tensor(b2c, b2g[:, 0, :], b2g[:, 1, :], ALU.add))
            nodes_wide = [P, T, D]
            dve.wait_ge(nt_ready, 2 * T)
            st.do(nc.vector.tensor_tensor(N, N, b2c.unsqueeze(1).to_broadcast(nodes_wide), ALU.add))
            accumulate(N)
            statistics(N)
            for t in range(T):
                st.add(nc.vector.tensor_scalar(N[:, t, :], N[:, t, :], mv[:, t, 0:1], rstd[:, t:t + 1], ALU.subtract, ALU.mult))
            st.settle()
            dve.wait_ge(b2_loaded, 32)
            st.do(nc.vector.tensor_tensor(N, N, gamma_b.unsqueeze(1).to_broadcast(nodes_wide), ALU.mult))
            st.do(nc.vector.tensor_tensor(N, N, beta_b.unsqueeze(1).to_broadcast(nodes_wide), ALU.add))
            st.do(nc.vector.tensor_tensor(X[:, :, :], X[:, :, :], N, ALU.add))
            if level < 4:
                dve.sem_inc(stored_ready, 1)
                return

            normalise()
            dve.wait_ge(wb_loaded, 160)
            st.add(nc.vector.tensor_scalar(gpre, gpre, float(D) ** 0.5, None, ALU.mult))
            st.do(nc.vector.tensor_scalar(gout_b, gout_b, float(D) ** 0.5, None, ALU.mult))
            for c in range(KC):
                st.add(nc.vector.tensor_scalar(wqkv[:, c, :], wqkv[:, c, :], gpre[:, c:c + 1], None, ALU.mult))
            st.settle()
            dve.sem_inc(mix_sb, 1)

            def over_norm(n):
                dve.wait_ge(norm_asked, n)
                st.do(nc.vector.tensor_scalar(rn, rn, 1e-12, None, ALU.max))
                nc.vector.reciprocal(rn, rn).then_inc(rn_ready, 1)
                dve.wait_ge(rn_ready, n)

            over_norm(1)

            def normalise_queries(t):
                q3 = q1[:, t % 2, :].rearrange("p (h d) -> p h d", d=DH1)
                stat = sc[:, 8 * (t % 2):8 * (t % 2) + H1]
                wide_stat = stat.unsqueeze(2).to_broadcast([P, H1, DH1])
                dve.wait_ge(q_in, t + 1)
                st.do(nc.vector.tensor_reduce(stat, q3, AX, ALU.max))
                nc.vector.tensor_tensor(q3, q3, wide_stat, ALU.subtract).then_inc(asked, 1)
                answer()
                st.do(nc.vector.tensor_reduce(stat, q3, AX, ALU.add))
                st.do(nc.vector.reciprocal(stat, stat))
                nc.vector.tensor_tensor(q3, q3, wide_stat, ALU.mult).then_inc(q_normed, 1)

            def key_maxima():
                dve.wait_ge(pa_free, out_of_ring(T - 1))
                st.do(nc.vector.tensor_reduce(kmax, kv1[:, 0, 0:T - 1, :].rearrange("p t c -> p c t"), AX, ALU.max))
                nc.vector.tensor_tensor(kmax[0:LAST, :], kmax[0:LAST, :], kv1[0:LAST, 0, T - 1, :], ALU.max).then_inc(qk_ready, 1)

            def all_maxima():
                o = V.next()
                st.add(nc.vector.tensor_reduce(sc[:, 17:18], memkT, AX, ALU.max))
                nc.vector.tensor_reduce(sc[:, 16:17], o[:, 0:P], AX, ALU.max).then_inc(pv_free, 1)
                dve.wait_ge(pv_free, V.n)
                st.settle()
                st.do(nc.vector.tensor_tensor(sc[:, 16:17], sc[:, 16:17], sc[:, 17:18], ALU.max))
                nc.vector.tensor_scalar(diag1, ident[:, :], sc[:, 16:17], None, ALU.mult).then_inc(qk_ready, 1)

            def keys_less_maxima():
                o = V.next()
                k3 = kv1[:, 0, :, :]
                nc.vector.tensor_tensor(k3, k3, o[:, 0:P].unsqueeze(1).to_broadcast([P, T, P]), ALU.subtract).then_inc(asked, 1)
                dve.wait_ge(asked, roots[0] + 1)
                nc.vector.tensor_tensor(memk, memk, o[0:MEM, 0:P], ALU.subtract).then_inc(asked, 1)
                dve.wait_ge(asked, roots[0] + 2)
                dve.sem_inc(pv_free, 1)

            def keys_ready():
                answer()
                answer()
                dve.sem_inc(qk_ready, 1)
                st.do(nc.vector.memset(ctx_bd, 0.0))

            def context_heads():
                dve.wait_ge(mix_mm, 1)
                for h in range(H1):
                    s = slice(h * DH1, (h + 1) * DH1)
                    st.add(nc.vector.tensor_copy(ctx_bd[s, s], PACC[s, s]))
                st.do(nc.vector.reciprocal(sc[:, 18:19], PACC[:, P:P + 1]))
                st.do(nc.vector.tensor_scalar(sc[:, 18:19], sc[:, 18:19], float(DH1) ** -0.5, None, ALU.mult))
                dve.sem_inc(qk_ready, 1)

            def context_scaled():
                o = V.next()
                nc.vector.tensor_scalar(m2, o[:, 0:D], sc[:, 18:19], None, ALU.mult).then_inc(pv_free, 1)
                dve.wait_ge(pv_free, V.n)
                dve.sem_inc(qk_ready, 1)

            def attention_in(t):
                nc.vector.tensor_tensor(Y[:, t, :], V.next()[:, 0:D], bout_b, ALU.add).then_inc(pv_free, 1)

            beside_hop3 = {t: lambda t=t: normalise_queries(t) for t in range(T)}
            beside_hop3[T] = key_maxima
            beside_hop3[T + 1] = all_maxima
            beside_hop3[T + 2] = keys_less_maxima
            beside_hop3[T + 3] = keys_ready
            beside_hop3[T + 7] = context_heads
            beside_hop3[T + 8] = context_scaled
            for t in range(0, T, 2):
                beside_hop3[ROUND_OUT + t // 2] = lambda t=t: [attention_in(n) for n in range(t, min(t + 2, T))]

            def attention_normed():
                over_norm(2)
                for t in range(T):
                    st.add(nc.vector.tensor_scalar(Y[:, t, :], Y[:, t, :], rn[:, t:t + 1], None, ALU.mult))
                st.settle()

            def into_stream():
                st.do(nc.vector.tensor_tensor(X[:, :, :], X[:, :, :], N, ALU.add))
                st.do(nc.vector.tensor_tensor(X[:, :, :], X[:, :, :], Y, ALU.add))

            beside_hop3[ROUNDS - 3] = attention_normed
            beside_hop3[ROUNDS - 2] = lambda: st.do(nc.vector.tensor_tensor(
                Y, Y, gout_b.unsqueeze(1).to_broadcast(nodes_wide), ALU.mult))

            st.add(nc.vector.memset(wgt[:, 0:C - 1], 1.0))
            st.add(nc.vector.tensor_scalar(wgt[:, C - 1:C], iota_p, float(EDGES - (C - 1) * P), None, ALU.is_lt))
            st.add(nc.vector.memset(AT[:, :, NP:WIDE], 0.0))
            st.do(nc.vector.tensor_scalar(eps_c, eps_in, 1.0, None, ALU.add))
            for c in range(KC):
                st.add(nc.vector.tensor_scalar(AT[:, c, 0:NP], NT[:, c, :], eps_c[:, 0:1], None, ALU.mult))
            st.settle()
            dve.sem_inc(at_ready, 1)
            add_pass(dve, st, 3, beside_hop3)
            into_stream()
            dve.sem_inc(at_ready, 1)
            dve.wait_ge(table_sbuf[3], T)
            for c in range(HC):
                st.add(nc.vector.tensor_scalar(AT[:, c, 0:NP], AT[:, c, 0:NP], eps_c[:, 1:2], None, ALU.mult))
            st.settle()
            dve.sem_inc(at_ready, 1)
            add_pass(dve, st, 4)
            dve.sem_inc(at_ready, 1)
            st.do(nc.vector.tensor_tensor(X[:, :, :], X[:, :, :], b2b_b.unsqueeze(1).to_broadcast(nodes_wide), ALU.add))
            accumulate(X)
            if level < 6:
                dve.sem_inc(stored_ready, 1)
                return

            normalise()
            dve.wait_ge(route_mm, 3)
            p, hit, rest, one, two, dense = route
            groups = [P, T, E1]
            c0, c1, c2, c3, c4 = rcol[0:5]

            def each(col):
                return col.unsqueeze(2).to_broadcast(groups)

            st.do(nc.vector.tensor_tensor(p, PACC[:, 0:T * E1].rearrange("p (t e) -> p t e", e=E1),
                                          rb2.unsqueeze(1).to_broadcast(groups), ALU.add))
            softmax(p, p, c0)
            index = iota6.unsqueeze(1).to_broadcast(groups)

            def first_hit(prob, best, mask):
                st.do(nc.vector.tensor_reduce(best, prob, AX, ALU.max))
                st.do(nc.vector.tensor_tensor(hit, prob, each(best), ALU.is_lt))
                st.do(nc.vector.tensor_scalar(hit, hit, 99.0, None, ALU.mult))
                st.do(nc.vector.tensor_tensor(hit, hit, index, ALU.add))
                st.do(nc.vector.tensor_reduce(c4, hit, AX, ALU.min))
                st.do(nc.vector.tensor_tensor(mask, hit, each(c4), ALU.is_equal))

            first_hit(p, c1, one)
            st.do(nc.vector.tensor_scalar(rest, one, -2.0, None, ALU.mult))
            st.do(nc.vector.tensor_tensor(rest, rest, p, ALU.add))
            first_hit(rest, c2, two)
            nc.vector.tensor_tensor(c0, c2, c1, ALU.subtract).then_inc(asked, 1)
            answer()
            st.do(nc.vector.tensor_scalar(c1, c0, 1.0, None, ALU.add))
            st.do(nc.vector.reciprocal(c1, c1))
            st.do(nc.vector.tensor_tensor(c2, c0, c1, ALU.mult))
            st.do(nc.vector.tensor_tensor(one, one, each(c1), ALU.mult))
            st.do(nc.vector.tensor_tensor(two, two, each(c2), ALU.mult))
            st.do(nc.vector.tensor_tensor(dense, one, two, ALU.add))
            dve.sem_inc(route_sb, 1)
            accumulate(X)
            for e in range(E1):
                for t in range(T):
                    o = V.next()
                    nc.vector.scalar_tensor_tensor(out=X[:, t, :], in0=o[:, 0:D], scalar=dense[:, t, e:e + 1], in1=X[:, t, :],
                                                   op0=ALU.mult, op1=ALU.add).then_inc(pv_free, 1)
            dve.wait_ge(pv_free, V.n)
            dve.sem_inc(stored_ready, 1)


STOP = None


def kernel(**inputs):
    import numpy as np
    import concourse.bacc as bacc
    from concourse.bass_utils import run_bass_kernel_spmd

    def by_partition(m):
        m = np.asarray(m)
        return np.ascontiguousarray(m.reshape(-1, P, m.shape[1]).transpose(1, 0, 2).reshape(P, -1))

    def columns(v):
        return np.asarray(v).reshape(-1, P).T

    def rows_of(v):
        return np.broadcast_to(np.asarray(v).reshape(1, -1), (P, np.asarray(v).size))

    g = {k: np.asarray(v) for k, v in inputs.items()}
    mem = g["L1_mix_mem_kv"]
    pad = C * P - EDGES
    src = np.pad(g["src"], (0, pad)).astype(np.int32)
    src_pc = src.reshape(C, P).T
    dst = np.pad(g["dst"], (0, pad), mode="edge").astype(np.int32)
    ew = np.pad(g["edge_weight"], (0, pad))
    arrays = {
        "x": g["x"],
        "src_pc": np.concatenate([src_pc, src_pc[:, :U]], axis=1), "dst_pc": dst.reshape(C, P).T, "wgt_pc": ew.reshape(C, P).T,
        "dst_rounds": dst.reshape(ROUNDS, U * P),
        "wkvT": by_partition(g["L0_mix_w_qkv"][512:].T), "wq": by_partition(g["L0_mix_w_qkv"][:512]),
        "woT": by_partition(g["L0_mix_w_out"].T), "wgT": by_partition(g["L0_gnn_W"].T),
        "L0_gnn_b": g["L0_gnn_b"], "L0_mix_b_out": g["L0_mix_b_out"],
        "L0_ffn_gamma": g["L0_ffn_gamma"], "L0_ffn_beta": g["L0_ffn_beta"],
        "w1_rows": g["L0_ffn_W1"].reshape(E0 * D, HID), "w2_rows": g["L0_ffn_W2"].reshape(E0 * HID, D),
        "b1_rows": g["L0_ffn_b1"].reshape(E0, HC, P).transpose(0, 2, 1).reshape(E0 * P, HC), "b2_rows": g["L0_ffn_b2"],
        "cols": np.concatenate([
            mem[0].reshape(HD1, MEM), columns(g["L1_mix_g_pre"]), columns(g["L1_gnn_b1a"]), columns(g["L1_gnn_b1b"]),
            columns(g["L1_gnn_b2a"]), columns(g["L1_ffn_expert_b1"]), columns(g["L1_ffn_expert_b2"]),
            columns(g["L1_ffn_router_b1"]), rows_of(g["L1_ffn_router_b2"]), by_partition(g["L0_ffn_Wr"]),
            rows_of(g["L0_ffn_br"]), rows_of(g["L1_gnn_eps1"]), rows_of(g["L1_gnn_eps2"])], axis=1),
        "wqkv1": by_partition(g["L1_mix_w_qkv"]), "L1_mix_w_out": g["L1_mix_w_out"],
        "memk": mem[0].reshape(HD1, MEM).T, "memv": mem[1].reshape(HD1, MEM).T,
        "rw1": by_partition(g["L1_ffn_router_w1"]), "L1_ffn_router_w2": g["L1_ffn_router_w2"],
        "L1_ffn_expert_b3": g["L1_ffn_expert_b3"], "L1_mix_g_out": g["L1_mix_g_out"], "L1_mix_b_out": g["L1_mix_b_out"],
        "L1_gnn_b2b": g["L1_gnn_b2b"],
        "w1a": by_partition(g["L1_gnn_W1a"]), "w1b": by_partition(g["L1_gnn_W1b"]),
        "w2a": by_partition(g["L1_gnn_W2a"]), "w2b": by_partition(g["L1_gnn_W2b"]),
        "experts1": np.stack([np.concatenate([by_partition(g[f"L1_ffn_expert_w{i}"][e]) for i in (1, 2, 3)], axis=1)
                              for e in range(E1)]),
    }
    nc = bacc.Bacc("TRN2", target_bir_lowering=False, num_devices=1)
    arrays = {"in_" + k: np.ascontiguousarray(v) for k, v in arrays.items()}
    args = {k[3:]: nc.dram_tensor(k, v.shape, mybir.dt.from_np(v.dtype), kind="ExternalInput").ap()
            for k, v in arrays.items()}
    out = nc.dram_tensor("out_0", (NODES, D), F32, kind="ExternalOutput").ap()
    build(nc, args, out, STOP)
    r = run_bass_kernel_spmd(nc, [arrays], core_ids=[0])
    return r.results[0]["out_0"]
```

```python
from contextlib import ExitStack

import concourse.bass as bass
from concourse import mybir

F32 = mybir.dt.float32
F16 = mybir.dt.float16
BF16 = mybir.dt.bfloat16
I32 = mybir.dt.int32
U32 = mybir.dt.uint32
ALU = mybir.AluOpType
ACT = mybir.ActivationFunctionType
AX = mybir.AxisListType.X

P = 128
NODES, D = 3125, 256
EDGES = 53125
T = -(-NODES // P)
LAST = NODES - (T - 1) * P
NP = T * P
WIDE = NP + P
U = 8
C = -(-EDGES // (P * U)) * U
ROUNDS = C // U
KC = D // P
HID = 512
HC = HID // P
SL = 400
SLICES = NP // SL
PARTS = 4
LN_EPS = 1e-5
H0, DH0 = 8, 64
E0, CAP_FACTOR = 8, 1.25
CAPACITY = float(-int(-(NODES * CAP_FACTOR) // E0))
GROUP = 5
HALF = GROUP * P // 2
GROUPS = T // GROUP
GN = GROUP * P
H1, DH1, MEM = 4, 32, 4
HD1 = H1 * DH1
E1 = 6


class Bank:

    def __init__(self, eng, banks, wait_on, writer):
        self.eng, self.banks, self.wait_on, self.writer, self.n = eng, banks, wait_on, writer, 0

    def next(self):
        need = self.n + 1 - (len(self.banks) if self.writer else 0)
        if need > 0:
            self.eng.wait_ge(self.wait_on, need)
        bank = self.banks[self.n % len(self.banks)]
        self.n += 1
        return bank


class Steps:

    def __init__(self, eng, sem):
        self.eng, self.sem, self.n = eng, sem, 0

    def add(self, ins):
        ins.then_inc(self.sem, 1)
        self.n += 1

    def settle(self):
        self.eng.wait_ge(self.sem, self.n)

    def do(self, ins):
        self.add(ins)
        self.settle()


def build(nc, a, out):
    with ExitStack() as ctx:
        def sb(name, shape, dt=F32):
            return ctx.enter_context(nc.sbuf_tensor(name, shape, dt))

        def sem(name):
            return ctx.enter_context(nc.semaphore(name))

        X = sb("X", [P, T, D])
        NN = sb("NN", [P, 2 * T * D])
        N = NN[:, 0:T * D].rearrange("p (t d) -> p t d", d=D)
        NT = NN[:, T * D:2 * T * D].rearrange("p (c n) -> p c n", n=NP)
        HT = NN[:, :].rearrange("p (c n) -> p c n", n=NP)
        AS = sb("AS", [P, HC * WIDE])
        AT = AS[:, :].rearrange("p (c n) -> p c n", n=WIDE)
        rows = sb("rows", [P, U, HID])
        VB = sb("VB", [P, WIDE])
        WA = sb("WA", [P, 5120])
        WB = sb("WB", [P, 3072])
        onehot = sb("onehot", [P, 2 * U, P])
        src_i = sb("src_i", [P, C + U], I32)
        cur = sb("cur", [P, 2 * U], I32)
        rel = sb("rel", [P, C + U])
        wgt = sb("wgt", [P, C + U])
        base_i = sb("base_i", [1, ROUNDS], I32)
        first_base = sb("first_base", [1, ROUNDS], mybir.dt.uint16)
        passes_i = sb("passes_i", [1, 1], I32)
        ident = sb("ident", [P, P])
        ones = sb("ones", [P, P])
        iota_w = sb("iota_w", [P, P])
        small = sb("small", [P, 896])
        bias_b = sb("bias_b", [P, D])

        ps = [ctx.enter_context(nc.psum_tensor(f"ps{i}", [P, 512], F32)) for i in range(8)]
        TA, EDGE, TV, PACC = ps[0:3], ps[3:5], ps[5:7], ps[7]

        stats = small[:, 0:150].rearrange("p (t s) -> p t s", s=6)
        mv = small[:, 150:200].rearrange("p (t s) -> p t s", s=2)
        rstd = small[:, 200:225]
        valid = small[:, 225:250]
        iota_p = small[:, 250:251]
        sc = small[:, 256:640]
        eps_c = small[:, 251:253]
        cols = small[:, 640:896]

        table = [nc.dram_tensor(f"table{i}", (NP, HID if i == 3 else D), F32, kind="Internal").ap()
                 for i in range(4)]

        pa_full, pa_free = sem("pa_full"), sem("pa_free")
        pv_full, pv_free = sem("pv_full"), sem("pv_free")
        dve_step, act_step, pool_step = sem("dve_step"), sem("act_step"), sem("pool_step")
        x_zeroed, x_loaded = sem("x_zeroed"), sem("x_loaded")
        edges_loaded, dst_loaded = sem("edges_loaded"), sem("dst_loaded")
        wa_loaded = [sem("wa0_loaded"), sem("wa1_loaded")]
        wb_loaded = sem("wb_loaded")
        ranges_ready, range_mm, diag_ready = sem("ranges_ready"), sem("range_mm"), sem("diag_ready")
        xn_ready, nt_ready = sem("xn_ready"), sem("nt_ready")
        edge_wait = sem("edge_wait")
        idx_ready = [sem(f"idx_ready{h}") for h in range(4)]
        gathered = [[sem(f"gathered{h}_{k}") for k in range(U)] for h in range(4)]
        onehot_ready = [sem(f"onehot_ready{h}") for h in range(5)]
        product_done = [sem(f"product_done{h}") for h in range(5)]
        added = [sem(f"added{h}") for h in range(5)]
        pass_ready = [sem(f"pass_ready{h}") for h in range(5)]
        table_sbuf = [sem(f"table_sbuf{h}") for h in range(4)]
        table_written = [sem(f"table_written{h}") for h in range(3)]
        quad_written = [sem("even_quad_written"), sem("odd_quad_written")]
        at_ready = sem("at_ready")
        out_stored = sem("out_stored")
        stored_ready = sem("stored_ready")
        kv_ready, kv_normed, kv_used = sem("kv_ready"), sem("kv_normed"), sem("kv_used")
        wkv_centred = sem("wkv_centred")
        mix_mm, mix_sb = sem("mix_mm"), sem("mix_sb")
        bias_loaded = sem("bias_loaded")
        route_mm, route_sb = sem("route_mm"), sem("route_sb")
        expert_loaded = sem("expert_loaded")
        w2_scaled, w2b_loaded = sem("w2_scaled"), sem("w2b_loaded")
        w2a_loaded, q_normed, q_in = sem("w2a_loaded"), sem("q_normed"), sem("q_in")
        rn_ready, norm_asked = sem("rn_ready"), sem("norm_asked")
        experts_loaded = [sem("experts0_loaded"), sem("experts1_loaded")]
        experts_gathered = [sem("expert0_gathered"), sem("expert1_gathered")]
        idx0_ready = sem("idx0_ready")
        cols_loaded, b2_loaded = sem("cols_loaded"), sem("b2_loaded")
        w1_loaded, w1_used = sem("w1_loaded"), sem("w1_used")
        qk_ready, stream_ready, w2_gathered = sem("qk_ready"), sem("stream_ready"), sem("w2_gathered")
        degree_ready, degree_mm, rows_scaled = sem("degree_ready"), sem("degree_mm"), sem("rows_scaled")
        slice_ready, relu_ready = sem("slice_ready"), sem("relu_ready")
        asked, answered = sem("asked"), sem("answered")

        def load(eng, dst, src, s):
            eng.dma_start(dst, src).then_inc(s, 16)

        block = ctx.enter_context(nc.Block())

        wkvT = WA[:, 0:2048].rearrange("p (c n) -> p c n", n=1024)
        wq = WA[:, 2048:3072].rearrange("p (j f) -> p j f", f=D)
        woT = WA[:, 3072:4096].rearrange("p (j f) -> p j f", f=D)
        wgT = WA[:, 4096:4608].rearrange("p (c f) -> p c f", f=D)
        mixM = WA[:, 4608:5120].rearrange("p (c f) -> p c f", f=D)
        w1g = WA[:, 0:2048].rearrange("p (e c f) -> p e c f", c=KC, f=HID)
        w2g = WA[:, 2048:4096].rearrange("p (e c f) -> p e c f", c=HC, f=D)
        hG = AS[:, 0:2 * 8 * GROUP * P].rearrange("p (b c n) -> p b c n", c=8, n=GROUP * P)
        rflat = rows[:, :, :].rearrange("p u d -> p (u d)")
        b2g = rflat[:, 0:512].rearrange("p (e f) -> p e f", f=D)
        gamma_b, beta_b, b2c = rflat[:, 512:768], rflat[:, 768:1024], rflat[:, 1024:1280]
        ybar = rflat[:, 1280:1536].rearrange("p (c m) -> p c m", m=P)
        w1a = WA[:, 0:1024].rearrange("p (c f) -> p c f", f=HID)
        w1b = WA[:, 1024:3072].rearrange("p (c f) -> p c f", f=HID)
        w2a = WA[:, 3072:5120].rearrange("p (c f) -> p c f", f=HID)
        w2b = WA[:, 0:1024].rearrange("p (c f) -> p c f", f=D)
        wqkv = WB[:, 0:768].rearrange("p (c f) -> p c f", f=3 * HD1)
        wout1 = WB[:, 768:1024]
        memk, memv = WB[0:MEM, 1024:1152], WB[0:MEM, 1152:1280]
        gout_b, bout_b, b2b_b = WB[:, 1280:1536], WB[:, 1536:1792], WB[:, 1792:2048]
        rw1 = WB[:, 2048:2304].rearrange("p (c f) -> p c f", f=P)
        rw2 = WB[:, 2304:2304 + E1]
        b3 = WB[0:E1, 2560:2816]
        mixb_b = WB[:, 2816:3072]
        kv1 = AS[:, 2 * WIDE:2 * WIDE + 2 * NP].rearrange("p (s t c) -> p s t c", s=2, c=HD1)
        Y = AS[:, 2 * WIDE:2 * WIDE + T * D].rearrange("p (t d) -> p t d", d=D)
        qT = VB[:, 0:NP]
        W3 = WA[:, 3072:5120]
        junk = W3[:, 0:256]
        kmax, diag1, ctx_bd = W3[:, 256:384], W3[:, 384:512], W3[:, 512:640]
        m2 = W3[:, 640:896]
        rn = W3[:, 896:896 + T]
        q1 = W3[:, 1024:1280].rearrange("p (b c) -> p b c", b=2)
        we = WA[:, 0:3072].rearrange("p (b l c f) -> p b l c f", b=2, l=3, f=D)
        N3 = AS[:, 0:T * D].rearrange("p (t d) -> p t d", d=D)
        h1 = AS[:, 0:KC * NP].rearrange("p (c n) -> p c n", n=NP)
        h2 = AS[:, KC * NP:2 * KC * NP].rearrange("p (c n) -> p c n", n=NP)
        wT = rflat[0:E1, 0:NP]
        route = [WA[:, 3072 + 150 * i:3222 + 150 * i].rearrange("p (t e) -> p t e", e=E1) for i in range(6)]
        rcol = [WA[:, 4000 + 32 * i:4000 + 32 * i + T] for i in range(8)]
        memkT, gpre = cols[:, 0:4], cols[:, 4:6]
        b1a, b1b, b2a = cols[:, 6:10], cols[:, 10:14], cols[:, 14:18]
        eb1, eb2 = cols[:, 18:30], cols[:, 30:42]
        rb1, rb2 = cols[:, 42:43], cols[:, 43:49]
        wr = cols[:, 49:65].rearrange("p (c e) -> p c e", e=E0)
        br = cols[:, 65:73]
        eps_in = cols[:, 73:75]
        b1g = cols[:, 80:88]
        gidx = cols[:, 96:112].bitcast(I32)
        iota4, iota6 = cols[:, 112:116], cols[:, 116:122]
        V_GNN0, V_FFN0 = 1 + 2 * T, 1 + 3 * T
        DEGREE_BANKS = -(-T // 4)
        A_HOP1 = T + DEGREE_BANKS + 2 * T
        ROUND_OUT = T + 10
        assert ROUND_OUT + T // 2 + 3 < ROUNDS
        A_MIX1 = T + DEGREE_BANKS + 2 * T + 4 + KC + T + T + GROUPS * 16 + T

        def out_of_ring(t):
            return A_MIX1 + max(1, 2 * t)
        V_MIX1 = V_FFN0 + 3 + T
        V_GNN1 = V_MIX1 + T
        V_B3 = V_GNN1 + T
        A2 = AS[:, 2 * WIDE:4 * WIDE]
        onehot16 = onehot[:, 0:U, :].rearrange("p u n -> p (u n)").bitcast(BF16).rearrange("p (b u n) -> p b u n", b=2, n=P)
        rel16, iota16 = A2[:, 0:(C + U) // 2].bitcast(F16), A2[:, 512:512 + P // 2].bitcast(F16)
        wflat = A2[:, 640:640 + (PARTS * C + P) // 2].bitcast(BF16)
        wparts = wflat[:, 0:PARTS * C].rearrange("p (c s) -> p c s", s=PARTS)
        wrest = A2[:, 2048:2048 + C]
        dnode = cols[:, 128:128 + 3 * T]
        R = A2[:, 0:T * D].rearrange("p (t d) -> p t d", d=D)
        kv = A2[:, 0:2048].rearrange("p (b n) -> p b n", n=1024)
        kvsq = A2[:, 2048:4096].rearrange("p (b n) -> p b n", n=1024)
        pj = A2[:, 4096:5120].rearrange("p (j f) -> p j f", f=D)
        bdT = A2[:, 5120:5632].rearrange("p (j d) -> p j d", d=P)

        QUADS = -(-T // 4)
        TABLE_DMAS = [2, GROUPS, GROUPS]

        def hop_width(h):
            return HC if h == 4 else KC

        A_ROWS = T * 3 // 5

        def rows_of_table(i, first, last):
            return table[i][first * P:last * P, :].rearrange("(t p) d -> p t d", p=P)

        def slice_of(s):
            return slice(s * SL, min((s + 1) * SL, NODES))

        def tiles_of(s):
            return [t for t in range(T) if ((t + 1) * P - 1) // SL == s]

        def group(g):
            return range(g * GROUP, (g + 1) * GROUP)

        @block.sync
        def _(sp):
            load(sp, src_i[:, :], a["src_pc"], edges_loaded)
            load(sp, wgt[:, 0:C], a["wgt_pc"], edges_loaded)
            load(sp, rel[:, 0:C].bitcast(I32), a["dst_pc"], edges_loaded)
            load(sp, AS[0:ROUNDS, 0:U * P].bitcast(I32), a["dst_rounds"], dst_loaded)
            sp.wait_ge(x_zeroed, 1)
            load(sp, X[:, 0:T - 1, :], a["x"][0:(T - 1) * P, :].rearrange("(t p) d -> p t d", p=P), x_loaded)
            load(sp, X[0:LAST, T - 1, :], a["x"][(T - 1) * P:NODES, :], x_loaded)
            load(sp, WA[:, 0:2048], a["wkvT"], wa_loaded[0])
            load(sp, WA[:, 2048:3072], a["wq"], wa_loaded[0])
            load(sp, WA[:, 3072:4096], a["woT"], wa_loaded[0])
            load(sp, WA[:, 4096:4608], a["wgT"], wa_loaded[0])
            load(sp, bias_b[:, :], a["L0_gnn_b"].partition_broadcast(P), bias_loaded)
            load(sp, mixb_b, a["L0_mix_b_out"].partition_broadcast(P), bias_loaded)
            load(sp, cols[:, 0:75], a["cols"], cols_loaded)
            for dst, src in ((WB[:, 0:768], "wqkv1"), (wout1, "L1_mix_w_out"), (memk, "memk"), (memv, "memv"),
                             (WB[:, 2048:2304], "rw1"), (rw2, "L1_ffn_router_w2"), (b3, "L1_ffn_expert_b3")):
                load(sp, dst, a[src], wb_loaded)
            for dst, src in ((gout_b, "L1_mix_g_out"), (bout_b, "L1_mix_b_out"), (b2b_b, "L1_gnn_b2b")):
                load(sp, dst, a[src].partition_broadcast(P), wb_loaded)
            sp.wait_ge(table_sbuf[0], A_ROWS)
            load(sp, rows_of_table(0, 0, A_ROWS), R[:, 0:A_ROWS, :], table_written[0])
            sp.wait_ge(rows_scaled, T - A_ROWS)
            load(sp, rows_of_table(0, A_ROWS, T), R[:, A_ROWS:T, :], table_written[0])
            for g in range(GROUPS):
                sp.wait_ge(table_sbuf[1], (g + 1) * GROUP)
                load(sp, rows_of_table(1, g * GROUP, (g + 1) * GROUP), N[:, g * GROUP:(g + 1) * GROUP, :], table_written[1])
            sp.wait_ge(pv_full, V_GNN0)
            load(sp, gamma_b, a["L0_ffn_gamma"].partition_broadcast(P), b2_loaded)
            load(sp, beta_b, a["L0_ffn_beta"].partition_broadcast(P), b2_loaded)
            sp.wait_ge(pv_full, V_FFN0)
            load(sp, WA[:, 0:1024], a["w1a"], w1_loaded)
            load(sp, WA[:, 1024:3072], a["w1b"], w1_loaded)
            for g in range(GROUPS):
                sp.wait_ge(xn_ready, 2 * T + (g + 1) * GROUP)
                load(sp, rows_of_table(2, g * GROUP, (g + 1) * GROUP), N[:, g * GROUP:(g + 1) * GROUP, :], table_written[2])
            sp.wait_ge(stream_ready, 1)
            load(sp, WA[:, 3072:5120], a["w2a"], w2a_loaded)
            for q in range(QUADS):
                n = min(4, T - 4 * q)
                sp.wait_ge(table_sbuf[3], 4 * q + n)
                load(sp, rows_of_table(3, 4 * q, 4 * q + n), rows[:, 4 * (q % 2):4 * (q % 2) + n, :], quad_written[q % 2])
            sp.wait_ge(w1_used, 1)
            load(sp, WA[:, 0:1024], a["w2b"], w2b_loaded)
            for e in range(E1):
                sp.wait_ge(pv_full, V_GNN1 if e < 2 else V_B3 + T * (e - 1))
                load(sp, WA[:, (e % 2) * 1536:(e % 2) * 1536 + 1536], a["experts1"][e], experts_loaded[e % 2])
            for g in range(GROUPS):
                first, last = g * GROUP, min((g + 1) * GROUP, T - 1)
                sp.wait_ge(stored_ready, g + 1)
                load(sp, out[first * P:last * P, :].rearrange("(t p) d -> p t d", p=P), X[:, first:last, :], out_stored)
            load(sp, out[(T - 1) * P:NODES, :], X[0:LAST, T - 1, :], out_stored)
            sp.wait_ge(out_stored, 16 * (GROUPS + 1))

        def gather_pass(pool, h):
            if h < 4:
                pool.wait_ge(table_written[h - 1], 16 * TABLE_DMAS[h - 1])
            else:
                for odd in range(2):
                    pool.wait_ge(quad_written[odd], 16 * len(range(odd, QUADS, 2)))
            pool.wait_ge(ranges_ready, 2)
            windows = pool.value_load(passes_i[0:1, 0:1], min_val=1, max_val=T)
            with pool.Fori(0, windows) as w:
                with pool.Fori(0, ROUNDS // 2) as i:
                    for j in range(2):
                        r = pool.snap(w * ROUNDS + i * 2 + j)
                        for half in range(2):
                            if half == 0:
                                pool.wait_ge(idx_ready[h - 1], r + 1)
                            pool.wait_ge(product_done[h], r * U + half * 4 + 4)
                            pool.sem_inc(edge_wait, 1)
                            for k in range(half * 4, half * 4 + 4):
                                nc.gpsimd.indirect_dma_start(
                                    rows[:, k, 0:hop_width(h) * P], None, table[h - 1][:, :],
                                    bass.IndirectOffsetOnAxis(cur[:, j * U + k:j * U + k + 1], 0)).then_inc(gathered[h - 1][k], 16)

        def product_pass(pe, h, side=None):
            def one_round(r, j, hots):
                pe.wait_ge(added[h], r + 1)
                for k in range(U):
                    pe.wait_ge(onehot_ready[h], hots + k + 1)
                    pe.wait_ge(gathered[h - 1][k], r * 16 + 16)
                    for c in range(hop_width(h)):
                        mm = nc.tensor.matmul(EDGE[j][:, c * P:(c + 1) * P], rows[:, k, c * P:(c + 1) * P],
                                              onehot[:, j * U + k, :], start=(k == 0 and c == 0), stop=(k == U - 1),
                                              skip_group_check=True)
                    mm.then_inc(product_done[h], 1)
                    if side:
                        side.get((r, k), lambda: None)()

            def window(w):
                with pe.Fori(0, ROUNDS // 2) as i:
                    for j in range(2):
                        one_round(pe.snap(w * ROUNDS + i * 2 + j), j, pe.snap(w * (C + U) + i * 2 * U + j * U))

            pe.sem_inc(product_done[h], U)
            pe.wait_ge(ranges_ready, 2)
            windows = pe.value_load(passes_i[0:1, 0:1], min_val=1, max_val=T)
            if side:
                for r in range(ROUNDS):
                    one_round(r, r % 2, r * U)
                side = None
                with pe.If(windows > 1):
                    with pe.Fori(1, windows) as w:
                        window(w)
            else:
                with pe.Fori(0, windows) as w:
                    window(w)

        def degree_products(pe):
            pe.sem_inc(product_done[0], 2)
            pe.wait_ge(ranges_ready, 2)
            windows = pe.value_load(passes_i[0:1, 0:1], min_val=1, max_val=T)
            with pe.Fori(0, windows) as w:
                with pe.Fori(0, ROUNDS // 2) as i:
                    for j in range(2):
                        pe.wait_ge(added[0], pe.snap(w * ROUNDS + i * 2 + j) + 1)
                        pe.wait_ge(onehot_ready[0], pe.snap(w * (ROUNDS + 1) + i * 2 + j) + 1)
                        for k in range(U):
                            mm = nc.tensor.matmul(EDGE[j][:, 0:P], wflat[:, bass.ds((i * 2 * U + j * U + k) * PARTS, P)],
                                                  onehot16[:, j, k, :], start=(k == 0), stop=(k == U - 1))
                        mm.then_inc(product_done[0], 1)

        def degree_sums(dve, st):
            dve.sem_inc(added[0], 2)
            windows = dve.value_load(passes_i[0:1, 0:1], min_val=1, max_val=T)
            def one_hots(chunk, buffer):
                nc.vector.tensor_tensor(
                    onehot16[:, buffer, :, :], iota16.unsqueeze(1).to_broadcast([P, U, P]),
                    rel16[:, bass.ds(chunk, U)].unsqueeze(2).to_broadcast([P, U, P]), ALU.is_equal).then_inc(onehot_ready[0], 1)

            with dve.Fori(0, windows) as w:
                nc.vector.tensor_scalar(rel16[:, 0:C], rel[:, 0:C], iota_w[:, 0:1], None, ALU.subtract).then_inc(pass_ready[0], 1)
                dve.wait_ge(pass_ready[0], w * 3 + 1)
                one_hots(0, 0)
                with dve.Fori(0, ROUNDS // 2) as i:
                    for j in range(2):
                        r = dve.snap(w * ROUNDS + i * 2 + j)
                        dve.wait_ge(product_done[0], r + 2)
                        dve.wait_ge(onehot_ready[0], r + 1)
                        one_hots(i * 2 * U + (j + 1) * U, 1 - j)
                        b = dve.value_load(base_i[0:1, bass.ds(i * 2 + j, 1)], min_val=0, max_val=NP)
                        dve.wait_ge(added[0], r + 2)
                        dve.wait_ge(product_done[0], r + 3)
                        win = VB[0:PARTS, bass.ds(b, P)]
                        nc.vector.tensor_tensor(win, win, EDGE[j][0:PARTS, 0:P], ALU.add).then_inc(added[0], 1)
                dve.wait_ge(onehot_ready[0], w * (ROUNDS + 1) + ROUNDS + 1)
                nc.vector.tensor_scalar(iota_w[:, :], iota_w[:, :], float(P), None, ALU.add).then_inc(pass_ready[0], 1)
                dve.wait_ge(pass_ready[0], w * 3 + 2)
                nc.vector.tensor_scalar(base_i[:, :], base_i[:, :], P, NP, ALU.add, ALU.min).then_inc(pass_ready[0], 1)
                dve.wait_ge(pass_ready[0], w * 3 + 3)
            dve.wait_ge(added[0], 2 + ROUNDS)

        def first_sources(h):
            nc.vector.tensor_copy(cur[:, 0:U], src_i[:, 0:U]).then_inc(idx_ready[h - 1], 1)

        def add_pass(dve, st, h, side=None):
            nch = hop_width(h)

            def one_hots(row, buffer, r=None):
                for k in range(U):
                    c = row * U + k
                    if r is not None:
                        dve.wait_ge(product_done[h], r * U + k + 1)
                    nc.vector.tensor_scalar(onehot[:, buffer * U + k, :], iota_w[:, :], rel[:, bass.ds(c, 1)], wgt[:, bass.ds(c, 1)],
                                            ALU.is_equal, ALU.mult).then_inc(onehot_ready[h], 1)

            def one_round(r, row, j):
                one_hots(row + 1, 1 - j, r)
                nc.vector.tensor_copy(cur[:, (1 - j) * U:(2 - j) * U], src_i[:, bass.ds((row + 1) * U, U)]).then_inc(idx_ready[h - 1], 1)
                b = dve.value_load(base_i[0:1, bass.ds(row, 1)], min_val=0, max_val=NP)
                dve.wait_ge(added[h], r + 2)
                dve.wait_ge(product_done[h], r * U + 2 * U)
                win = AT[:, 0:nch, bass.ds(b, P)]
                nc.vector.tensor_tensor(win, win, EDGE[j][:, 0:nch * P].rearrange("p (c n) -> p c n", n=P),
                                        ALU.add).then_inc(added[h], 1)

            def window(w):
                one_hots(0, 0)
                with dve.Fori(0, ROUNDS // 2) as i:
                    for j in range(2):
                        one_round(dve.snap(w * ROUNDS + i * 2 + j), i * 2 + j, j)

            def next_window(w):
                dve.wait_ge(onehot_ready[h], w * (C + U) + C + U)
                dve.sem_inc(edge_wait, 1)
                nc.vector.tensor_scalar(iota_w[:, :], iota_w[:, :], float(P), None, ALU.add).then_inc(pass_ready[h], 1)
                dve.wait_ge(pass_ready[h], w * 2 + 1)
                nc.vector.tensor_scalar(base_i[:, :], base_i[:, :], P, NP, ALU.add, ALU.min).then_inc(pass_ready[h], 1)
                dve.wait_ge(pass_ready[h], w * 2 + 2)

            st.add(nc.vector.tensor_copy(base_i[:, :], first_base[:, :]))
            st.do(nc.vector.tensor_copy(sc[:, 26:27], iota_w[:, 0:1]))
            st.do(nc.vector.tensor_scalar(iota_w[:, :], iota_w[:, :], sc[:, 26:27], None, ALU.subtract))
            dve.sem_inc(added[h], 2)
            windows = dve.value_load(passes_i[0:1, 0:1], min_val=1, max_val=T)
            if side:
                one_hots(0, 0)
                for r in range(ROUNDS):
                    one_round(r, r, r % 2)
                    side.get(r, lambda: None)()
                next_window(0)
                with dve.If(windows > 1):
                    with dve.Fori(1, windows) as w:
                        window(w)
                        next_window(w)
            else:
                with dve.Fori(0, windows) as w:
                    window(w)
                    next_window(w)
            dve.wait_ge(added[h], 2 + ROUNDS)
            if h < 4:
                first_sources(h + 1)

        @block.gpsimd
        def _(pool):
            st = Steps(pool, pool_step)
            nc.gpsimd.memset(X[:, T - 1, :], 0.0).then_inc(x_zeroed, 1)
            st.add(nc.gpsimd.memset(ident[:, :], 1.0))
            st.add(nc.gpsimd.memset(ones[:, :], 1.0))
            st.do(nc.gpsimd.memset(valid, 1.0))
            st.add(nc.gpsimd.affine_select(out=ident[:, :], in_=ident[:, :], compare_op=ALU.is_equal, fill=0.0,
                                           base=0, pattern=[[-1, P]], channel_multiplier=1))
            st.add(nc.gpsimd.affine_select(out=valid, in_=valid, compare_op=ALU.is_ge, fill=0.0,
                                           base=NODES - 1, pattern=[[-P, T]], channel_multiplier=-1))
            st.add(nc.gpsimd.iota(iota_w[:, :], pattern=[[1, P]], base=0, channel_multiplier=0,
                                  allow_small_or_imprecise_dtypes=True))
            st.add(nc.gpsimd.iota(iota_p, pattern=[[0, 1]], base=0, channel_multiplier=1,
                                  allow_small_or_imprecise_dtypes=True))
            pool.wait_ge(cols_loaded, 16)
            st.add(nc.gpsimd.iota(iota4, pattern=[[P, 4]], base=0, channel_multiplier=1,
                                  allow_small_or_imprecise_dtypes=True))
            st.add(nc.gpsimd.iota(iota6, pattern=[[1, E1]], base=0, channel_multiplier=0,
                                  allow_small_or_imprecise_dtypes=True))
            st.settle()
            gather_pass(pool, 1)
            gather_pass(pool, 2)
            pool.wait_ge(idx0_ready, 1)
            pool.wait_ge(pv_full, V_GNN0)
            pool.sem_inc(edge_wait, 1)
            def expert_rows(dst, src, column, s):
                nc.gpsimd.indirect_dma_start(dst, None, a[src][:, :], bass.IndirectOffsetOnAxis(
                    gidx[:, column:column + 1], 0)).then_inc(s, 16)

            for e in range(2):
                for c in range(KC):
                    expert_rows(w1g[:, e, c, :], "w1_rows", 8 * e + c, experts_gathered[e])
                expert_rows(b1g[:, 4 * e:4 * e + 4], "b1_rows", 8 * e + 6, experts_gathered[e])
            for e in range(2):
                for c in range(HC):
                    expert_rows(w2g[:, e, c, :], "w2_rows", 8 * e + 2 + c, w2_gathered)
                expert_rows(b2g[:, e, :], "b2_rows", 8 * e + 7, w2_gathered)
            gather_pass(pool, 3)
            gather_pass(pool, 4)

        @block.tensor
        def _(pe):
            A = Bank(pe, TA, pa_free, True)
            V = Bank(pe, TV, pv_free, True)
            pe.wait_ge(pool_step, 7)
            pe.wait_ge(diag_ready, 1)
            nc.tensor.matmul(PACC[:, 0:ROUNDS], ones[0:ROUNDS, :], sc[0:ROUNDS, 0:ROUNDS],
                             start=True, stop=True).then_inc(range_mm, 1)
            pe.wait_ge(diag_ready, 2)
            nc.tensor.transpose(V.next()[0:1, 0:ROUNDS], sc[0:ROUNDS, 82:83], ident[0:ROUNDS, 0:ROUNDS]).then_inc(pv_full, 1)

            def normalised_transposed(first, g, src=N):
                for t in group(g):
                    pe.wait_ge(xn_ready, first * T + t + 1)
                    o = A.next()
                    for c in range(KC):
                        mm = nc.tensor.transpose(o[:, c * P:(c + 1) * P], src[:, t, c * P:(c + 1) * P], ident[:, :])
                    mm.then_inc(pa_full, 1)

            degree_products(pe)
            pe.wait_ge(degree_ready, 1)
            for t in range(T):
                mm = nc.tensor.transpose(PACC[:, t * PARTS:(t + 1) * PARTS], VB[0:PARTS, t * P:(t + 1) * P], ident[0:PARTS, 0:PARTS])
            mm.then_inc(degree_mm, 1)
            pe.wait_ge(degree_ready, 2)
            for q in range(0, T, 4):
                o = A.next()
                for t in range(q, min(q + 4, T)):
                    mm = nc.tensor.transpose(o[:, (t - q) * P:(t - q + 1) * P], dnode[:, t:t + 1].to_broadcast([P, P]), ident[:, :])
                mm.then_inc(pa_full, 1)
            for g in range(GROUPS):
                normalised_transposed(0, g)

            kv_bank = [None]

            def keys_and_values(t, half, c):
                if t == 0:
                    pe.wait_ge(wkv_centred, 1)
                    pe.wait_ge(nt_ready, T)
                if c == 0:
                    kv_bank[0] = A.next()
                mm = nc.tensor.matmul(kv_bank[0][:, :], NT[:, c, t * P:(t + 1) * P], wkvT[:, c, half * 512:(half + 1) * 512],
                                      start=(c == 0), stop=(c == KC - 1))
                if c == KC - 1:
                    mm.then_inc(pa_full, 1)

            def head_products(t, first):
                if first == 0:
                    pe.wait_ge(kv_normed, t + 1)
                for j in range(first, first + 2):
                    mm = nc.tensor.matmul(PACC[:, j * P:(j + 1) * P], kv[:, t % 2, 512 + j * P:512 + (j + 1) * P],
                                          kv[:, t % 2, j * P:(j + 1) * P], start=(t == 0 and j == 0),
                                          stop=(t == T - 1), skip_group_check=True)
                if first == 2:
                    mm.then_inc(kv_used, 1)

            beside_hop1 = {}
            for t in range(T):
                for half in range(2):
                    for c in range(KC):
                        beside_hop1[2 * t + half, 1 + 4 * c] = lambda t=t, half=half, c=c: keys_and_values(t, half, c)
                    beside_hop1[2 * t + 3, 3 + 4 * half] = lambda t=t, half=half: head_products(t, 2 * half)
            assert max(beside_hop1)[0] < ROUNDS

            def heads_by_output():
                pe.wait_ge(mix_sb, 1)
                for j in range(4):
                    o = A.next()
                    nc.tensor.matmul(o[:, 0:D], bdT[:, j, :], woT[:, j, :], start=True, stop=True).then_inc(pa_full, 1)

            def queries_by_heads():
                pe.wait_ge(mix_sb, 5)
                for c in range(KC):
                    o = A.next()
                    for j in range(4):
                        mm = nc.tensor.matmul(o[:, 0:D], wq[:, j, c * P:(c + 1) * P], pj[:, j, :], start=(j == 0), stop=(j == 3))
                    mm.then_inc(pa_full, 1)

            product_pass(pe, 1, beside_hop1)
            for t in range(T):
                if t % GROUP == 0:
                    pe.wait_ge(slice_ready, t // GROUP + 1)
                o = A.next()
                for c in range(KC):
                    mm = nc.tensor.transpose(o[:, c * P:(c + 1) * P], AT[:, c, t * P:(t + 1) * P], ident[:, :])
                mm.then_inc(pa_full, 1)
            def attention_product(t):
                if t == 0:
                    pe.wait_ge(mix_sb, 6)
                o = V.next()
                for c in range(KC):
                    mm = nc.tensor.matmul(o[:, 0:D], NT[:, c, t * P:(t + 1) * P], mixM[:, c, :], start=(c == 0), stop=(c == KC - 1))
                mm.then_inc(pv_full, 1)

            beside_hop2 = {(2 * t + 2, 3): lambda t=t: attention_product(t) for t in range(T)}
            beside_hop2[0, 1], beside_hop2[0, 5] = heads_by_output, queries_by_heads
            product_pass(pe, 2, beside_hop2)

            def hops_out(t):
                if t % GROUP == 0:
                    pe.wait_ge(relu_ready, t // GROUP + 1)
                o = V.next()
                for c in range(KC):
                    mm = nc.tensor.matmul(o[:, 0:D], AT[:, c, t * P:(t + 1) * P], wgT[:, c, :], start=(c == 0), stop=(c == KC - 1))
                mm.then_inc(pv_full, 1)

            for s in range(GROUPS + 2):
                if s < GROUPS:
                    for t in group(s):
                        hops_out(t)
                if s >= 2:
                    normalised_transposed(1, s - 2)
                    for t in group(s - 2):
                        for c in range(KC):
                            mm = nc.tensor.matmul(PACC[:, c:c + 1], N[:, t, c * P:(c + 1) * P], valid[:, t:t + 1],
                                                  start=(t == 0 and c == 0), stop=(t == T - 1), skip_group_check=True)
            mm.then_inc(route_mm, 1)

            pe.wait_ge(route_sb, 1)
            pe.wait_ge(cols_loaded, 16)
            for c in range(KC):
                mm = nc.tensor.matmul(PACC[:, 8:8 + E0], ybar[:, c, :], wr[:, c, :], start=(c == 0), stop=(c == KC - 1))
            mm.then_inc(route_mm, 1)
            pe.wait_ge(nt_ready, 2 * T)
            first_done = [0] * GROUPS
            for g in range(GROUPS + 1):
                if g < GROUPS:
                    for c in range(8):
                        if g == 0 and c % 4 == 0:
                            pe.wait_ge(experts_gathered[c // 4], 16 * (KC + 1))
                        for half in range(2):
                            o = A.next()
                            n0 = g * GN + half * HALF
                            n = min(HALF, NODES - n0)
                            for k in range(KC):
                                mm = nc.tensor.matmul(o[:, 0:n], w1g[:, c // 4, k, (c % 4) * P:(c % 4 + 1) * P],
                                                      NT[:, k, n0:n0 + n], start=(k == 0), stop=(k == KC - 1))
                            mm.then_inc(pa_full, 1)
                    first_done[g] = A.n
                if g >= 1:
                    pe.wait_ge(pa_free, first_done[g - 1])
                    if g == 1:
                        pe.wait_ge(w2_scaled, 1)
                    for t in range(GROUP):
                        o = V.next()
                        for c in range(8):
                            mm = nc.tensor.matmul(o[:, 0:D], hG[:, (g - 1) % 2, c, t * P:(t + 1) * P], w2g[:, c // 4, c % 4, :],
                                                  start=(c == 0), stop=(c == 7))
                        mm.then_inc(pv_full, 1)
                if g >= 4:
                    normalised_transposed(2, g - 4)
            assert V.n == V_FFN0 and GROUPS > 4

            for g in range(GROUPS - 3, GROUPS):
                normalised_transposed(2, g)
            pe.wait_ge(mix_sb, 7)
            pe.wait_ge(nt_ready, 3 * T)

            qkv_bank = [None]

            def queries_keys_values(t, c):
                if c == 0:
                    qkv_bank[0] = A.next()
                mm = nc.tensor.matmul(qkv_bank[0][:, 0:3 * HD1], NT[:, c, t * P:(t + 1) * P], wqkv[:, c, :],
                                      start=(c == 0), stop=(c == KC - 1))
                if c == KC - 1:
                    mm.then_inc(pa_full, 1)

            def turn_queries(t):
                pe.wait_ge(q_normed, t + 1)
                nc.tensor.transpose(A.next()[:, 0:P], q1[:, t % 2, :], ident[:, :]).then_inc(pa_full, 1)

            def turn_maxima():
                pe.wait_ge(qk_ready, 1)
                nc.tensor.transpose(V.next()[:, 0:P], kmax, ident[:, :]).then_inc(pv_full, 1)

            def spread_maxima():
                pe.wait_ge(qk_ready, 2)
                nc.tensor.matmul(V.next()[:, 0:P], ones[:, :], diag1, start=True, stop=True).then_inc(pv_full, 1)

            def context(first, last):
                pe.wait_ge(qk_ready, 3)
                for t in range(first, last):
                    m = P if t < T - 1 else LAST
                    nc.tensor.matmul(PACC[:, 0:P], kv1[0:m, 1, t, :], kv1[0:m, 0, t, :], start=(t == 0), stop=False)
                if last == T:
                    nc.tensor.matmul(PACC[:, 0:P], memv, memk, start=False, stop=True)

            def key_sums():
                for t in range(T):
                    m = P if t < T - 1 else LAST
                    nc.tensor.matmul(PACC[:, P:P + 1], kv1[0:m, 0, t, :], ones[0:m, 0:1], start=(t == 0), stop=False)
                nc.tensor.matmul(PACC[:, P:P + 1], memk, ones[0:MEM, 0:1], start=False, stop=True).then_inc(mix_mm, 1)

            def context_out():
                pe.wait_ge(qk_ready, 4)
                nc.tensor.matmul(V.next()[:, 0:D], ctx_bd, wout1, start=True, stop=True).then_inc(pv_full, 1)

            def attention_out(t):
                if t == 0:
                    pe.wait_ge(qk_ready, 5)
                    pe.wait_ge(pa_free, A_MIX1 + 2 * T)
                nc.tensor.matmul(V.next()[:, 0:D], qT[:, t * P:(t + 1) * P], m2, start=True, stop=True).then_inc(pv_full, 1)

            beside_hop3 = {}
            for t in range(T):
                for c in range(KC):
                    beside_hop3[t, 2 * c] = lambda t=t, c=c: queries_keys_values(t, c)
                beside_hop3[t + 1, 7] = lambda t=t: turn_queries(t)
                beside_hop3[ROUND_OUT + t // 2, 1 + 4 * (t % 2)] = lambda t=t: attention_out(t)
            beside_hop3[T + 1, 0] = turn_maxima
            beside_hop3[T + 2, 0] = spread_maxima
            for n in range(5):
                beside_hop3[T + 4 + n // 2, 1 + 4 * (n % 2)] = lambda n=n: context(5 * n, 5 * n + 5)
            beside_hop3[T + 6, 5] = key_sums
            beside_hop3[T + 8, 0] = context_out

            def turn_hidden(t, ends):
                pe.wait_ge(pa_free, ends[((t + 1) * P - 1) // SL])
                o = A.next()
                for c in range(HC):
                    mm = nc.tensor.transpose(o[:, c * P:(c + 1) * P], AT[:, c, t * P:(t + 1) * P], ident[:, :])
                mm.then_inc(pa_full, 1)

            def wide(weights, src, chunks, ready, then=None):
                ends = []
                for s in range(SLICES):
                    if ready:
                        pe.wait_ge(pa_free, ready[s])
                    for c in range(weights.shape[2] // P):
                        o = A.next()
                        n = slice_of(s)
                        for k in range(chunks):
                            mm = nc.tensor.matmul(o[:, 0:n.stop - n.start], weights[:, k, c * P:(c + 1) * P], src[:, k, n],
                                                  start=(k == 0), stop=(k == chunks - 1))
                        mm.then_inc(pa_full, 1)
                    ends.append(A.n)
                    if then:
                        then(s, ends)
                return ends

            pe.wait_ge(at_ready, 1)
            product_pass(pe, 3, beside_hop3)
            assert V.n == V_MIX1 and A.n == A_MIX1 + 2 * T
            pe.wait_ge(w1_loaded, 32)
            pe.wait_ge(added[3], 2 + ROUNDS)
            pe.wait_ge(at_ready, 2)
            ends = wide(w1a, AT, KC, None)
            done = wide(w1b, HT, HC, ends, then=lambda s, ends: [turn_hidden(t, ends) for t in tiles_of(s - 1)])
            for t in tiles_of(SLICES - 1):
                turn_hidden(t, done)
            pe.sem_inc(w1_used, 1)
            pe.wait_ge(at_ready, 3)
            product_pass(pe, 4)
            pe.wait_ge(at_ready, 4)
            pe.wait_ge(w2a_loaded, 16)
            wide(w2a, AT, HC, None)
            pe.wait_ge(pa_free, A.n)
            pe.wait_ge(w2b_loaded, 16)

            def hidden_out(t):
                o = V.next()
                for c in range(HC):
                    mm = nc.tensor.matmul(o[:, 0:D], HT[:, c, t * P:(t + 1) * P], w2b[:, c, :], start=(c == 0), stop=(c == HC - 1))
                mm.then_inc(pv_full, 1)

            for t in range(T):
                hidden_out(t)
            assert V.n == V_GNN1

            for g in range(GROUPS):
                normalised_transposed(3, g, N3)
            pe.wait_ge(nt_ready, 4 * T)
            ends = wide(rw1, NT, KC, None)
            for t in range(T):
                pe.wait_ge(pa_free, ends[((t + 1) * P - 1) // SL])
                mm = nc.tensor.matmul(PACC[:, t * E1:(t + 1) * E1], VB[:, t * P:(t + 1) * P], rw2, start=True, stop=True)
            mm.then_inc(route_mm, 1)
            for e in range(E1):
                w = we[:, e % 2]
                pe.wait_ge(experts_loaded[e % 2], 16 * (e // 2 + 1))
                ends = wide(w[:, 0], NT, KC, None)
                ends = wide(w[:, 1], h1, KC, ends)
                if e == 0:
                    pe.wait_ge(route_sb, 2)
                    for q in range(0, T, 4):
                        o = A.next()
                        for t in range(q, min(q + 4, T)):
                            mm = nc.tensor.transpose(o[0:E1, (t - q) * P:(t - q + 1) * P], route[5][:, t, :], ident[:, :])
                        mm.then_inc(pa_full, 1)
                    pe.wait_ge(pa_free, A.n)
                    for t in range(T):
                        nc.tensor.matmul(V.next()[:, 0:D], wT[:, t * P:(t + 1) * P], b3, start=True, stop=True).then_inc(pv_full, 1)
                    assert V.n == V_B3
                for t in range(T):
                    pe.wait_ge(pa_free, ends[((t + 1) * P - 1) // SL])
                    o = V.next()
                    for k in range(KC):
                        mm = nc.tensor.matmul(o[:, 0:D], h2[:, k, t * P:(t + 1) * P], w[:, 2, k, :], start=(k == 0), stop=(k == KC - 1))
                    mm.then_inc(pv_full, 1)

        @block.scalar
        def _(act):
            A = Bank(act, TA, pa_full, False)
            st = Steps(act, act_step)
            roots = [0]

            def root(v):
                roots[0] += 1
                act.wait_ge(asked, roots[0])
                nc.scalar.activation(v, v, ACT.Sqrt).then_inc(answered, 1)

            def exp(v):
                roots[0] += 1
                act.wait_ge(asked, roots[0])
                nc.scalar.activation(v, v, ACT.Exp).then_inc(answered, 1)

            def transposed_copies(tiles):
                for t in tiles:
                    o = A.next()
                    nc.scalar.copy(NT[:, :, t * P:(t + 1) * P], o[:, 0:D].rearrange("p (c n) -> p c n", n=P)).then_inc(pa_free, 1)
                    act.wait_ge(pa_free, A.n)
                    act.sem_inc(nt_ready, 1)

            root(dnode[:, 0:T])
            root(rstd)
            act.wait_ge(degree_ready, 2)
            for t in range(A_ROWS):
                act.wait_ge(xn_ready, t + 1)
                nc.scalar.activation(R[:, t, :], N[:, t, :], ACT.Identity, scale=dnode[:, t:t + 1]).then_inc(table_sbuf[0], 1)
            for q in range(0, T, 4):
                n = (min(q + 4, T) - q) * P
                o = A.next()
                nc.scalar.copy(VB[:, q * P:q * P + n], o[:, 0:n]).then_inc(pa_free, 1)
            transposed_copies(range(T))
            act.wait_ge(table_written[0], 16 * TABLE_DMAS[0])

            for t in range(T):
                b = t % 2
                if t >= 2:
                    act.wait_ge(kv_used, t - 1)
                for half in range(2):
                    o = A.next()
                    part = slice(half * 512, (half + 1) * 512)
                    nc.scalar.copy(kv[:, b, part], o[:, :]).then_inc(kv_ready, 1)
                    nc.scalar.activation(kvsq[:, b, part], o[:, :], ACT.Square).then_inc(pa_free, 1)
                root(sc[:, 256 + 32 * b:256 + 32 * b + 16])
            act.wait_ge(degree_ready, 3)
            for t in range(T):
                o = A.next()
                nc.scalar.activation(N[:, t, :], o[:, 0:D], ACT.Identity, scale=dnode[:, 2 * T + t:2 * T + t + 1]).then_inc(pa_free, 1)
                act.wait_ge(pa_free, A.n)
                act.sem_inc(table_sbuf[1], 1)
            for j in range(4):
                o = A.next()
                nc.scalar.mul(pj[:, j, :], o[:, 0:D], 1.0 / NODES).then_inc(pa_free, 1)
            act.wait_ge(pa_free, A.n)
            act.sem_inc(mix_sb, 4)
            for c in range(KC):
                o = A.next()
                nc.scalar.copy(mixM[:, c, :], o[:, 0:D]).then_inc(pa_free, 1)
            act.wait_ge(pa_free, A.n)
            act.sem_inc(mix_sb, 1)
            for s in range(GROUPS + 2):
                if s < GROUPS:
                    act.wait_ge(slice_ready, GROUPS + s + 1)
                    part = AT[:, 0:KC, s * GN:(s + 1) * GN]
                    nc.scalar.activation(part, part, ACT.Relu).then_inc(relu_ready, 1)
                if 1 <= s <= GROUPS:
                    root(rstd[:, (s - 1) * GROUP:s * GROUP])
                if s >= 2:
                    transposed_copies(group(s - 2))

            exp(sc[:, 0:8])
            exp(sc[:, 0:8])
            exp(sc[:, 40:41])
            for g in range(GROUPS + 3):
                for c in range(8 if g < GROUPS else 0):
                    if g == 0 and c % 4 == 0:
                        act.wait_ge(experts_gathered[c // 4], 16 * (KC + 1))
                    for half in range(2):
                        o = A.next()
                        n = min(HALF, NODES - g * GN - half * HALF)
                        nc.scalar.activation(hG[:, g % 2, c, half * HALF:half * HALF + n], o[:, 0:n], ACT.Gelu,
                                             bias=b1g[:, c:c + 1]).then_inc(pa_free, 1)
                for n in (g - 3, g - 2):
                    if 0 <= n < GROUPS:
                        root(rstd[:, n * GROUP:(n + 1) * GROUP])
                if g >= 4:
                    transposed_copies(group(g - 4))
            transposed_copies(group(GROUPS - 1))

            def norms(src, n):
                for t in range(T):
                    if t:
                        st.settle()
                    st.add(nc.scalar.activation(junk, src[:, t, :], ACT.Square, accum_out=rn[:, t:t + 1]))
                st.settle()
                nc.scalar.activation(rn, rn, ACT.Sqrt).then_inc(norm_asked, 1)

            act.wait_ge(xn_ready, 3 * T)
            norms(N, 1)
            act.wait_ge(rn_ready, 1)
            for t in range(T + 1):
                if t < T:
                    o = A.next()
                    nc.scalar.activation(q1[:, t % 2, :], o[:, 0:HD1], ACT.Identity, scale=rn[:, t:t + 1]).then_inc(q_in, 1)
                    nc.scalar.activation(kv1[:, :, t, :], o[:, HD1:3 * HD1].rearrange("p (s c) -> p s c", c=HD1), ACT.Identity,
                                         scale=rn[:, t:t + 1]).then_inc(pa_free, 1)
                if t >= 1:
                    o = A.next()
                    nc.scalar.copy(qT[:, (t - 1) * P:t * P], o[:, 0:P]).then_inc(pa_free, 1)
                if t < T:
                    exp(q1[:, t % 2, :])
            exp(kv1[:, 0, :, :].rearrange("p t c -> p (t c)"))
            exp(memk)
            act.wait_ge(pv_free, V_MIX1)
            norms(Y, 2)

            def wide(dst, bias, chunks, then=None):
                for s in range(SLICES):
                    for c in range(chunks):
                        o = A.next()
                        n = slice_of(s)
                        nc.scalar.activation(dst[:, c, n], o[:, 0:n.stop - n.start], ACT.Relu,
                                             bias=bias[:, c:c + 1]).then_inc(pa_free, 1)
                    if then:
                        then(s)

            def hidden_rows(tiles):
                for t in tiles:
                    if t % 4 == 0 and t >= 8:
                        act.wait_ge(quad_written[t // 4 % 2], 16 * (t // 8))
                    o = A.next()
                    nc.scalar.copy(rows[:, t % 8, :], o[:, :]).then_inc(pa_free, 1)
                    act.wait_ge(pa_free, A.n)
                    act.sem_inc(table_sbuf[3], 1)

            act.wait_ge(table_written[2], 16 * TABLE_DMAS[2])
            act.wait_ge(at_ready, 2)
            wide(HT, b1a, HC)
            act.wait_ge(stream_ready, 1)
            wide(AT, b1b, HC, then=lambda s: hidden_rows(tiles_of(s - 1)))
            hidden_rows(tiles_of(SLICES - 1))
            wide(HT, b2a, HC)

            for g in range(GROUPS):
                root(rstd[:, g * GROUP:(g + 1) * GROUP])
            for g in range(GROUPS):
                transposed_copies(group(g))
            wide(VB[:, :].rearrange("p (c n) -> p c n", c=1), rb1, 1)
            exp(route[0].rearrange("p t e -> p (t e)"))
            for e in range(E1):
                wide(h1, eb1[:, 2 * e:2 * e + 2], KC)
                if e == 0:
                    exp(rcol[0])
                wide(h2, eb2[:, 2 * e:2 * e + 2], KC)
                if e == 0:
                    for q in range(0, T, 4):
                        n = (min(q + 4, T) - q) * P
                        o = A.next()
                        nc.scalar.copy(wT[:, q * P:q * P + n], o[0:E1, 0:n]).then_inc(pa_free, 1)

        @block.vector
        def _(dve):
            st = Steps(dve, dve_step)
            V = Bank(dve, TV, pv_full, False)

            dve.wait_ge(edges_loaded, 48)
            dve.wait_ge(dst_loaded, 16)
            dve.wait_ge(pool_step, 7)
            low, high = sc[0:ROUNDS, 80:81], sc[0:ROUNDS, 81:82]
            dstf = AS[0:ROUNDS, U * P:2 * U * P]
            st.add(nc.vector.memset(rel[:, C:C + U], 0.0))
            st.add(nc.vector.memset(wgt[:, C:C + U], 0.0))
            st.add(nc.vector.tensor_copy(rel[:, 0:C], rel[:, 0:C].bitcast(I32)))
            st.do(nc.vector.tensor_copy(dstf, AS[0:ROUNDS, 0:U * P].bitcast(I32)))
            st.add(nc.vector.tensor_reduce(low, dstf, AX, ALU.min))
            st.do(nc.vector.tensor_reduce(high, dstf, AX, ALU.max))
            nc.vector.tensor_scalar(sc[0:ROUNDS, 0:ROUNDS], ident[0:ROUNDS, 0:ROUNDS], low, None, ALU.mult).then_inc(diag_ready, 1)
            nc.vector.tensor_tensor(sc[0:ROUNDS, 82:83], high, low, ALU.subtract).then_inc(diag_ready, 1)
            dve.wait_ge(range_mm, 1)
            rel_r = rel[:, 0:C].rearrange("p (r k) -> p r k", k=U)
            st.add(nc.vector.tensor_tensor(rel_r, rel_r, PACC[:, 0:ROUNDS].unsqueeze(2).to_broadcast([P, ROUNDS, U]), ALU.subtract))
            st.do(nc.vector.tensor_copy(first_base[:, :], PACC[0:1, 0:ROUNDS]))
            nc.vector.tensor_copy(base_i[:, :], first_base[:, :]).then_inc(ranges_ready, 1)
            o = V.next()
            nc.vector.tensor_reduce(sc[0:1, 83:84], o[0:1, 0:ROUNDS], AX, ALU.max).then_inc(pv_free, 1)
            st.add(nc.vector.tensor_scalar(sc[0:1, 96:96 + T - 1], iota_w[0:1, 1:T], float(P), None, ALU.mult))
            dve.wait_ge(pv_free, V.n)
            st.settle()
            st.do(nc.vector.tensor_scalar(sc[0:1, 128:128 + T - 1], sc[0:1, 96:96 + T - 1], sc[0:1, 83:84], None, ALU.is_le))
            st.do(nc.vector.tensor_reduce(sc[0:1, 84:85], sc[0:1, 128:128 + T - 1], AX, ALU.add))
            nc.vector.tensor_scalar(passes_i[:, :], sc[0:1, 84:85], 1.0, None, ALU.add).then_inc(ranges_ready, 1)
            dve.wait_ge(ranges_ready, 2)
            first_sources(1)

            roots = [0]

            def one_over_root(v):
                roots[0] += 1
                dve.wait_ge(answered, roots[0])
                st.do(nc.vector.reciprocal(v, v))

            def stats_of(src, g):
                for t in group(g):
                    st.add(nc.vector.bn_stats(stats[:, t, :], src[:, t, :]))
                st.settle()
                for t in group(g):
                    st.add(nc.vector.bn_aggr(mv[:, t, :], stats[:, t, :]))
                st.settle()
                nc.vector.tensor_scalar(rstd[:, g * GROUP:(g + 1) * GROUP], mv[:, g * GROUP:(g + 1) * GROUP, 1],
                                        LN_EPS, None, ALU.add).then_inc(asked, 1)

            def normalised(src, g, ready=None, dst=N):
                one_over_root(rstd[:, g * GROUP:(g + 1) * GROUP])
                for t in group(g):
                    ins = nc.vector.tensor_scalar(dst[:, t, :], src[:, t, :], mv[:, t, 0:1], rstd[:, t:t + 1],
                                                  ALU.subtract, ALU.mult)
                    if ready is None:
                        st.add(ins)
                    else:
                        ins.then_inc(ready, 1)

            def degrees():
                st.add(nc.vector.memset(rel16, 0.0))
                st.add(nc.vector.memset(wflat, 0.0))
                st.add(nc.vector.memset(VB[0:PARTS, :], 0.0))
                st.add(nc.vector.tensor_copy(iota16, iota_w[:, :]))
                st.settle()
                st.add(nc.vector.memset(VB[0:1, :], 1.0))
                for part in range(3):
                    st.do(nc.vector.tensor_copy(wparts[:, :, part], wgt[:, 0:C] if part == 0 else wrest))
                    if part < 2:
                        st.do(nc.vector.tensor_tensor(wrest, wgt[:, 0:C] if part == 0 else wrest, wparts[:, :, part], ALU.subtract))
                degree_sums(dve, st)
                dve.sem_inc(degree_ready, 1)

            def first_statistics():
                dve.wait_ge(x_loaded, 32)
                for t in range(T):
                    st.add(nc.vector.bn_stats(stats[:, t, :], X[:, t, :]))
                st.settle()
                for t in range(T):
                    st.add(nc.vector.bn_aggr(mv[:, t, :], stats[:, t, :]))
                st.settle()

            def first_rows():
                dve.wait_ge(degree_mm, 1)
                st.do(nc.vector.tensor_reduce(dnode[:, 0:T], PACC[:, 0:PARTS * T].rearrange("p (t s) -> p t s", s=PARTS), AX, ALU.add))
                st.do(nc.vector.tensor_scalar(dnode[:, T:2 * T], dnode[:, 0:T], 0.0, None, ALU.is_gt))
                nc.vector.tensor_scalar(dnode[:, 0:T], dnode[:, 0:T], 1e-12, None, ALU.max).then_inc(asked, 1)
                nc.vector.tensor_scalar(rstd, mv[:, :, 1], LN_EPS, None, ALU.add).then_inc(asked, 1)
                one_over_root(dnode[:, 0:T])
                nc.vector.tensor_tensor(dnode[:, 0:T], dnode[:, 0:T], dnode[:, T:2 * T], ALU.mult).then_inc(degree_ready, 1)
                one_over_root(rstd)
                for t in range(T):
                    nc.vector.tensor_scalar(N[:, t, :], X[:, t, :], mv[:, t, 0:1], rstd[:, t:t + 1],
                                            ALU.subtract, ALU.mult).then_inc(xn_ready, 1)
                dve.wait_ge(degree_ready, 2)
                dve.wait_ge(xn_ready, T)
                for t in range(A_ROWS, T):
                    nc.vector.tensor_scalar(R[:, t, :], N[:, t, :], dnode[:, t:t + 1], None, ALU.mult).then_inc(rows_scaled, 1)
                nc.vector.tensor_scalar(dnode[:, 2 * T:3 * T], dnode[:, 0:T], 0.5, None, ALU.mult).then_inc(degree_ready, 1)

            def normalise_kv(t):
                b = t % 2
                dve.wait_ge(kv_ready, 2 * t + 2)
                dve.wait_ge(pa_free, DEGREE_BANKS + T + 2 * t + 2)
                ss = sc[:, 256 + 32 * b:256 + 32 * b + 16]
                st.do(nc.vector.tensor_reduce(ss, kvsq[:, b, :].rearrange("p (g d) -> p g d", d=DH0), AX, ALU.add))
                nc.vector.tensor_scalar(ss, ss, 1.0 / DH0, LN_EPS, ALU.mult, ALU.add).then_inc(asked, 1)
                one_over_root(ss)
                r = sc[:, 320 + 8 * b:328 + 8 * b]
                st.do(nc.vector.tensor_tensor(r, ss[:, 0:8], ss[:, 8:16], ALU.mult))
                vh = kv[:, b, 512:1024].rearrange("p (g d) -> p g d", d=DH0)
                nc.vector.tensor_tensor(vh, vh, r.unsqueeze(2).to_broadcast([P, H0, DH0]), ALU.mult).then_inc(kv_normed, 1)

            def head_products_out():
                st.do(nc.vector.memset(bdT, 0.0))
                dve.wait_ge(kv_used, T)
                for half in range(2):
                    s = slice(half * DH0, (half + 1) * DH0)
                    st.add(nc.vector.tensor_copy(bdT[s, :, s], PACC[s, :].rearrange("p (j d) -> p j d", d=P)[:, :, s]))
                st.settle()
                dve.sem_inc(mix_sb, 1)

            degrees()
            first_statistics()
            first_rows()
            dve.wait_ge(wa_loaded[0], 64)
            heads = WA[:, 0:2048].rearrange("p (g d) -> p g d", d=DH0)
            st.do(nc.vector.tensor_reduce(sc[:, 256:256 + 32], heads, AX, ALU.add))
            st.do(nc.vector.tensor_scalar(sc[:, 256:256 + 32], sc[:, 256:256 + 32], 1.0 / DH0, None, ALU.mult))
            nc.vector.tensor_tensor(heads, heads, sc[:, 256:256 + 32].unsqueeze(2).to_broadcast([P, 32, DH0]),
                                    ALU.subtract).then_inc(wkv_centred, 1)
            dve.wait_ge(bias_loaded, 32)
            st.do(nc.vector.tensor_tensor(bias_b[:, :], bias_b[:, :], mixb_b, ALU.add))
            st.do(nc.vector.memset(AT[:, 0:KC, NP:WIDE], 0.0))
            dve.wait_ge(nt_ready, T)
            dinv = VB[:, 0:NP]
            dve.wait_ge(pa_free, T + DEGREE_BANKS)
            for c in range(KC):
                st.add(nc.vector.tensor_tensor(AT[:, c, 0:NP], NT[:, c, :], dinv, ALU.mult))
            st.add(nc.vector.tensor_scalar(WA[:, 4096:4608], WA[:, 4096:4608], 0.5, None, ALU.mult))
            st.settle()

            def part_of(v, s):
                return v[:, :, s * GN:(s + 1) * GN]

            def dinv_of(s):
                return dinv[:, s * GN:(s + 1) * GN].unsqueeze(1).to_broadcast([P, KC, GN])

            def close_hop(s):
                at = part_of(AT[:, 0:KC, :], s)
                st.do(nc.vector.tensor_tensor(at, at, dinv_of(s), ALU.mult))
                nc.vector.tensor_tensor(at, at, part_of(NT, s), ALU.add).then_inc(slice_ready, 1)

            def add_bias(g):
                x = X[:, g * GROUP:(g + 1) * GROUP, :]
                st.do(nc.vector.tensor_tensor(x, x, bias_b[:, :].unsqueeze(1).to_broadcast([P, GROUP, D]), ALU.add))

            beside_hop1 = {2 * t + 1: lambda t=t: normalise_kv(t) for t in range(T)}
            for g in range(GROUPS):
                beside_hop1[2 * g + 2] = lambda g=g: add_bias(g)
            add_pass(dve, st, 1, beside_hop1)
            for s in range(GROUPS):
                close_hop(s)
            for s in range(GROUPS):
                at = part_of(AT[:, 0:KC, :], s)
                dve.wait_ge(pa_full, A_HOP1 + (s + 1) * GROUP)
                st.add(nc.vector.scalar_tensor_tensor(out=at, in0=at, scalar=0.5, in1=dinv_of(s), op0=ALU.mult, op1=ALU.mult))
            st.settle()
            def accumulate(dst, tiles=range(T)):
                for t in tiles:
                    o = V.next()
                    nc.vector.tensor_tensor(dst[:, t, :], dst[:, t, :], o[:, 0:D], ALU.add).then_inc(pv_free, 1)
                dve.wait_ge(pv_free, V.n)

            head_products_out()
            add_pass(dve, st, 2, {2 * t + 2: lambda t=t: accumulate(X, [t]) for t in range(T)})

            def softmax(v, part, stat):
                wide_stat = stat.unsqueeze(2).to_broadcast(list(part.shape))
                st.do(nc.vector.tensor_reduce(stat, part, AX, ALU.max))
                nc.vector.tensor_tensor(part, part, wide_stat, ALU.subtract).then_inc(asked, 1)
                answer()
                st.do(nc.vector.tensor_reduce(stat, part, AX, ALU.add))
                st.do(nc.vector.reciprocal(stat, stat))
                st.do(nc.vector.tensor_tensor(part, part, wide_stat, ALU.mult))

            def answer():
                roots[0] += 1
                dve.wait_ge(answered, roots[0])

            for s in range(GROUPS + 2):
                if s < GROUPS:
                    close_hop(s)
                if 1 <= s <= GROUPS:
                    accumulate(X, group(s - 1))
                    stats_of(X, s - 1)
                if s >= 2:
                    normalised(X, s - 2, xn_ready)

            dve.wait_ge(route_mm, 1)
            for c in range(KC):
                st.add(nc.vector.tensor_scalar(ybar[:, c, :], PACC[:, c:c + 1].to_broadcast([P, P]), 1.0 / NODES, None, ALU.mult))
            st.settle()
            dve.sem_inc(route_sb, 1)
            dve.wait_ge(route_mm, 2)
            dve.wait_ge(cols_loaded, 16)
            rw = sc[:, 0:8]
            rw3, stat = rw.unsqueeze(1), sc[:, 8:9]
            st.do(nc.vector.tensor_tensor(rw, PACC[:, 8:16], br, ALU.add))
            softmax(rw, rw3, stat)
            st.do(nc.vector.tensor_scalar(sc[:, 16:24], rw, float(NODES), None, ALU.mult))
            st.do(nc.vector.reciprocal(sc[:, 16:24], sc[:, 16:24]))
            st.do(nc.vector.tensor_scalar(sc[:, 16:24], sc[:, 16:24], CAPACITY, 1.0, ALU.mult, ALU.min))
            st.do(nc.vector.tensor_tensor(rw, rw, sc[:, 16:24], ALU.mult))
            softmax(rw, rw3, stat)
            st.do(nc.vector.max(sc[:, 24:32], rw))
            st.do(nc.vector.max_index(sc[:, 32:40].bitcast(U32), sc[:, 24:32], rw))
            nc.vector.tensor_tensor(sc[:, 40:41], sc[:, 25:26], sc[:, 24:25], ALU.subtract).then_inc(asked, 1)
            st.do(nc.vector.tensor_copy(sc[:, 48:50], sc[:, 32:34].bitcast(U32)))
            for e in range(2):
                chosen = sc[:, 48 + e:49 + e]
                for i, (first, n, rows_each) in enumerate(((0, KC, D), (2, HC, HID), (6, 1, P))):
                    k = sc[:, 56 + 4 * e + i:57 + 4 * e + i]
                    st.do(nc.vector.tensor_scalar(k, chosen, float(rows_each), None, ALU.mult))
                    st.add(nc.vector.tensor_scalar(gidx[:, 8 * e + first:8 * e + first + n], iota4[:, 0:n], k, None, ALU.add))
                st.add(nc.vector.tensor_copy(gidx[:, 8 * e + 7:8 * e + 8], chosen))
            st.settle()
            dve.sem_inc(idx0_ready, 1)
            answer()
            st.do(nc.vector.tensor_scalar(sc[:, 41:42], sc[:, 40:41], 1.0, None, ALU.add))
            st.do(nc.vector.reciprocal(sc[:, 41:42], sc[:, 41:42]))
            st.do(nc.vector.tensor_tensor(sc[:, 42:43], sc[:, 40:41], sc[:, 41:42], ALU.mult))
            dve.wait_ge(w2_gathered, 16 * 2 * (HC + 1))
            for e in range(2):
                st.add(nc.vector.tensor_scalar(WA[:, 2048 + 1024 * e:3072 + 1024 * e], WA[:, 2048 + 1024 * e:3072 + 1024 * e],
                                               sc[:, 41 + e:42 + e], None, ALU.mult))
                st.add(nc.vector.tensor_scalar(b2g[:, e, :], b2g[:, e, :], sc[:, 41 + e:42 + e], None, ALU.mult))
            st.settle()
            dve.sem_inc(w2_scaled, 1)
            st.do(nc.vector.tensor_tensor(b2c, b2g[:, 0, :], b2g[:, 1, :], ALU.add))
            nodes_wide = [P, T, D]

            def scale_attention_weights():
                dve.wait_ge(wb_loaded, 160)
                st.add(nc.vector.tensor_scalar(gpre, gpre, float(D) ** 0.5, None, ALU.mult))
                st.do(nc.vector.tensor_scalar(gout_b, gout_b, float(D) ** 0.5, None, ALU.mult))
                for c in range(KC):
                    st.add(nc.vector.tensor_scalar(wqkv[:, c, :], wqkv[:, c, :], gpre[:, c:c + 1], None, ALU.mult))
                st.settle()
                dve.sem_inc(mix_sb, 1)

            dve.wait_ge(nt_ready, 2 * T)
            st.do(nc.vector.tensor_tensor(N, N, b2c.unsqueeze(1).to_broadcast(nodes_wide), ALU.add))
            scale_attention_weights()
            dve.wait_ge(b2_loaded, 32)
            def into_stream(g):
                one_over_root(rstd[:, g * GROUP:(g + 1) * GROUP])
                n, x = N[:, g * GROUP:(g + 1) * GROUP, :], X[:, g * GROUP:(g + 1) * GROUP, :]
                for t in group(g):
                    st.add(nc.vector.scalar_tensor_tensor(out=N[:, t, :], in0=N[:, t, :], scalar=mv[:, t, 0:1], in1=gamma_b,
                                                          op0=ALU.subtract, op1=ALU.mult))
                yield
                st.settle()
                for t in group(g):
                    st.add(nc.vector.scalar_tensor_tensor(out=N[:, t, :], in0=N[:, t, :], scalar=rstd[:, t:t + 1], in1=beta_b,
                                                          op0=ALU.mult, op1=ALU.add))
                yield
                st.settle()
                st.do(nc.vector.tensor_tensor(x, x, n, ALU.add))
                yield
                stats_of(X, g)
                yield

            for s in range(GROUPS + 2):
                if s >= 2:
                    normalised(X, s - 2, xn_ready)
                behind = into_stream(s - 1) if 1 <= s <= GROUPS else iter(())
                if s < GROUPS:
                    for t in group(s):
                        accumulate(N, [t])
                        next(behind, None)
                for _ in behind:
                    pass
                if s < GROUPS:
                    stats_of(N, s)

            def over_norm(n):
                dve.wait_ge(norm_asked, n)
                st.do(nc.vector.tensor_scalar(rn, rn, 1e-12, None, ALU.max))
                nc.vector.reciprocal(rn, rn).then_inc(rn_ready, 1)
                dve.wait_ge(rn_ready, n)

            def normalise_queries(t):
                q3 = q1[:, t % 2, :].rearrange("p (h d) -> p h d", d=DH1)
                stat = sc[:, 8 * (t % 2):8 * (t % 2) + H1]
                wide_stat = stat.unsqueeze(2).to_broadcast([P, H1, DH1])
                dve.wait_ge(q_in, t + 1)
                st.do(nc.vector.tensor_reduce(stat, q3, AX, ALU.max))
                nc.vector.tensor_tensor(q3, q3, wide_stat, ALU.subtract).then_inc(asked, 1)
                answer()
                st.do(nc.vector.tensor_reduce(stat, q3, AX, ALU.add))
                st.do(nc.vector.reciprocal(stat, stat))
                nc.vector.tensor_tensor(q3, q3, wide_stat, ALU.mult).then_inc(q_normed, 1)

            def key_maxima():
                dve.wait_ge(pa_free, out_of_ring(T - 1))
                st.do(nc.vector.tensor_reduce(kmax, kv1[:, 0, 0:T - 1, :].rearrange("p t c -> p c t"), AX, ALU.max))
                nc.vector.tensor_tensor(kmax[0:LAST, :], kmax[0:LAST, :], kv1[0:LAST, 0, T - 1, :], ALU.max).then_inc(qk_ready, 1)

            def all_maxima():
                o = V.next()
                st.add(nc.vector.tensor_reduce(sc[:, 17:18], memkT, AX, ALU.max))
                nc.vector.tensor_reduce(sc[:, 16:17], o[:, 0:P], AX, ALU.max).then_inc(pv_free, 1)
                dve.wait_ge(pv_free, V.n)
                st.settle()
                st.do(nc.vector.tensor_tensor(sc[:, 16:17], sc[:, 16:17], sc[:, 17:18], ALU.max))
                nc.vector.tensor_scalar(diag1, ident[:, :], sc[:, 16:17], None, ALU.mult).then_inc(qk_ready, 1)

            def keys_less_maxima():
                o = V.next()
                k3 = kv1[:, 0, :, :]
                nc.vector.tensor_tensor(k3, k3, o[:, 0:P].unsqueeze(1).to_broadcast([P, T, P]), ALU.subtract).then_inc(asked, 1)
                dve.wait_ge(asked, roots[0] + 1)
                nc.vector.tensor_tensor(memk, memk, o[0:MEM, 0:P], ALU.subtract).then_inc(asked, 1)
                dve.wait_ge(asked, roots[0] + 2)
                dve.sem_inc(pv_free, 1)

            def keys_ready():
                answer()
                answer()
                dve.sem_inc(qk_ready, 1)
                st.do(nc.vector.memset(ctx_bd, 0.0))

            def context_heads():
                dve.wait_ge(mix_mm, 1)
                for h in range(H1):
                    s = slice(h * DH1, (h + 1) * DH1)
                    st.add(nc.vector.tensor_copy(ctx_bd[s, s], PACC[s, s]))
                st.do(nc.vector.reciprocal(sc[:, 18:19], PACC[:, P:P + 1]))
                st.do(nc.vector.tensor_scalar(sc[:, 18:19], sc[:, 18:19], float(DH1) ** -0.5, None, ALU.mult))
                dve.sem_inc(qk_ready, 1)

            def context_scaled():
                o = V.next()
                nc.vector.tensor_scalar(m2, o[:, 0:D], sc[:, 18:19], None, ALU.mult).then_inc(pv_free, 1)
                dve.wait_ge(pv_free, V.n)
                dve.sem_inc(qk_ready, 1)

            def attention_in(t):
                nc.vector.tensor_tensor(Y[:, t, :], V.next()[:, 0:D], bout_b, ALU.add).then_inc(pv_free, 1)

            beside_hop3 = {t: lambda t=t: ([over_norm(1)] if t == 0 else []) + [normalise_queries(t)] for t in range(T)}
            beside_hop3[T] = key_maxima
            beside_hop3[T + 1] = all_maxima
            beside_hop3[T + 2] = keys_less_maxima
            beside_hop3[T + 3] = keys_ready
            beside_hop3[T + 7] = context_heads
            beside_hop3[T + 8] = context_scaled
            for t in range(0, T, 2):
                beside_hop3[ROUND_OUT + t // 2] = lambda t=t: [attention_in(n) for n in range(t, min(t + 2, T))]

            def attention_into_stream():
                over_norm(2)
                for t in range(T):
                    st.add(nc.vector.tensor_scalar(Y[:, t, :], Y[:, t, :], rn[:, t:t + 1], None, ALU.mult))
                st.settle()
                st.do(nc.vector.tensor_tensor(Y, Y, gout_b.unsqueeze(1).to_broadcast(nodes_wide), ALU.mult))
                st.do(nc.vector.tensor_tensor(X[:, :, :], X[:, :, :], Y, ALU.add))

            free = [T + 4, T + 5, T + 6, T + 9, ROUND_OUT + T // 2 + 1]
            for g in range(GROUPS):
                beside_hop3[free[g]] = lambda g=g: st.do(nc.vector.tensor_tensor(
                    X[:, g * GROUP:(g + 1) * GROUP, :], X[:, g * GROUP:(g + 1) * GROUP, :], N[:, g * GROUP:(g + 1) * GROUP, :], ALU.add))

            st.add(nc.vector.memset(wgt[:, 0:C - 1], 1.0))
            st.add(nc.vector.tensor_scalar(wgt[:, C - 1:C], iota_p, float(EDGES - (C - 1) * P), None, ALU.is_lt))
            st.add(nc.vector.memset(AT[:, :, NP:WIDE], 0.0))
            st.add(nc.vector.memset(AT[:, HC - 1, NODES:NP], 0.0))
            st.do(nc.vector.tensor_scalar(eps_c, eps_in, 1.0, None, ALU.add))
            for g in range(GROUPS):
                dve.wait_ge(nt_ready, 2 * T + (g + 1) * GROUP)
                st.add(nc.vector.tensor_scalar(part_of(AT[:, 0:KC, :], g), part_of(NT, g), eps_c[:, 0:1], None, ALU.mult))
            st.settle()
            dve.sem_inc(at_ready, 1)
            add_pass(dve, st, 3, beside_hop3)
            dve.sem_inc(at_ready, 1)
            attention_into_stream()
            dve.sem_inc(stream_ready, 1)
            for g in range(GROUPS):
                dve.wait_ge(table_sbuf[3], (g + 1) * GROUP)
                st.add(nc.vector.tensor_scalar(part_of(AT, g), part_of(AT, g), eps_c[:, 1:2], None, ALU.mult))
            st.settle()
            dve.sem_inc(at_ready, 1)
            add_pass(dve, st, 4)
            dve.sem_inc(at_ready, 1)
            st.do(nc.vector.tensor_tensor(X[:, :, :], X[:, :, :], b2b_b.unsqueeze(1).to_broadcast(nodes_wide), ALU.add))
            for s in range(GROUPS + 1):
                if s < GROUPS:
                    accumulate(X, group(s))
                    stats_of(X, s)
                if s >= 1:
                    normalised(X, s - 1, xn_ready, N3)

            dve.wait_ge(route_mm, 3)
            p, hit, rest, one, two, dense = route
            groups = [P, T, E1]
            c0, c1, c2, c3 = rcol[0:4]

            def each(col):
                return col.unsqueeze(2).to_broadcast(groups)

            st.do(nc.vector.tensor_tensor(p, PACC[:, 0:T * E1].rearrange("p (t e) -> p t e", e=E1),
                                          rb2.unsqueeze(1).to_broadcast(groups), ALU.add))
            softmax(p, p, c0)
            index = iota6.unsqueeze(1).to_broadcast(groups)

            def first_hit(prob, best, mask):
                st.do(nc.vector.tensor_reduce(best, prob, AX, ALU.max))
                st.do(nc.vector.tensor_tensor(hit, prob, each(best), ALU.is_lt))
                st.do(nc.vector.tensor_scalar(hit, hit, 99.0, None, ALU.mult))
                st.do(nc.vector.tensor_tensor(hit, hit, index, ALU.add))
                st.do(nc.vector.tensor_reduce(c3, hit, AX, ALU.min))
                st.do(nc.vector.tensor_tensor(mask, hit, each(c3), ALU.is_equal))

            first_hit(p, c1, one)
            st.do(nc.vector.tensor_scalar(rest, one, -2.0, None, ALU.mult))
            st.do(nc.vector.tensor_tensor(rest, rest, p, ALU.add))
            first_hit(rest, c2, two)
            nc.vector.tensor_tensor(c0, c2, c1, ALU.subtract).then_inc(asked, 1)
            answer()
            st.do(nc.vector.tensor_scalar(c1, c0, 1.0, None, ALU.add))
            st.do(nc.vector.reciprocal(c1, c1))
            st.do(nc.vector.tensor_tensor(c2, c0, c1, ALU.mult))
            st.do(nc.vector.tensor_tensor(one, one, each(c1), ALU.mult))
            st.do(nc.vector.tensor_tensor(two, two, each(c2), ALU.mult))
            st.do(nc.vector.tensor_tensor(dense, one, two, ALU.add))
            dve.sem_inc(route_sb, 1)
            accumulate(X)
            for e in range(E1):
                for t in range(T):
                    o = V.next()
                    nc.vector.scalar_tensor_tensor(out=X[:, t, :], in0=o[:, 0:D], scalar=dense[:, t, e:e + 1], in1=X[:, t, :],
                                                   op0=ALU.mult, op1=ALU.add).then_inc(pv_free, 1)
                    if e == E1 - 1 and t % GROUP == GROUP - 1:
                        dve.wait_ge(pv_free, V.n)
                        dve.sem_inc(stored_ready, 1)


def kernel(**inputs):
    import numpy as np
    import concourse.bacc as bacc
    from concourse.bass_utils import run_bass_kernel_spmd

    def by_partition(m):
        m = np.asarray(m)
        return np.ascontiguousarray(m.reshape(-1, P, m.shape[1]).transpose(1, 0, 2).reshape(P, -1))

    def columns(v):
        return np.asarray(v).reshape(-1, P).T

    def rows_of(v):
        return np.broadcast_to(np.asarray(v).reshape(1, -1), (P, np.asarray(v).size))

    g = {k: np.asarray(v) for k, v in inputs.items()}
    mem = g["L1_mix_mem_kv"]
    pad = C * P - EDGES
    src = np.pad(g["src"], (0, pad)).astype(np.int32)
    src_pc = src.reshape(C, P).T
    dst = np.pad(g["dst"], (0, pad), mode="edge").astype(np.int32)
    ew = np.pad(g["edge_weight"], (0, pad))
    arrays = {
        "x": g["x"],
        "src_pc": np.concatenate([src_pc, src_pc[:, :U]], axis=1), "dst_pc": dst.reshape(C, P).T, "wgt_pc": ew.reshape(C, P).T,
        "dst_rounds": dst.reshape(ROUNDS, U * P),
        "wkvT": by_partition(g["L0_mix_w_qkv"][512:].T), "wq": by_partition(g["L0_mix_w_qkv"][:512]),
        "woT": by_partition(g["L0_mix_w_out"].T), "wgT": by_partition(g["L0_gnn_W"].T),
        "L0_gnn_b": g["L0_gnn_b"], "L0_mix_b_out": g["L0_mix_b_out"],
        "L0_ffn_gamma": g["L0_ffn_gamma"], "L0_ffn_beta": g["L0_ffn_beta"],
        "w1_rows": g["L0_ffn_W1"].reshape(E0 * D, HID), "w2_rows": g["L0_ffn_W2"].reshape(E0 * HID, D),
        "b1_rows": g["L0_ffn_b1"].reshape(E0, HC, P).transpose(0, 2, 1).reshape(E0 * P, HC), "b2_rows": g["L0_ffn_b2"],
        "cols": np.concatenate([
            mem[0].reshape(HD1, MEM), columns(g["L1_mix_g_pre"]), columns(g["L1_gnn_b1a"]), columns(g["L1_gnn_b1b"]),
            columns(g["L1_gnn_b2a"]), columns(g["L1_ffn_expert_b1"]), columns(g["L1_ffn_expert_b2"]),
            columns(g["L1_ffn_router_b1"]), rows_of(g["L1_ffn_router_b2"]), by_partition(g["L0_ffn_Wr"]),
            rows_of(g["L0_ffn_br"]), rows_of(g["L1_gnn_eps1"]), rows_of(g["L1_gnn_eps2"])], axis=1),
        "wqkv1": by_partition(g["L1_mix_w_qkv"]), "L1_mix_w_out": g["L1_mix_w_out"],
        "memk": mem[0].reshape(HD1, MEM).T, "memv": mem[1].reshape(HD1, MEM).T,
        "rw1": by_partition(g["L1_ffn_router_w1"]), "L1_ffn_router_w2": g["L1_ffn_router_w2"],
        "L1_ffn_expert_b3": g["L1_ffn_expert_b3"], "L1_mix_g_out": g["L1_mix_g_out"], "L1_mix_b_out": g["L1_mix_b_out"],
        "L1_gnn_b2b": g["L1_gnn_b2b"],
        "w1a": by_partition(g["L1_gnn_W1a"]), "w1b": by_partition(g["L1_gnn_W1b"]),
        "w2a": by_partition(g["L1_gnn_W2a"]), "w2b": by_partition(g["L1_gnn_W2b"]),
        "experts1": np.stack([np.concatenate([by_partition(g[f"L1_ffn_expert_w{i}"][e]) for i in (1, 2, 3)], axis=1)
                              for e in range(E1)]),
    }
    nc = bacc.Bacc("TRN2", target_bir_lowering=False, num_devices=1)
    arrays = {"in_" + k: np.ascontiguousarray(v) for k, v in arrays.items()}
    args = {k[3:]: nc.dram_tensor(k, v.shape, mybir.dt.from_np(v.dtype), kind="ExternalInput").ap()
            for k, v in arrays.items()}
    out = nc.dram_tensor("out_0", (NODES, D), F32, kind="ExternalOutput").ap()
    build(nc, args, out)
    r = run_bass_kernel_spmd(nc, [arrays], core_ids=[0])
    return r.results[0]["out_0"]
```
